# Optimizing a Trainium2 kernel written in Bass

```python
import numpy as np
import jax
import jax.numpy as jnp

def _softmax(x, axis=-1):
    return jax.nn.softmax(x, axis=axis)

def _gelu(x):
    return jax.nn.gelu(x, approximate=True)

def _silu(x):
    return jax.nn.silu(x)

def _sigmoid(x):
    return jax.nn.sigmoid(x)

def _layernorm(x, axis=-1, eps=1e-05):
    m = jnp.mean(x, axis=axis, keepdims=True)
    v = jnp.var(x, axis=axis, keepdims=True)
    return (x - m) / jnp.sqrt(v + eps)

def _scatter_add(tgt, idx, src, axis=0):
    return tgt.at[idx].add(src)

def _segment_sum(src, seg, n):
    return jax.ops.segment_sum(src, seg, n)
kernel_name = 'mk_recurrent_d2_jaxref_r4_a7e6e2'

def setup_inputs(seed: int=0):
    np.random.seed(seed)
    _w = jnp.asarray

    def _L0_attn_setup():
        import jax, jax.numpy as jnp
        import numpy as np
        H = 512
        NH = 16
        KD = H // 2
        VD = H // 2
        DK = KD // NH
        DV = VD // NH
        RLOW = 64
        GLOW = 64
        EPS = 1e-05
        B, T = (2, 256)
        key = jax.random.key(seed)
        ks = jax.random.split(key, 18)

        def rn(k, shape, scale=0.02):
            return (jax.random.normal(k, shape) * scale).astype(jnp.float32)
        return {'x': jax.random.normal(ks[0], (B, T, H), dtype=jnp.float32), 'mu_x': rn(ks[1], (H,), 0.5), 'Wx1': rn(ks[2], (H, 5 * RLOW)), 'Wx2': rn(ks[3], (H, 5, RLOW)), 'x_bias': rn(ks[4], (5, H)), 'Wr': rn(ks[5], (H, KD)), 'Wk': rn(ks[6], (H, KD)), 'Wv': rn(ks[7], (H, VD)), 'Ww_a': rn(ks[8], (H, GLOW)), 'Ww_b': rn(ks[9], (GLOW, KD)), 'bw': rn(ks[10], (KD,)), 'Wg_a': rn(ks[11], (H, GLOW)), 'Wg_b': rn(ks[12], (GLOW, VD)), 'bg': rn(ks[13], (VD,)), 'bonus': rn(ks[14], (NH, DK), 0.5), 'ln_w': jnp.ones((DV,), jnp.float32), 'ln_b': jnp.zeros((DV,), jnp.float32), 'Wo': rn(ks[15], (VD, H))}
    _L0_attn_in = _L0_attn_setup()

    def _L0_ffn_setup():
        import jax, jax.numpy as jnp
        import numpy as np
        _FP4_LUT = jnp.array([0.0, 0.5, 1.0, 1.5, 2.0, 3.0, 4.0, 6.0, -0.0, -0.5, -1.0, -1.5, -2.0, -3.0, -4.0, -6.0], dtype=jnp.float32)
        GROUP_SIZE = 128
        EPS = 1e-06

        def _dequant_fp4(packed_i32, scales_f16, group_size):
            out_f, in_p = packed_i32.shape
            w = packed_i32.astype(jnp.uint32)
            shifts = jnp.arange(8, dtype=jnp.uint32) * 4
            nib = w[:, :, None] >> shifts & jnp.uint32(15)
            vals = _FP4_LUT[nib.astype(jnp.int32)].reshape(out_f, in_p * 8)
            s = scales_f16.astype(jnp.float32).T
            s_full = jnp.repeat(s, group_size, axis=1)
            return vals * s_full
        key = jax.random.key(seed)
        k1, k2, k3, k4, k5 = jax.random.split(key, 5)
        B, S, H, I = (4, 512, 512, 1408)
        x = jax.random.normal(k1, (B, S, H), dtype=jnp.float32)
        gate_up_packed = jax.random.randint(k2, (2 * I, H // 8), 0, 2147483647, dtype=jnp.int32)
        gate_up_scales = jax.random.uniform(k3, (H // GROUP_SIZE, 2 * I), dtype=jnp.float32).astype(jnp.float16)
        down_packed = jax.random.randint(k4, (H, I // 8), 0, 2147483647, dtype=jnp.int32)
        down_scales = jax.random.uniform(k5, (I // GROUP_SIZE, H), dtype=jnp.float32).astype(jnp.float16)
        return {'x': x, 'gate_up_packed': gate_up_packed, 'gate_up_scales': gate_up_scales, 'down_packed': down_packed, 'down_scales': down_scales}
    _L0_ffn_in = _L0_ffn_setup()

    def _L1_attn_setup():
        import jax, jax.numpy as jnp
        import numpy as np
        H = 16
        KVH = 4
        D = 128
        HID = 512
        EPS = 1e-06
        GROUPS = H // KVH

        def elu_plus_one(x):
            return jax.nn.elu(x) + 1.0

        def _repeat_kv(x, b, s):
            x = x.reshape(b, s, KVH, 1, D)
            x = jnp.broadcast_to(x, (b, s, KVH, GROUPS, D))
            return x.reshape(b, s, H * D)

        def _split_heads(x, b, s, nh):
            return x.reshape(b, s, nh, D).transpose(0, 2, 1, 3)
        key = jax.random.key(seed)
        ks = jax.random.split(key, 8)
        s = 0.02
        return {'hidden_states': jax.random.normal(ks[0], (2, 1024, HID), jnp.float32), 'Wq': jax.random.normal(ks[1], (H * D, HID), jnp.float32) * s, 'bq': jnp.zeros((H * D,), jnp.float32), 'Wk': jax.random.normal(ks[2], (KVH * D, HID), jnp.float32) * s, 'bk': jnp.zeros((KVH * D,), jnp.float32), 'Wv': jax.random.normal(ks[3], (KVH * D, HID), jnp.float32) * s, 'bv': jnp.zeros((KVH * D,), jnp.float32), 'Wo': jax.random.normal(ks[4], (HID, H * D), jnp.float32) * s}
    _L1_attn_in = _L1_attn_setup()

    def _L1_ffn_setup():
        import jax, jax.numpy as jnp
        import numpy as np
        BLOCK = 64

        def dequant4bit(q, scale):
            return (q.astype(jnp.float32) - 7.5) * jnp.repeat(scale, BLOCK, axis=1)
        key = jax.random.key(seed)
        ks = jax.random.split(key, 11)
        B, S, D, H, R = (4, 512, 512, 2048, 16)
        return {'x1': jax.random.normal(ks[0], (B, S, D), jnp.float32), 'w_up_q': jax.random.randint(ks[1], (H, D), 0, 16, dtype=jnp.int32), 'w_up_scale': jax.random.uniform(ks[2], (H, D // BLOCK), jnp.float32) * 0.02, 'b_up': jax.random.normal(ks[3], (H,), jnp.float32) * 0.01, 'w_up_lora_a': jax.random.normal(ks[4], (D, R), jnp.float32) * 0.02, 'w_up_lora_b': jax.random.normal(ks[5], (R, H), jnp.float32) * 0.02, 'w_down_q': jax.random.randint(ks[6], (D, H), 0, 16, dtype=jnp.int32), 'w_down_scale': jax.random.uniform(ks[7], (D, H // BLOCK), jnp.float32) * 0.02, 'b_down': jax.random.normal(ks[8], (D,), jnp.float32) * 0.01, 'w_down_lora_a': jax.random.normal(ks[9], (H, R), jnp.float32) * 0.02, 'w_down_lora_b': jax.random.normal(ks[10], (R, D), jnp.float32) * 0.02}
    _L1_ffn_in = _L1_ffn_setup()
    _d = {'L0_attn_x': _L0_attn_in['x'], 'L0_attn_mu_x': _L0_attn_in['mu_x'], 'L0_attn_Wx1': _L0_attn_in['Wx1'], 'L0_attn_Wx2': _L0_attn_in['Wx2'], 'L0_attn_x_bias': _L0_attn_in['x_bias'], 'L0_attn_Wr': _L0_attn_in['Wr'], 'L0_attn_Wk': _L0_attn_in['Wk'], 'L0_attn_Wv': _L0_attn_in['Wv'], 'L0_attn_Ww_a': _L0_attn_in['Ww_a'], 'L0_attn_Ww_b': _L0_attn_in['Ww_b'], 'L0_attn_bw': _L0_attn_in['bw'], 'L0_attn_Wg_a': _L0_attn_in['Wg_a'], 'L0_attn_Wg_b': _L0_attn_in['Wg_b'], 'L0_attn_bg': _L0_attn_in['bg'], 'L0_attn_bonus': _L0_attn_in['bonus'], 'L0_attn_ln_w': _L0_attn_in['ln_w'], 'L0_attn_ln_b': _L0_attn_in['ln_b'], 'L0_attn_Wo': _L0_attn_in['Wo'], 'L0_ffn_gate_up_packed': _L0_ffn_in['gate_up_packed'], 'L0_ffn_gate_up_scales': _L0_ffn_in['gate_up_scales'], 'L0_ffn_down_packed': _L0_ffn_in['down_packed'], 'L0_ffn_down_scales': _L0_ffn_in['down_scales'], 'L1_attn_Wq': _L1_attn_in['Wq'], 'L1_attn_bq': _L1_attn_in['bq'], 'L1_attn_Wk': _L1_attn_in['Wk'], 'L1_attn_bk': _L1_attn_in['bk'], 'L1_attn_Wv': _L1_attn_in['Wv'], 'L1_attn_bv': _L1_attn_in['bv'], 'L1_attn_Wo': _L1_attn_in['Wo'], 'L1_ffn_w_up_q': _L1_ffn_in['w_up_q'], 'L1_ffn_w_up_scale': _L1_ffn_in['w_up_scale'], 'L1_ffn_b_up': _L1_ffn_in['b_up'], 'L1_ffn_w_up_lora_a': _L1_ffn_in['w_up_lora_a'], 'L1_ffn_w_up_lora_b': _L1_ffn_in['w_up_lora_b'], 'L1_ffn_w_down_q': _L1_ffn_in['w_down_q'], 'L1_ffn_w_down_scale': _L1_ffn_in['w_down_scale'], 'L1_ffn_b_down': _L1_ffn_in['b_down'], 'L1_ffn_w_down_lora_a': _L1_ffn_in['w_down_lora_a'], 'L1_ffn_w_down_lora_b': _L1_ffn_in['w_down_lora_b']}
    _x0 = _d['L0_attn_x']
    _d['L0_attn_x'] = jax.random.normal(jax.random.fold_in(jax.random.key(seed), 1), (4, 512, 512), dtype=_x0.dtype)
    del _x0
    return _d

def reference(L0_attn_x, L0_attn_mu_x, L0_attn_Wx1, L0_attn_Wx2, L0_attn_x_bias, L0_attn_Wr, L0_attn_Wk, L0_attn_Wv, L0_attn_Ww_a, L0_attn_Ww_b, L0_attn_bw, L0_attn_Wg_a, L0_attn_Wg_b, L0_attn_bg, L0_attn_bonus, L0_attn_ln_w, L0_attn_ln_b, L0_attn_Wo, L0_ffn_gate_up_packed, L0_ffn_gate_up_scales, L0_ffn_down_packed, L0_ffn_down_scales, L1_attn_Wq, L1_attn_bq, L1_attn_Wk, L1_attn_bk, L1_attn_Wv, L1_attn_bv, L1_attn_Wo, L1_ffn_w_up_q, L1_ffn_w_up_scale, L1_ffn_b_up, L1_ffn_w_up_lora_a, L1_ffn_w_up_lora_b, L1_ffn_w_down_q, L1_ffn_w_down_scale, L1_ffn_b_down, L1_ffn_w_down_lora_a, L1_ffn_w_down_lora_b):

    def _L0_attn_ref(x, mu_x, Wx1, Wx2, x_bias, Wr, Wk, Wv, Ww_a, Ww_b, bw, Wg_a, Wg_b, bg, bonus, ln_w, ln_b, Wo):
        import jax, jax.numpy as jnp
        import numpy as np
        H = 512
        NH = 16
        KD = H // 2
        VD = H // 2
        DK = KD // NH
        DV = VD // NH
        RLOW = 64
        GLOW = 64
        EPS = 1e-05
        B, T = (2, 256)
        b, t, _ = x.shape
        shifted = jnp.pad(x, ((0, 0), (1, 0), (0, 0)))[:, :t]
        delta = shifted - x
        lr = jnp.tanh(((x + delta * mu_x) @ Wx1).reshape(b, t, 5, RLOW))
        mus = jnp.einsum('btnr,hnr->btnh', lr, Wx2) + x_bias
        mr, mw, mk, mv, mg = (mus[:, :, i] for i in range(5))
        r = (x + delta * mr) @ Wr
        w = jnp.tanh((x + delta * mw) @ Ww_a) @ Ww_b + bw
        k = (x + delta * mk) @ Wk
        v = (x + delta * mv) @ Wv
        g = jnp.tanh((x + delta * mg) @ Wg_a) @ Wg_b + bg
        r = r.reshape(b, t, NH, DK)
        k = k.reshape(b, t, NH, DK)
        v = v.reshape(b, t, NH, DV)
        decay = jnp.exp(-jnp.exp(w.reshape(b, t, NH, DK)))
        xs = (jnp.moveaxis(r, 1, 0), jnp.moveaxis(k, 1, 0), jnp.moveaxis(v, 1, 0), jnp.moveaxis(decay, 1, 0))
        S0 = jnp.zeros((b, NH, DK, DV), x.dtype)

        def step(S, inp):
            rt, kt, vt, dt = inp
            kv = kt[..., :, None] * vt[..., None, :]
            ot = jnp.einsum('bhk,bhkv->bhv', rt, S + bonus[None, :, :, None] * kv)
            S = dt[..., None] * S + kv
            return (S, ot)
        _, o = jax.lax.scan(step, S0, xs)
        o = jnp.moveaxis(o, 0, 1)
        g = g.reshape(b, t, NH, DV)
        mean = o.mean(-1, keepdims=True)
        var = o.var(-1, keepdims=True)
        on = (o - mean) * jax.lax.rsqrt(var + EPS) * ln_w + ln_b
        o = on * g * jax.nn.sigmoid(g)
        return o.reshape(b, t, VD) @ Wo

    def _L0_ffn_ref(x, gate_up_packed, gate_up_scales, down_packed, down_scales):
        import jax, jax.numpy as jnp
        import numpy as np
        _FP4_LUT = jnp.array([0.0, 0.5, 1.0, 1.5, 2.0, 3.0, 4.0, 6.0, -0.0, -0.5, -1.0, -1.5, -2.0, -3.0, -4.0, -6.0], dtype=jnp.float32)
        GROUP_SIZE = 128
        EPS = 1e-06

        def _dequant_fp4(packed_i32, scales_f16, group_size):
            out_f, in_p = packed_i32.shape
            w = packed_i32.astype(jnp.uint32)
            shifts = jnp.arange(8, dtype=jnp.uint32) * 4
            nib = w[:, :, None] >> shifts & jnp.uint32(15)
            vals = _FP4_LUT[nib.astype(jnp.int32)].reshape(out_f, in_p * 8)
            s = scales_f16.astype(jnp.float32).T
            s_full = jnp.repeat(s, group_size, axis=1)
            return vals * s_full
        I = gate_up_packed.shape[0] // 2
        w_gu = _dequant_fp4(gate_up_packed, gate_up_scales, GROUP_SIZE)
        w_down = _dequant_fp4(down_packed, down_scales, GROUP_SIZE)
        gate_up = jnp.einsum('bsh,oh->bso', x, w_gu)
        gate, up = (gate_up[..., :I], gate_up[..., I:])
        h = jax.nn.silu(gate) * up
        y = jnp.einsum('bsi,hi->bsh', h, w_down)
        rms = jnp.sqrt(jnp.mean(y * y, axis=-1, keepdims=True) + EPS)
        return y / rms

    def _L1_attn_ref(hidden_states, Wq, bq, Wk, bk, Wv, bv, Wo):
        import jax, jax.numpy as jnp
        import numpy as np
        H = 16
        KVH = 4
        D = 128
        HID = 512
        EPS = 1e-06
        GROUPS = H // KVH

        def elu_plus_one(x):
            return jax.nn.elu(x) + 1.0

        def _repeat_kv(x, b, s):
            x = x.reshape(b, s, KVH, 1, D)
            x = jnp.broadcast_to(x, (b, s, KVH, GROUPS, D))
            return x.reshape(b, s, H * D)

        def _split_heads(x, b, s, nh):
            return x.reshape(b, s, nh, D).transpose(0, 2, 1, 3)
        b, s, _ = hidden_states.shape
        q = hidden_states @ Wq.T + bq
        k = hidden_states @ Wk.T + bk
        v = hidden_states @ Wv.T + bv
        k = _repeat_kv(k, b, s)
        v = _repeat_kv(v, b, s)
        q = _split_heads(q, b, s, H)
        k = _split_heads(k, b, s, H)
        v = _split_heads(v, b, s, H)
        sq = elu_plus_one(q)
        sk = elu_plus_one(k)
        kv = jnp.einsum('bhsd,bhse->bhde', sk, v)
        qkv = jnp.einsum('bhsd,bhde->bhse', sq, kv)
        k_sum = sk.sum(axis=2)
        norm = jnp.einsum('bhsd,bhd->bhs', sq, k_sum)
        attn = qkv / (norm[..., None] + EPS)
        attn = attn.transpose(0, 2, 1, 3).reshape(b, s, H * D)
        return attn @ Wo.T

    def _L1_ffn_ref(x1, w_up_q, w_up_scale, b_up, w_up_lora_a, w_up_lora_b, w_down_q, w_down_scale, b_down, w_down_lora_a, w_down_lora_b):
        import jax, jax.numpy as jnp
        import numpy as np
        BLOCK = 64

        def dequant4bit(q, scale):
            return (q.astype(jnp.float32) - 7.5) * jnp.repeat(scale, BLOCK, axis=1)
        w_up = dequant4bit(w_up_q, w_up_scale).T
        y1 = x1 @ w_up + b_up + x1 @ w_up_lora_a @ w_up_lora_b
        x2 = jax.nn.relu(y1)
        w_down = dequant4bit(w_down_q, w_down_scale).T
        y2 = x2 @ w_down + b_down + x2 @ w_down_lora_a @ w_down_lora_b
        return y2
    x = L0_attn_x
    xn = _layernorm(x, axis=-1)
    s = _L0_attn_ref(xn, L0_attn_mu_x, L0_attn_Wx1, L0_attn_Wx2, L0_attn_x_bias, L0_attn_Wr, L0_attn_Wk, L0_attn_Wv, L0_attn_Ww_a, L0_attn_Ww_b, L0_attn_bw, L0_attn_Wg_a, L0_attn_Wg_b, L0_attn_bg, L0_attn_bonus, L0_attn_ln_w, L0_attn_ln_b, L0_attn_Wo)
    g = _silu(_L0_ffn_ref(xn, L0_ffn_gate_up_packed, L0_ffn_gate_up_scales, L0_ffn_down_packed, L0_ffn_down_scales))
    x = x + s * g
    xn = _layernorm(x, axis=-1)
    s = _L1_attn_ref(xn, L1_attn_Wq, L1_attn_bq, L1_attn_Wk, L1_attn_bk, L1_attn_Wv, L1_attn_bv, L1_attn_Wo)
    g = _silu(_L1_ffn_ref(xn, L1_ffn_w_up_q, L1_ffn_w_up_scale, L1_ffn_b_up, L1_ffn_w_up_lora_a, L1_ffn_w_up_lora_b, L1_ffn_w_down_q, L1_ffn_w_down_scale, L1_ffn_b_down, L1_ffn_w_down_lora_a, L1_ffn_w_down_lora_b))
    x = x + s * g
    return x

_drawn_inputs = setup_inputs


def setup_inputs(seed=0):
    import zlib

    import numpy as np

    out = dict(_drawn_inputs(seed))
    spreads = {'L0_attn_ln_w': (1.0, 0.6),
     'L0_attn_ln_b': (0.0, 0.8),
     'L1_attn_bq': (0.0, 2.0),
     'L1_attn_bk': (0.0, 2.0),
     'L1_attn_bv': (0.0, 0.1)}
    factors = {'L0_attn_mu_x': 8.0,
     'L0_attn_Wx1': 8.0,
     'L0_attn_Wx2': 8.0,
     'L0_attn_x_bias': 8.0,
     'L0_attn_Wr': 7.658,
     'L0_attn_Wk': 7.629,
     'L0_attn_Wv': 7.64,
     'L0_attn_Ww_a': 8.0,
     'L0_attn_Ww_b': 8.0,
     'L0_attn_bw': 8.0,
     'L0_attn_Wg_a': 8.0,
     'L0_attn_Wg_b': 8.0,
     'L0_attn_bg': 8.0,
     'L0_attn_bonus': 8.0,
     'L0_attn_Wo': 7.624,
     'L0_ffn_gate_up_scales': 8.0,
     'L0_ffn_down_scales': 8.0,
     'L1_attn_Wq': 200.0,
     'L1_attn_Wk': 200.0,
     'L1_ffn_b_up': 64.0,
     'L1_ffn_w_up_lora_a': 8.0,
     'L1_ffn_w_up_lora_b': 8.0,
     'L1_ffn_b_down': 200.0,
     'L1_ffn_w_down_lora_a': 8.0,
     'L1_ffn_w_down_lora_b': 8.0}
    for name, (base, spread) in spreads.items():
        noise = np.random.default_rng([zlib.crc32(name.encode()), seed]).standard_normal(out[name].shape)
        drawn = base * np.exp(spread * noise) if base else spread * noise
        out[name] = jnp.asarray(drawn.astype(out[name].dtype))
    for name, factor in factors.items():
        out[name] = (out[name] * factor).astype(out[name].dtype)
    return out
```

```python
import numpy as np
import concourse.bass as bass
from concourse import mybir
from contextlib import ExitStack

F32 = mybir.dt.float32
F32R = mybir.dt.float32r
F16 = mybir.dt.float16
I32 = mybir.dt.int32
U32 = mybir.dt.uint32
ALU = mybir.AluOpType
ACT = mybir.ActivationFunctionType
AX = mybir.AxisListType

P = 128
B = 4
T = 512
TT = T // P
C = 512
KT = C // P
NH, DK = 16, 16
KD = NH * DK
HH = KD // P
HPT = P // DK
LOW = 64
I0 = 1408
JT = I0 // P
QH, KVH, D = 16, 4, 128
GROUPS = QH // KVH
I1 = 2048
UT = I1 // P
RANK = 16

CHANNELS = np.array([8 * (p % 64) + 2 * kt + p // 64 for kt in range(KT) for p in range(P)])
HIDDEN0 = np.array([P * m + 8 * (p % 16) + p // 16 for m in range(JT) for p in range(P)])


GQ = 2 * I0 // B
DQ = -(-JT // B)
UNPACK_STEPS = 3 * (2 + DQ)


class Signal:

    def __init__(self, ctx, nc, name, per, unit=1):
        self.sem, self.per, self.unit = ctx.enter_context(nc.semaphore(name)), per, unit

    def ahead(self, eng):
        eng.sem_inc(self.sem, self.per * self.unit)

    def now(self, b, k):
        return self.sem, b * (self.per * self.unit) + (self.per + k) * self.unit

    def before(self, b, k):
        return self.sem, b * (self.per * self.unit) + k * self.unit


class Ring:

    def __init__(self, ctx, nc, name, places, jobs, reader):
        self.places, self.n, self.jobs, self.reader = places, len(places), jobs, reader
        self.index = {job: i for i, job in enumerate(jobs)}
        assert len(self.index) == len(jobs) >= self.n
        self.done = Signal(ctx, nc, name + "_product", len(jobs))

    def slot(self, job):
        return self.index[job] % self.n

    def place(self, job):
        return self.places[self.slot(job)]

    def product(self, job, b):
        return self.done.now(b, self.index[job] + 1)

    def product_before(self, job, b):
        return self.done.before(b, self.index[job] + 1)

    def vacated(self, job, b):
        i = self.index[job]
        if i >= self.n:
            signal, k = self.reader[self.jobs[i - self.n]]
            return signal.now(b, k)
        last = max(j for j in range(len(self.jobs)) if j % self.n == i)
        signal, k = self.reader[self.jobs[last]]
        return signal.before(b, k)


def rows(ap, b):
    return ap[bass.ds(b * T, T), :].rearrange("(t p) c -> p t c", p=P)


def slab(ap, b):
    return ap[bass.ds(b * P, P), :]


def flat(ap):
    return ap.rearrange("p a b -> p (a b)")


def front(nc, w, x, spill, Wgu, Wdn):
    MIX = ["r", "w", "k", "v", "g"]
    ORDER = [2, 0, 3, 1, 4]
    N_MIX = len(ORDER) * KT

    def mixes(n):
        return [("mix", n, kt) for kt in range(KT)]

    def projections(n):
        return [("proj", n, hh) for hh in range(HH)] if MIX[ORDER[n]] in "rkv" else [("down", n)]

    jobs = [("xT", kt) for kt in range(KT)] + [("low", m) for m in range(3)] + mixes(0)
    for n in range(1, len(ORDER)):
        jobs += mixes(n) + projections(n - 1)
    jobs += [("decay", hh) for hh in range(HH)] + projections(4) + [("gate", h) for h in range(2)]

    with ExitStack() as ctx:
        def sb(name, shape, dt=F32):
            return ctx.enter_context(nc.sbuf_tensor("f_" + name, shape, dt))

        def signal(name, per, unit=1):
            return Signal(ctx, nc, "f_" + name, per, unit)

        W = sb("W", [P, KT, 1216])
        Wx1 = W[:, :, 0:320]
        Wproj = {"r": W[:, :, 320:576], "k": W[:, :, 576:832], "v": W[:, :, 832:1088]}
        Wdown = {"w": W[:, :, 1088:1152], "g": W[:, :, 1152:1216]}
        Wx2 = sb("Wx2", [P, 3, C])
        Wb = sb("Wb", [LOW, 2, KD])
        col = sb("col", [P, 6 * KT + HH])
        mu_x = col[:, 0:KT]
        bias = col[:, KT:6 * KT]
        bw = col[:, 6 * KT:6 * KT + HH]
        bg = sb("bg", [P, KD])
        ident = sb("ident", [P, P])
        x_tok = sb("x_tok", [P, TT, C])
        stats = sb("stats", [P, TT, 6])
        mv = sb("mv", [P, TT, 2])
        veps = sb("veps", [P, TT])
        pause = sb("pause", [P, 1])
        half = sb("half", [P, TT])
        rstd = sb("rstd", [P, TT])
        xT = sb("xT", [P, KT, T + 2])
        delta = sb("delta", [P, KT, T])
        mixed = [sb(f"mixed{i}", [P, KT, T]) for i in range(2)]
        xn = mixed[1]
        low = sb("low", [P, 3, T])
        tlow = {s: sb("tlow" + s, [LOW, T]) for s in "wg"}
        out = {s: sb("out" + s, [P, HH, T]) for s in "rkvw"}
        expw = sb("expw", [P, T])
        gu_words = sb("gu_words", [P, GQ], U32)
        gu_scale = sb("gu_scale", [P, GQ], F16)
        dn_words = sb("dn_words", [P, DQ, C], U32)
        dn_scale = sb("dn_scale", [P, DQ, C], F16)
        shift = sb("shift", [P, 3], I32)
        shifted = sb("shifted", [P, GQ], U32)
        value = sb("value", [P, GQ], U32)
        g = sb("g", [P, TT, KD])
        tanhg = sb("tanhg", [P, TT, KD])
        gate = sb("gate", [P, TT, KD])
        banks = [ctx.enter_context(nc.psum_tensor(f"f_ps{i}", [P, 512], F32)) for i in range(8)]

        w_loaded = ctx.enter_context(nc.semaphore("f_w_loaded"))
        const_set = ctx.enter_context(nc.semaphore("f_const_set"))
        x_loaded = signal("x_loaded", 1, 16)
        stats_ready = signal("stats_ready", 1)
        mv_ready = signal("mv_ready", 1)
        var_ready = signal("var_ready", 1)
        rstd_ready = signal("rstd_ready", 1)
        xn_ready = signal("xn_ready", TT)
        xT_ready = signal("xT_ready", KT)
        delta_ready = signal("delta_ready", KT)
        x_mixed = signal("x_mixed", KT)
        part_ready = signal("part_ready", N_MIX)
        mix_ready = signal("mix_ready", N_MIX)
        low_ready = signal("low_ready", 3)
        tlow_ready = signal("tlow_ready", 2)
        out_ready = {s: signal("out_ready" + s, HH) for s in "rkvw"}
        expw_ready = signal("expw_ready", HH)
        g_ready = signal("g_ready", 2)
        tanhg_ready = signal("tanhg_ready", 2)
        gate_ready = signal("gate_ready", 2)
        packed_loaded = signal("packed_loaded", 1, 64)
        unpack_step = signal("unpack_step", UNPACK_STEPS)
        unpacked = signal("unpacked", 2 + DQ)
        stored = {s: signal("stored" + s, 1, 16) for s in "xrkvwg"}

        reader = {}
        for job in jobs:
            kind, n = job[0], job[1]
            if kind == "xT":
                reader[job] = (xT_ready, n + 1)
            elif kind == "low":
                reader[job] = (low_ready, n + 1)
            elif kind == "mix":
                reader[job] = (part_ready, n * KT + job[2] + 1)
            elif kind == "proj":
                reader[job] = (out_ready[MIX[ORDER[n]]], job[2] + 1)
            elif kind == "down":
                reader[job] = (tlow_ready, 1 if MIX[ORDER[n]] == "w" else 2)
            elif kind == "decay":
                reader[job] = (expw_ready, n + 1)
            else:
                reader[job] = (g_ready, n + 1)
        ring = Ring(ctx, nc, "f", banks, jobs, reader)

        def last_reader(use):
            return ("low", 2) if use == 0 else projections(use - 1)[-1]

        block = ctx.enter_context(nc.Block())

        @block.sync
        def _(sp):
            sp.dma_start(ident[:, :], w["ident"]).then_inc(w_loaded, 16)
            sp.dma_start(flat(W[:, :, :]), w["front"]).then_inc(w_loaded, 16)
            sp.dma_start(flat(Wx2[:, :, :]), w["Wx2"]).then_inc(w_loaded, 16)
            sp.dma_start(flat(Wb[:, :, :]), w["Wb"]).then_inc(w_loaded, 16)
            sp.dma_start(col[:, :], w["front_col"]).then_inc(w_loaded, 16)
            sp.dma_start(bg[:, :], w["bg"]).then_inc(w_loaded, 16)
            sp.dma_start(shift[:, :], w["shift"]).then_inc(w_loaded, 16)
            for s in [x_loaded, packed_loaded, *stored.values()]:
                s.ahead(sp)
            with sp.Fori(0, B) as b:
                sp.wait_ge(*xn_ready.before(b, TT))
                sp.dma_start(x_tok[:, :, :], rows(x, b)).then_inc(x_loaded.sem, 16)
                sp.wait_ge(*unpacked.before(b, 2 + DQ))
                sp.dma_start(gu_words[:, :].bitcast(I32), w["gu_words"][:, bass.ds(b * GQ, GQ)]).then_inc(packed_loaded.sem, 16)
                sp.dma_start(gu_scale[:, :], w["gu_scale"][:, bass.ds(b * GQ, GQ)]).then_inc(packed_loaded.sem, 16)
                sp.dma_start(flat(dn_words[:, :, :]).bitcast(I32),
                             w["dn_words"][:, bass.ds(b * (DQ * C), DQ * C)]).then_inc(packed_loaded.sem, 16)
                sp.dma_start(flat(dn_scale[:, :, :]),
                             w["dn_scale"][:, bass.ds(b * (DQ * C), DQ * C)]).then_inc(packed_loaded.sem, 16)
                sp.wait_ge(*xT_ready.now(b, KT))
                sp.dma_start(slab(spill["x"], b).rearrange("p (n t) -> p n t", n=KT),
                             xT[:, :, 2:T + 2]).then_inc(stored["x"].sem, 16)
                for s in "krvw":
                    sp.wait_ge(*out_ready[s].now(b, HH))
                    sp.dma_start(slab(spill[s], b), flat(out[s][:, :, :])).then_inc(stored[s].sem, 16)
                sp.wait_ge(*gate_ready.now(b, 2))
                sp.dma_start(slab(spill["g"], b), flat(gate[:, :, :])).then_inc(stored["g"].sem, 16)
            for s in stored.values():
                sp.wait_ge(s.sem, 16 * (B + 1))

        @block.gpsimd
        def _(pool):
            nc.gpsimd.memset(half[:, :], -0.5).then_inc(const_set, 1)
            nc.gpsimd.memset(xT[:, :, 0:2], 0.0).then_inc(const_set, 1)
            pool.wait_ge(const_set, 2)
            for s in (rstd_ready, delta_ready, mix_ready):
                s.ahead(pool)
            with pool.Fori(0, B) as b:
                pool.wait_ge(*var_ready.now(b, 1))
                nc.gpsimd.tensor_tensor(rstd[:, :], veps[:, :], half[:, :], ALU.pow).then_inc(rstd_ready.sem, 1)
                for kt in range(KT):
                    pool.wait_ge(*xT_ready.now(b, kt + 1))
                    nc.gpsimd.tensor_tensor(delta[:, kt, :], xT[:, kt, 1:T + 1], xT[:, kt, 2:T + 2],
                                            ALU.subtract).then_inc(delta_ready.sem, 1)
                for n in range(len(ORDER)):
                    for kt in range(KT):
                        m = mixed[(n + 1) % 2][:, kt, :]
                        pool.wait_ge(*part_ready.now(b, n * KT + kt + 1))
                        nc.gpsimd.tensor_tensor(m, m, xT[:, kt, 2:T + 2], ALU.add).then_inc(mix_ready.sem, 1)

        @block.vector
        def _(dve):
            dve.wait_ge(w_loaded, 7 * 16)
            for s in (stats_ready, mv_ready, var_ready, xn_ready, x_mixed, part_ready, g_ready, gate_ready,
                      unpack_step, unpacked):
                s.ahead(dve)

            def unpack(b, n, words, shift_by, width):
                if n > 0:
                    dve.wait_ge(*unpacked.now(b, n))
                nc.vector.tensor_scalar(shifted[:, 0:width], words, shift_by, None,
                                        ALU.logical_shift_left).then_inc(unpack_step.sem, 1)
                dve.wait_ge(*unpack_step.now(b, 3 * n + 1))
                nc.vector.tensor_scalar(value[:, 0:width], shifted[:, 0:width], 3, 0x0E000E00,
                                        ALU.logical_shift_right, ALU.bitwise_and).then_inc(unpack_step.sem, 1)
                dve.wait_ge(*unpack_step.now(b, 3 * n + 2))
                nc.vector.scalar_tensor_tensor(value[:, 0:width], shifted[:, 0:width], 0x80008000,
                                               value[:, 0:width], ALU.bitwise_and,
                                               ALU.bitwise_or).then_inc(unpack_step.sem, 1)
                dve.wait_ge(*unpack_step.now(b, 3 * n + 3))

            def unpack_gate_up(b, jj):
                if jj == 0:
                    dve.wait_ge(*packed_loaded.now(b, 1))
                unpack(b, jj, gu_words[:, :], shift[:, jj:jj + 1].bitcast(U32), GQ)
                pair = value[:, :].bitcast(F16).rearrange("p (c e) -> p e c", e=2)
                for e in range(2):
                    last = nc.vector.scalar_tensor_tensor(Wgu[:, jj + 2 * e, bass.ds(b * GQ, GQ)], pair[:, e, :],
                                                          2.0 ** 14, gu_scale[:, :], ALU.mult, ALU.mult)
                last.then_inc(unpacked.sem, 1)

            def unpack_down(b, m):
                unpack(b, 2 + m, dn_words[:, m, :], shift[:, 2:3].bitcast(U32), C)
                pair = value[:, 0:C].bitcast(F16).rearrange("p (c e) -> p e c", e=2)
                for e in range(2):
                    rows_e = slice(64 * e, 64 * e + 64)
                    last = nc.vector.scalar_tensor_tensor(Wdn[rows_e, bass.ds(b * DQ + m, 1), :],
                                                          pair[rows_e, e:e + 1, :], 2.0 ** 14,
                                                          dn_scale[rows_e, m:m + 1, :], ALU.mult, ALU.mult)
                last.then_inc(unpacked.sem, 1)

            with dve.Fori(0, B) as b:
                dve.wait_ge(*x_loaded.now(b, 1))
                for t in range(TT):
                    last = nc.vector.bn_stats(stats[:, t, :], x_tok[:, t, :])
                last.then_inc(stats_ready.sem, 1)
                dve.wait_ge(*stats_ready.now(b, 1))
                nc.vector.memset(pause[:, :], 0.0)
                for t in range(TT):
                    last = nc.vector.bn_aggr(mv[:, t, :], stats[:, t, :])
                last.then_inc(mv_ready.sem, 1)
                dve.wait_ge(*mv_ready.now(b, 1))
                nc.vector.tensor_scalar(veps[:, :], mv[:, :, 1], 1e-5, None, ALU.add).then_inc(var_ready.sem, 1)
                dve.wait_ge(*rstd_ready.now(b, 1))
                dve.wait_ge(*ring.product_before(last_reader(5), b))
                for t in range(TT):
                    nc.vector.tensor_scalar(xn[:, t, :], x_tok[:, t, :], mv[:, t, 0:1], rstd[:, t:t + 1],
                                            ALU.subtract, ALU.mult).then_inc(xn_ready.sem, 1)
                dve.wait_ge(*ring.product_before(last_reader(4), b))
                for kt in range(KT):
                    dve.wait_ge(*delta_ready.now(b, kt + 1))
                    nc.vector.scalar_tensor_tensor(mixed[0][:, kt, :], delta[:, kt, :], mu_x[:, kt:kt + 1],
                                                   xT[:, kt, 2:T + 2], ALU.mult, ALU.add).then_inc(x_mixed.sem, 1)
                for n, i in enumerate(ORDER):
                    use = n + 1
                    if use == 1:
                        dve.wait_ge(*ring.product(("xT", KT - 1), b))
                    else:
                        dve.wait_ge(*ring.product(last_reader(use - 2), b))
                    for kt in range(KT):
                        dve.wait_ge(*ring.product(("mix", n, kt), b))
                        nc.vector.scalar_tensor_tensor(mixed[use % 2][:, kt, :], ring.place(("mix", n, kt))[:, :],
                                                       bias[:, i * KT + kt:i * KT + kt + 1], delta[:, kt, :],
                                                       ALU.add, ALU.mult).then_inc(part_ready.sem, 1)
                    if n < 2:
                        unpack_gate_up(b, n)
                    else:
                        unpack_down(b, n - 2)
                for h in range(2):
                    dve.wait_ge(*ring.product(("gate", h), b))
                    for n in range(2):
                        last = nc.vector.tensor_tensor(g[:, 2 * h + n, :],
                                                       ring.place(("gate", h))[:, n * KD:(n + 1) * KD], bg[:, :],
                                                       ALU.add)
                    last.then_inc(g_ready.sem, 1)
                dve.wait_ge(*stored["g"].before(b, 1))
                for h in range(2):
                    dve.wait_ge(*tanhg_ready.now(b, h + 1))
                    nc.vector.scalar_tensor_tensor(flat(gate[:, 2 * h:2 * h + 2, :]), flat(tanhg[:, 2 * h:2 * h + 2, :]),
                                                   1.0, flat(g[:, 2 * h:2 * h + 2, :]), ALU.add,
                                                   ALU.mult).then_inc(gate_ready.sem, 1)

        @block.scalar
        def _(act):
            act.wait_ge(w_loaded, 7 * 16)
            for s in (xT_ready, low_ready, tlow_ready, expw_ready, tanhg_ready, *out_ready.values()):
                s.ahead(act)
            with act.Fori(0, B) as b:
                act.wait_ge(*mix_ready.before(b, N_MIX))
                act.wait_ge(*stored["x"].before(b, 1))
                for job in jobs:
                    kind, n = job[0], job[1]
                    place = ring.place(job)
                    if kind in ("mix", "gate"):
                        continue
                    act.wait_ge(*ring.product(job, b))
                    if kind == "xT":
                        nc.scalar.activation(xT[:, n, 2:T + 2], place[:, :], ACT.Copy).then_inc(xT_ready.sem, 1)
                    elif kind == "low":
                        h = P if n < 2 else LOW
                        nc.scalar.activation(low[0:h, n, :], place[0:h, :], ACT.Tanh).then_inc(low_ready.sem, 1)
                    elif kind == "proj":
                        s, hh = MIX[ORDER[n]], job[2]
                        act.wait_ge(*stored[s].before(b, 1))
                        nc.scalar.activation(out[s][:, hh, :], place[:, :], ACT.Copy).then_inc(out_ready[s].sem, 1)
                    elif kind == "down":
                        s = MIX[ORDER[n]]
                        nc.scalar.activation(tlow[s][:, :], place[0:LOW, :], ACT.Tanh).then_inc(tlow_ready.sem, 1)
                    elif kind == "decay":
                        if n == 1:
                            act.wait_ge(*out_ready["w"].now(b, 1))
                        nc.scalar.activation(expw[:, :], place[:, :], ACT.Exp,
                                             bias=bw[:, n:n + 1]).then_inc(expw_ready.sem, 1)
                        act.wait_ge(*expw_ready.now(b, n + 1))
                        act.wait_ge(*stored["w"].before(b, 1))
                        nc.scalar.activation(out["w"][:, n, :], expw[:, :], ACT.Exp,
                                             scale=-1.0).then_inc(out_ready["w"].sem, 1)
                for h in range(2):
                    act.wait_ge(*g_ready.now(b, h + 1))
                    act.wait_ge(*gate_ready.before(b, h + 1))
                    nc.scalar.activation(flat(tanhg[:, 2 * h:2 * h + 2, :]), flat(g[:, 2 * h:2 * h + 2, :]), ACT.Tanh,
                                         scale=0.5).then_inc(tanhg_ready.sem, 1)

        @block.tensor
        def _(pe):
            pe.wait_ge(w_loaded, 7 * 16)
            ring.done.ahead(pe)
            with pe.Fori(0, B) as b:
                for job in jobs:
                    kind, n = job[0], job[1]
                    place = ring.place(job)
                    pe.wait_ge(*ring.vacated(job, b))
                    if kind == "xT":
                        for t in range(TT):
                            pe.wait_ge(*xn_ready.now(b, t + 1))
                            last = nc.tensor.transpose(place[:, t * P:(t + 1) * P], xn[:, t, n * P:(n + 1) * P],
                                                       ident[:, :])
                    elif kind == "low":
                        h = P if n < 2 else LOW
                        for kt in range(KT):
                            pe.wait_ge(*x_mixed.now(b, kt + 1))
                            last = nc.tensor.matmul(place[0:h, :], Wx1[:, kt, n * P:n * P + h], mixed[0][:, kt, :],
                                                    start=(kt == 0), stop=(kt == KT - 1))
                    elif kind == "mix":
                        i, kt = ORDER[n], job[2]
                        pe.wait_ge(*low_ready.now(b, i // 2 + 1))
                        p = LOW * (i % 2)
                        last = nc.tensor.matmul(place[:, :], Wx2[p:p + LOW, i // 2, kt * P:(kt + 1) * P],
                                                low[p:p + LOW, i // 2, :], start=True, stop=True)
                    elif kind in ("proj", "down"):
                        s = MIX[ORDER[n]]
                        buf = mixed[(n + 1) % 2]
                        if kind == "proj":
                            h, weight = P, Wproj[s][:, :, job[2] * P:(job[2] + 1) * P]
                        else:
                            h, weight = LOW, Wdown[s]
                        for kt in range(KT):
                            pe.wait_ge(*mix_ready.now(b, n * KT + kt + 1))
                            last = nc.tensor.matmul(place[0:h, :], weight[:, kt, :], buf[:, kt, :],
                                                    start=(kt == 0), stop=(kt == KT - 1))
                    elif kind == "decay":
                        pe.wait_ge(*tlow_ready.now(b, 1))
                        last = nc.tensor.matmul(place[:, :], Wb[:, 0, n * P:(n + 1) * P], tlow["w"][:, :],
                                                start=True, stop=True)
                    else:
                        pe.wait_ge(*tlow_ready.now(b, 2))
                        for m in range(2):
                            t = 2 * n + m
                            last = nc.tensor.matmul(place[:, m * KD:(m + 1) * KD], tlow["g"][:, t * P:(t + 1) * P],
                                                    Wb[:, 1, :], start=True, stop=True)
                    last.then_inc(ring.done.sem, 1)


def recurrence_and_gate(nc, w, x, spill, Wgu, Wdn, x1):
    UNITS = HH * DK
    LAG = 2
    A_jobs = ([("vtok", n) for n in range(2)] + [("spread", u) for u in range(UNITS)] + [("bonus", 0)]
              + [("oT", hh) for hh in range(HH)] + [("s", t) for t in range(TT)])
    DOWN = [(0, 1), (2,), (3,)]
    F_jobs = [("gu", j) for j in range(JT)] + [("down", n) for n in range(len(DOWN))]

    order = [("vtok", 0), ("vtok", 1)]
    gu = [("gu", j) for j in range(JT)]
    for u in range(UNITS):
        if u % 3 == 0:
            order.append(gu.pop(0))
        order.append(("spread", u))
        if u >= LAG:
            order.append(("sum", u - LAG))
    assert not gu
    order += [("sum", u) for u in range(UNITS - LAG, UNITS)]
    order += [("bonus", 0), ("down", 0), ("oT", 0), ("oT", 1), ("down", 1), ("down", 2)]
    order += [("s", t) for t in range(TT)]

    with ExitStack() as ctx:
        def sb(name, shape, dt=F32):
            return ctx.enter_context(nc.sbuf_tensor("r_" + name, shape, dt))

        def signal(name, per, unit=1):
            return Signal(ctx, nc, "r_" + name, per, unit)

        spread32 = sb("spread32", [P, P])
        spread = sb("spread", [P, DK, P], F32R)
        ident32 = sb("ident32", [P, P])
        ident = sb("ident", [P, P], F32R)
        heads = sb("heads", [P, HPT])
        Wo = sb("Wo", [P, HH, C])
        bonus = sb("bonus", [P, HH])
        lnw = sb("lnw", [P, KD])
        lnb = sb("lnb", [P, KD])
        half = sb("half", [P, NH * TT])
        xT = sb("xT", [P, KT, T])
        rT = [sb(f"rT{i}", [P, T]) for i in range(HH)]
        kT = [sb(f"kT{i}", [P, T]) for i in range(HH)]
        dT = [sb(f"dT{i}", [P, T]) for i in range(HH)]
        vT = sb("vT", [P, HH, T])
        v_hi = sb("v_hi", [P, HH, T], F32R)
        v_lo = sb("v_lo", [P, HH, T], F32R)
        v_tok = sb("v_tok", [P, TT, KD])
        kv = [sb(f"kv{i}", [P, T]) for i in range(2)]
        S = [sb(f"S{i}", [P, T + 1]) for i in range(2)]
        rS = [sb(f"rS{i}", [P, T]) for i in range(3)]
        rkb = sb("rkb", [P, HH, T])
        gate = sb("gate", [P, TT, KD])
        vc = sb("vc", [P, TT, KD])
        o = sb("o", [P, TT, KD])
        small = {s: sb(s, [P, TT * NH]) for s in ("osum", "oss", "oveps", "orstd")}
        oT = sb("oT", [P, HH, T])
        h = sb("h", [P, JT, T])
        tanh_gate = [sb(f"tanh_gate{i}", [P, T]) for i in range(2)]
        hg = sb("hg", [P, T])
        ysq = sb("ysq", [P, C])
        yss = sb("yss", [P, TT])
        yveps = sb("yveps", [P, TT])
        yr = sb("yr", [P, TT])
        hyr = sb("hyr", [P, TT])
        tanh_y = [sb(f"tanh_y{i}", [P, C]) for i in range(2)]
        u1 = sb("u1", [P, TT, C])
        xs = sb("xs", [P, TT, C])
        banks = [ctx.enter_context(nc.psum_tensor(f"r_ps{i}", [P, 512], F32)) for i in range(8)]

        w_loaded = ctx.enter_context(nc.semaphore("r_w_loaded"))
        spread_loaded = ctx.enter_context(nc.semaphore("r_spread_loaded"))
        const_set = ctx.enter_context(nc.semaphore("r_const_set"))
        rounded = ctx.enter_context(nc.semaphore("r_rounded"))
        xT_loaded = signal("xT_loaded", 1, 16)
        rkd_loaded = [signal(f"rkd_loaded{i}", 1, 48) for i in range(HH)]
        v_loaded = signal("v_loaded", 1, 16)
        g_loaded = signal("g_loaded", 1, 16)
        x_loaded = signal("x_loaded", 1, 16)
        x1_stored = signal("x1_stored", 1, 16)
        v_hi_ready = signal("v_hi_ready", 1)
        v_lo_ready = signal("v_lo_ready", 1)
        vtok_ready = signal("vtok_ready", 2)
        rk_ready = signal("rk_ready", HH)
        rkb_ready = signal("rkb_ready", HH)
        kv_ready = signal("kv_ready", UNITS)
        S_ready = signal("S_ready", UNITS)
        rS_ready = signal("rS_ready", UNITS)
        summed = signal("summed", UNITS)
        tanh_gate_ready = signal("tanh_gate_ready", JT)
        hg_ready = signal("hg_ready", JT)
        h_ready = signal("h_ready", JT)
        vc_ready = signal("vc_ready", 1)
        o_ready = signal("o_ready", TT)
        osum_ready = signal("osum_ready", 1)
        centred = signal("centred", 1)
        squared = signal("squared", 1)
        oss_ready = signal("oss_ready", 1)
        oveps_ready = signal("oveps_ready", 1)
        orstd_ready = signal("orstd_ready", 1)
        o_step = signal("o_step", 3)
        gated_ready = signal("gated_ready", 1)
        oT_ready = signal("oT_ready", HH)
        yss_ready = signal("yss_ready", TT)
        yveps_ready = signal("yveps_ready", len(DOWN))
        yr_ready = signal("yr_ready", len(DOWN))
        hyr_ready = signal("hyr_ready", len(DOWN))
        tanh_y_ready = signal("tanh_y_ready", TT)
        u1_ready = signal("u1_ready", TT)
        sg_ready = signal("sg_ready", TT)
        x1_ready = signal("x1_ready", TT)

        A = Ring(ctx, nc, "r_A", banks[0:2], A_jobs,
                 {**{("vtok", n): (vtok_ready, n + 1) for n in range(2)},
                  **{("spread", u): (kv_ready, u + 1) for u in range(UNITS)},
                  ("bonus", 0): (vc_ready, 1),
                  **{("oT", hh): (oT_ready, hh + 1) for hh in range(HH)},
                  **{("s", t): (sg_ready, t + 1) for t in range(TT)}})
        O = banks[2:4]
        F = Ring(ctx, nc, "r_F", [banks[4:6], banks[6:8]], F_jobs,
                 {**{("gu", j): (h_ready, j + 1) for j in range(JT)},
                  **{("down", n): (u1_ready, DOWN[n][-1] + 1) for n in range(len(DOWN))}})

        block = ctx.enter_context(nc.Block())

        @block.sync
        def _(sp):
            for dst, name in ((ident32, "ident"), (heads, "heads"), (bonus, "bonus"), (lnw, "lnw"), (lnb, "lnb")):
                sp.dma_start(dst[:, :], w[name]).then_inc(w_loaded, 16)
            sp.dma_start(flat(Wo[:, :, :]), w["Wo0"]).then_inc(w_loaded, 16)
            for v in range(DK):
                if v > 0:
                    sp.wait_ge(rounded, v)
                sp.dma_start(spread32[:, :], w["spread"][:, v * P:(v + 1) * P]).then_inc(spread_loaded, 16)
            for s in [xT_loaded, *rkd_loaded, v_loaded, g_loaded, x_loaded, x1_stored]:
                s.ahead(sp)
            with sp.Fori(0, B) as b:
                sp.wait_ge(*v_lo_ready.before(b, 1))
                sp.dma_start(flat(vT[:, :, :]), slab(spill["v"], b)).then_inc(v_loaded.sem, 16)
                sp.wait_ge(*F.product_before(("gu", JT - 1), b))
                sp.dma_start(flat(xT[:, :, :]), slab(spill["x"], b)).then_inc(xT_loaded.sem, 16)
                for hh in range(HH):
                    sp.wait_ge(*rS_ready.before(b, DK * (hh + 1)))
                    for dst, s in ((rT, "r"), (kT, "k"), (dT, "w")):
                        sp.dma_start(dst[hh][:, :], slab(spill[s], b)[:, hh * T:(hh + 1) * T]).then_inc(
                            rkd_loaded[hh].sem, 16)
                sp.wait_ge(*gated_ready.before(b, 1))
                sp.dma_start(flat(gate[:, :, :]), slab(spill["g"], b)).then_inc(g_loaded.sem, 16)
                sp.wait_ge(*x1_stored.before(b, 1))
                sp.dma_start(xs[:, :, :], rows(x, b)).then_inc(x_loaded.sem, 16)
                sp.wait_ge(*x1_ready.now(b, TT))
                sp.dma_start(rows(x1, b), xs[:, :, :]).then_inc(x1_stored.sem, 16)
            sp.wait_ge(x1_stored.sem, 16 * (B + 1))

        @block.gpsimd
        def _(pool):
            nc.gpsimd.memset(half[:, :], -0.5).then_inc(const_set, 1)
            for i in range(2):
                nc.gpsimd.memset(S[i][:, 0:1], 0.0).then_inc(const_set, 1)
            pool.wait_ge(const_set, 3)
            for s in (rS_ready, orstd_ready, yr_ready, x1_ready):
                s.ahead(pool)
            with pool.Fori(0, B) as b:
                for u in range(UNITS):
                    pool.wait_ge(*S_ready.now(b, u + 1))
                    if u >= 3:
                        pool.wait_ge(*summed.now(b, u - 2))
                    else:
                        pool.wait_ge(*summed.before(b, UNITS - (UNITS - 1 - u) % 3))
                    nc.gpsimd.tensor_tensor(rS[u % 3][:, :], S[u % 2][:, 0:T], rT[u // DK][:, :],
                                            ALU.mult).then_inc(rS_ready.sem, 1)
                pool.wait_ge(*oveps_ready.now(b, 1))
                nc.gpsimd.tensor_tensor(small["orstd"][:, :], small["oveps"][:, :], half[:, :],
                                        ALU.pow).then_inc(orstd_ready.sem, 1)
                for n, ts in enumerate(DOWN):
                    pool.wait_ge(*yveps_ready.now(b, n + 1))
                    cols = slice(ts[0], ts[-1] + 1)
                    nc.gpsimd.tensor_tensor(yr[:, cols], yveps[:, cols], half[:, cols],
                                            ALU.pow).then_inc(yr_ready.sem, 1)
                pool.wait_ge(*x_loaded.now(b, 1))
                for t in range(TT):
                    pool.wait_ge(*sg_ready.now(b, t + 1))
                    nc.gpsimd.tensor_tensor(xs[:, t, :], xs[:, t, :], u1[:, t, :], ALU.add).then_inc(x1_ready.sem, 1)

        @block.vector
        def _(dve):
            dve.wait_ge(w_loaded, 6 * 16)
            dve.wait_ge(const_set, 3)
            for s in (v_lo_ready, rk_ready, rkb_ready, kv_ready, S_ready, hg_ready, h_ready, vc_ready, o_ready,
                      osum_ready, centred, oss_ready, oveps_ready, o_step, gated_ready, yveps_ready, hyr_ready,
                      u1_ready, sg_ready):
                s.ahead(dve)
            with dve.Fori(0, B) as b:
                dve.wait_ge(*v_hi_ready.now(b, 1))
                nc.vector.tensor_tensor(flat(v_lo[:, :, :]), flat(vT[:, :, :]), flat(v_hi[:, :, :].bitcast(F32)),
                                        ALU.subtract).then_inc(v_lo_ready.sem, 1)
                dve.wait_ge(*F.product_before(("down", len(DOWN) - 1), b))

                def hidden(j):
                    dve.wait_ge(*tanh_gate_ready.now(b, j + 1))
                    gate_ps, up_ps = F.place(("gu", j))
                    dve.wait_ge(*(h_ready.now(b, j) if j > 0 else h_ready.before(b, JT)))
                    nc.vector.scalar_tensor_tensor(hg[:, :], tanh_gate[j % 2][:, :], 1.0, gate_ps[:, :], ALU.add,
                                                   ALU.mult).then_inc(hg_ready.sem, 1)
                    dve.wait_ge(*hg_ready.now(b, j + 1))
                    nc.vector.scalar_tensor_tensor(h[:, j, :], hg[:, :], 0.5, up_ps[:, :], ALU.mult,
                                                   ALU.mult).then_inc(h_ready.sem, 1)

                for u in range(UNITS):
                    hh = u // DK
                    if u % DK == 0:
                        dve.wait_ge(*rkd_loaded[hh].now(b, 1))
                        nc.vector.scalar_tensor_tensor(rkb[:, hh, :], rT[hh][:, :], bonus[:, hh:hh + 1], kT[hh][:, :],
                                                       ALU.mult, ALU.mult).then_inc(rkb_ready.sem, 1)
                    dve.wait_ge(*A.product(("spread", u), b))
                    dve.wait_ge(*(S_ready.now(b, u - 1) if u >= 2 else S_ready.before(b, UNITS - 1 + u)))
                    nc.vector.tensor_tensor(kv[u % 2][:, :], kT[hh][:, :], A.place(("spread", u))[:, :],
                                            ALU.mult).then_inc(kv_ready.sem, 1)
                    dve.wait_ge(*kv_ready.now(b, u + 1))
                    dve.wait_ge(*(rS_ready.now(b, u - 1) if u >= 2 else rS_ready.before(b, UNITS - 1 + u)))
                    nc.vector.tensor_tensor_scan(S[u % 2][:, 1:T + 1], dT[hh][:, :], kv[u % 2][:, :], 0.0, ALU.mult,
                                                 ALU.add).then_inc(S_ready.sem, 1)
                    if u % 3 == 2:
                        hidden(u // 3)
                hidden(JT - 1)

                dve.wait_ge(*A.product(("bonus", 0), b))
                dve.wait_ge(*vtok_ready.now(b, 2))
                by_head = "p t (h v) -> p (t h) v"
                wide = [P, TT * NH, DK]
                nc.vector.tensor_tensor(vc[:, :, :].rearrange(by_head, v=DK), v_tok[:, :, :].rearrange(by_head, v=DK),
                                        A.place(("bonus", 0))[:, 0:TT * NH].unsqueeze(2).broadcast_to(wide),
                                        ALU.mult).then_inc(vc_ready.sem, 1)
                dve.wait_ge(*vc_ready.now(b, 1))
                dve.wait_ge(*summed.now(b, UNITS))
                for t in range(TT):
                    ps = O[t // 2][:, (t % 2) * KD:(t % 2 + 1) * KD]
                    nc.vector.tensor_tensor(o[:, t, :].rearrange("p (g h v) -> p g h v", g=HH, v=DK),
                                            vc[:, t, :].rearrange("p (g h v) -> p g h v", g=HH, v=DK),
                                            ps.rearrange("p (g v h) -> p g h v", g=HH, v=DK),
                                            ALU.add).then_inc(o_ready.sem, 1)
                dve.wait_ge(*o_ready.now(b, TT))
                o3 = o[:, :, :].rearrange(by_head, v=DK)
                nc.vector.tensor_reduce(small["osum"][:, :], o3, AX.X, ALU.add).then_inc(osum_ready.sem, 1)
                dve.wait_ge(*osum_ready.now(b, 1))
                nc.vector.scalar_tensor_tensor(o3, small["osum"][:, :].unsqueeze(2).broadcast_to(wide), -1.0 / DK, o3,
                                               ALU.mult, ALU.add).then_inc(centred.sem, 1)
                dve.wait_ge(*squared.now(b, 1))
                nc.vector.tensor_reduce(small["oss"][:, :], vc[:, :, :].rearrange(by_head, v=DK), AX.X,
                                        ALU.add).then_inc(oss_ready.sem, 1)
                dve.wait_ge(*oss_ready.now(b, 1))
                nc.vector.tensor_scalar(small["oveps"][:, :], small["oss"][:, :], 1.0 / DK, 1e-5, ALU.mult,
                                        ALU.add).then_inc(oveps_ready.sem, 1)
                dve.wait_ge(*orstd_ready.now(b, 1))
                nc.vector.tensor_tensor(o3, o3, small["orstd"][:, :].unsqueeze(2).broadcast_to(wide),
                                        ALU.mult).then_inc(o_step.sem, 1)
                dve.wait_ge(*o_step.now(b, 1))
                nc.vector.tensor_tensor(o[:, :, :], o[:, :, :], lnw[:, :].unsqueeze(1).broadcast_to([P, TT, KD]),
                                        ALU.mult).then_inc(o_step.sem, 1)
                dve.wait_ge(*o_step.now(b, 2))
                nc.vector.tensor_tensor(o[:, :, :], o[:, :, :], lnb[:, :].unsqueeze(1).broadcast_to([P, TT, KD]),
                                        ALU.add).then_inc(o_step.sem, 1)
                dve.wait_ge(*o_step.now(b, 3))
                dve.wait_ge(*g_loaded.now(b, 1))
                nc.vector.scalar_tensor_tensor(flat(o[:, :, :]), flat(gate[:, :, :]), 0.5, flat(o[:, :, :]), ALU.mult,
                                               ALU.mult).then_inc(gated_ready.sem, 1)
                for n, ts in enumerate(DOWN):
                    cols = slice(ts[0], ts[-1] + 1)
                    dve.wait_ge(*yss_ready.now(b, ts[-1] + 1))
                    nc.vector.tensor_scalar(yveps[:, cols], yss[:, cols], 1.0 / C, 1e-6, ALU.mult,
                                            ALU.add).then_inc(yveps_ready.sem, 1)
                    dve.wait_ge(*yr_ready.now(b, n + 1))
                    nc.vector.tensor_scalar(hyr[:, cols], yr[:, cols], 0.5, None, ALU.mult).then_inc(hyr_ready.sem, 1)
                    for i, t in enumerate(ts):
                        dve.wait_ge(*tanh_y_ready.now(b, t + 1))
                        dve.wait_ge(*x1_ready.before(b, t + 1))
                        nc.vector.scalar_tensor_tensor(u1[:, t, :], tanh_y[t % 2][:, :], 1.0,
                                                       F.place(("down", n))[i][:, :], ALU.add,
                                                       ALU.mult).then_inc(u1_ready.sem, 1)
                for t in range(TT):
                    dve.wait_ge(*A.product(("s", t), b))
                    dve.wait_ge(*u1_ready.now(b, t + 1))
                    nc.vector.scalar_tensor_tensor(u1[:, t, :], A.place(("s", t))[:, :], hyr[:, t:t + 1], u1[:, t, :],
                                                   ALU.mult, ALU.mult).then_inc(sg_ready.sem, 1)

        @block.scalar
        def _(act):
            act.wait_ge(w_loaded, 6 * 16)
            for v in range(DK):
                act.wait_ge(spread_loaded, 16 * (v + 1))
                nc.scalar.activation(spread[:, v, :], spread32[:, :], ACT.Copy).then_inc(rounded, 1)
            nc.scalar.activation(ident[:, :], ident32[:, :], ACT.Copy).then_inc(rounded, 1)
            for s in (v_hi_ready, vtok_ready, tanh_gate_ready, squared, oT_ready, yss_ready, tanh_y_ready):
                s.ahead(act)
            with act.Fori(0, B) as b:
                act.wait_ge(*v_loaded.now(b, 1))
                act.wait_ge(*A.product_before(("spread", UNITS - 1), b))
                nc.scalar.activation(flat(v_hi[:, :, :]), flat(vT[:, :, :]), ACT.Copy).then_inc(v_hi_ready.sem, 1)
                act.wait_ge(*vc_ready.before(b, 1))
                for n in range(2):
                    act.wait_ge(*A.product(("vtok", n), b))
                    nc.scalar.activation(flat(v_tok[:, 2 * n:2 * n + 2, :]), A.place(("vtok", n))[:, :],
                                         ACT.Copy).then_inc(vtok_ready.sem, 1)
                for j in range(JT):
                    act.wait_ge(*F.product(("gu", j), b))
                    act.wait_ge(*(h_ready.now(b, j - 1) if j >= 2 else h_ready.before(b, JT)))
                    nc.scalar.activation(tanh_gate[j % 2][:, :], F.place(("gu", j))[0][:, :], ACT.Tanh,
                                         scale=0.5).then_inc(tanh_gate_ready.sem, 1)
                act.wait_ge(*centred.now(b, 1))
                nc.scalar.activation(flat(vc[:, :, :]), flat(o[:, :, :]), ACT.Square).then_inc(squared.sem, 1)

                def squares(n):
                    act.wait_ge(*F.product(("down", n), b))
                    for i, t in enumerate(DOWN[n]):
                        act.wait_ge(*(yss_ready.now(b, t) if t > 0 else yss_ready.before(b, TT)))
                        nc.scalar.activation(ysq[:, :], F.place(("down", n))[i][:, :], ACT.Square,
                                             accum_out=yss[:, t:t + 1]).then_inc(yss_ready.sem, 1)

                def tanhs(n):
                    act.wait_ge(*hyr_ready.now(b, n + 1))
                    for i, t in enumerate(DOWN[n]):
                        act.wait_ge(*(u1_ready.now(b, t - 1) if t >= 2 else u1_ready.before(b, t + 3)))
                        nc.scalar.activation(tanh_y[t % 2][:, :], F.place(("down", n))[i][:, :], ACT.Tanh,
                                             scale=hyr[:, t:t + 1]).then_inc(tanh_y_ready.sem, 1)

                squares(0)
                for hh in range(HH):
                    act.wait_ge(*A.product(("oT", hh), b))
                    nc.scalar.activation(oT[:, hh, :], A.place(("oT", hh))[:, :], ACT.Copy).then_inc(oT_ready.sem, 1)
                tanhs(0)
                for n in (1, 2):
                    squares(n)
                    tanhs(n)

        @block.tensor
        def _(pe):
            pe.wait_ge(w_loaded, 6 * 16)
            pe.wait_ge(rounded, DK + 1)
            for s in (A.done, F.done, summed):
                s.ahead(pe)
            with pe.Fori(0, B) as b:
                for job in order:
                    kind, n = job
                    if kind == "sum":
                        u, hh = n, n // DK
                        pe.wait_ge(*rS_ready.now(b, u + 1))
                        if u == 0:
                            pe.wait_ge(*o_ready.before(b, TT))
                        for t in range(TT):
                            at = (t % 2) * KD + hh * P + (u % DK) * HPT
                            last = nc.tensor.matmul(O[t // 2][:, at:at + HPT], rS[u % 3][:, t * P:(t + 1) * P],
                                                    heads[:, :], start=True, stop=True)
                        last.then_inc(summed.sem, 1)
                        continue
                    ring = F if kind in ("gu", "down") else A
                    place = ring.place(job)
                    pe.wait_ge(*ring.vacated(job, b))
                    if kind == "vtok":
                        pe.wait_ge(*v_lo_ready.now(b, 1))
                        for m in range(2):
                            t = 2 * n + m
                            for hh in range(HH):
                                at = m * KD + hh * P
                                for i, part in enumerate((v_hi, v_lo)):
                                    last = nc.tensor.matmul(place[:, at:at + P], part[:, hh, t * P:(t + 1) * P],
                                                            ident[:, :], start=(i == 0), stop=(i == 1))
                    elif kind == "spread":
                        for i, part in enumerate((v_hi, v_lo)):
                            last = nc.tensor.matmul(place[:, :], spread[:, n % DK, :], part[:, n // DK, :],
                                                    start=(i == 0), stop=(i == 1))
                    elif kind == "gu":
                        if n == 0:
                            pe.wait_ge(*xT_loaded.now(b, 1))
                        for side in range(2):
                            at = side * I0 + n * P
                            for kt in range(KT):
                                last = nc.tensor.matmul(place[side][:, :], Wgu[:, kt, at:at + P], xT[:, kt, :],
                                                        start=(kt == 0), stop=(kt == KT - 1))
                    elif kind == "down":
                        for i, t in enumerate(DOWN[n]):
                            for j in range(JT):
                                if n == 0 and i == 0:
                                    pe.wait_ge(*h_ready.now(b, j + 1))
                                last = nc.tensor.matmul(place[i][:, :], h[:, j, t * P:(t + 1) * P], Wdn[:, j, :],
                                                        start=(j == 0), stop=(j == JT - 1))
                    elif kind == "bonus":
                        pe.wait_ge(*rkb_ready.now(b, HH))
                        for t in range(TT):
                            for hh in range(HH):
                                at = t * NH + hh * HPT
                                last = nc.tensor.matmul(place[:, at:at + HPT], rkb[:, hh, t * P:(t + 1) * P],
                                                        heads[:, :], start=True, stop=True)
                    elif kind == "oT":
                        pe.wait_ge(*gated_ready.now(b, 1))
                        for t in range(TT):
                            last = nc.tensor.transpose(place[:, t * P:(t + 1) * P], o[:, t, n * P:(n + 1) * P],
                                                       ident32[:, :])
                    else:
                        if n == 0:
                            pe.wait_ge(*oT_ready.now(b, HH))
                        for hh in range(HH):
                            last = nc.tensor.matmul(place[:, :], oT[:, hh, n * P:(n + 1) * P], Wo[:, hh, :],
                                                    start=(hh == 0), stop=(hh == HH - 1))
                    last.then_inc(ring.done.sem, 1)


def linear_attention(nc, w, x1, spill):
    jobs = ([("xT", kt) for kt in range(KT)] + [(s, t) for s in "kv" for t in range(TT)]
            + [("kvT", 0), ("ksum", 0)])
    for h in range(QH + 1):
        if h < QH:
            jobs += [("q", h), ("M", h)]
        if h > 0:
            jobs += [("norm", h - 1)] + [("head", h - 1, t) for t in range(TT)]

    with ExitStack() as ctx:
        def sb(name, shape, dt=F32):
            return ctx.enter_context(nc.sbuf_tensor("l_" + name, shape, dt))

        def signal(name, per, unit=1):
            return Signal(ctx, nc, "l_" + name, per, unit)

        Wkv = {s: sb("W" + s, [P, KT, KVH * D]) for s in "kv"}
        Wq = sb("Wq", [P, KT, QH * D])
        Wo = sb("Wo", [P, QH, C])
        bkv = {s: sb("b" + s, [P, KVH * D]) for s in "kv"}
        bq = sb("bq", [P, QH])
        ident = sb("ident", [P, P])
        ones = sb("ones", [P, 1])
        half = sb("half", [P, TT])
        x_tok = sb("x_tok", [P, TT, C])
        stats = sb("stats", [P, TT, 6])
        mv = sb("mv", [P, TT, 2])
        veps = sb("veps", [P, TT])
        pause = sb("pause", [P, 1])
        rstd = sb("rstd", [P, TT])
        xn = sb("xn", [P, TT, C])
        xT = sb("xT", [P, KT, T])
        biased = [sb(f"biased{i}", [P, C]) for i in range(2)]
        expk = [sb(f"expk{i}", [P, C]) for i in range(2)]
        sk = sb("sk", [P, TT, KVH * D])
        v = sb("v", [P, TT, KVH * D])
        kvT = sb("kvT", [P, KVH, D])
        ksum = sb("ksum", [P, KVH])
        expq = [sb(f"expq{i}", [P, T]) for i in range(2)]
        reluq = [sb(f"reluq{i}", [P, T]) for i in range(2)]
        sq = [sb(f"sq{i}", [P, T]) for i in range(2)]
        M = [sb(f"M{i}", [P, C]) for i in range(2)]
        norm = [sb(f"norm{i}", [P, TT]) for i in range(2)]
        inv = [sb(f"inv{i}", [P, TT]) for i in range(2)]
        acc = sb("acc", [P, TT, C])
        banks = [ctx.enter_context(nc.psum_tensor(f"l_ps{i}", [P, 512], F32)) for i in range(8)]

        w_loaded = ctx.enter_context(nc.semaphore("l_w_loaded"))
        wkv_loaded = ctx.enter_context(nc.semaphore("l_wkv_loaded"))
        wqo_loaded = [ctx.enter_context(nc.semaphore(f"l_wqo_loaded{i}")) for i in range(4)]
        const_set = ctx.enter_context(nc.semaphore("l_const_set"))
        x_loaded = signal("x_loaded", 1, 16)
        stats_ready = signal("stats_ready", 1)
        mv_ready = signal("mv_ready", 1)
        var_ready = signal("var_ready", 1)
        rstd_ready = signal("rstd_ready", 1)
        xn_ready = signal("xn_ready", TT)
        xT_ready = signal("xT_ready", KT)
        biased_ready = signal("biased_ready", TT)
        expk_ready = signal("expk_ready", TT)
        mink_ready = signal("mink_ready", TT)
        sk_ready = signal("sk_ready", TT)
        v_ready = signal("v_ready", TT)
        kvT_ready = signal("kvT_ready", 1)
        ksum_ready = signal("ksum_ready", 1)
        expq_ready = signal("expq_ready", QH)
        reluq_ready = signal("reluq_ready", QH)
        minq_ready = signal("minq_ready", QH)
        sq_ready = signal("sq_ready", QH)
        M_ready = signal("M_ready", QH)
        norm_ready = signal("norm_ready", QH)
        inv_ready = signal("inv_ready", QH)
        acc_ready = signal("acc_ready", QH * TT)
        xT_stored = signal("xT_stored", 1, 16)
        s_stored = signal("s_stored", 1, 16)

        reader = {("kvT", 0): (kvT_ready, 1), ("ksum", 0): (ksum_ready, 1)}
        for kt in range(KT):
            reader["xT", kt] = (xT_ready, kt + 1)
        for t in range(TT):
            reader["k", t] = (biased_ready, t + 1)
            reader["v", t] = (v_ready, t + 1)
        for h in range(QH):
            reader["q", h] = (minq_ready, h + 1)
            reader["M", h] = (M_ready, h + 1)
            reader["norm", h] = (norm_ready, h + 1)
            for t in range(TT):
                reader["head", h, t] = (acc_ready, h * TT + t + 1)
        ring = Ring(ctx, nc, "l", banks, jobs, reader)

        block = ctx.enter_context(nc.Block())

        @block.sync
        def _(sp):
            for dst, name in ((ident, "ident"), (bkv["k"], "bk"), (bkv["v"], "bv"), (bq, "bq")):
                sp.dma_start(dst[:, :], w[name]).then_inc(w_loaded, 16)
            for s in [x_loaded, xT_stored, s_stored]:
                s.ahead(sp)

            def load_x(b):
                sp.wait_ge(*xn_ready.before(b, TT))
                sp.dma_start(x_tok[:, :, :], rows(x1, b)).then_inc(x_loaded.sem, 16)

            def store(b):
                sp.wait_ge(*xT_ready.now(b, KT))
                sp.dma_start(slab(spill["x2"], b), flat(xT[:, :, :])).then_inc(xT_stored.sem, 16)
                sp.wait_ge(*acc_ready.now(b, QH * TT))
                sp.dma_start(slab(spill["s"], b), flat(acc[:, :, :])).then_inc(s_stored.sem, 16)

            load_x(0)
            for s in "kv":
                sp.dma_start(flat(Wkv[s][:, :, :]), w["W" + s + "1"]).then_inc(wkv_loaded, 16)
            for i in range(4):
                for dst, name, n in ((Wq, "Wq1", QH * D // 4), (Wo, "Wo1", QH // 4)):
                    if name == "Wq1":
                        sp.dma_start(Wq[:, :, i * n:(i + 1) * n],
                                     w[name].rearrange("p (k c) -> p k c", k=KT)[:, :, i * n:(i + 1) * n]).then_inc(
                                         wqo_loaded[i], 16)
                    else:
                        sp.dma_start(flat(Wo[:, i * n:(i + 1) * n, :]), w[name][:, i * n * C:(i + 1) * n * C]).then_inc(
                            wqo_loaded[i], 16)
            store(0)
            with sp.Fori(1, B) as b:
                load_x(b)
                store(b)
            sp.wait_ge(xT_stored.sem, 16 * (B + 1))
            sp.wait_ge(s_stored.sem, 16 * (B + 1))

        @block.gpsimd
        def _(pool):
            nc.gpsimd.memset(half[:, :], -0.5).then_inc(const_set, 1)
            nc.gpsimd.memset(ones[:, :], 1.0).then_inc(const_set, 1)
            pool.wait_ge(const_set, 2)
            rstd_ready.ahead(pool)
            sq_ready.ahead(pool)
            with pool.Fori(0, B) as b:
                pool.wait_ge(*var_ready.now(b, 1))
                nc.gpsimd.tensor_tensor(rstd[:, :], veps[:, :], half[:, :], ALU.pow).then_inc(rstd_ready.sem, 1)
                for h in range(QH):
                    pool.wait_ge(*expq_ready.now(b, h + 1))
                    pool.wait_ge(*reluq_ready.now(b, h + 1))
                    pool.wait_ge(*(ring.product(("head", h - 2, TT - 1), b) if h >= 2 else
                                   ring.product_before(("head", QH - 2 + h, TT - 1), b)))
                    nc.gpsimd.tensor_tensor(sq[h % 2][:, :], expq[h % 2][:, :], reluq[h % 2][:, :],
                                            ALU.add).then_inc(sq_ready.sem, 1)

        @block.vector
        def _(dve):
            dve.wait_ge(w_loaded, 4 * 16)
            for s in (stats_ready, mv_ready, var_ready, xn_ready, biased_ready, mink_ready, sk_ready, v_ready,
                      minq_ready, norm_ready, inv_ready, acc_ready):
                s.ahead(dve)
            with dve.Fori(0, B) as b:
                dve.wait_ge(*x_loaded.now(b, 1))
                for t in range(TT):
                    last = nc.vector.bn_stats(stats[:, t, :], x_tok[:, t, :])
                last.then_inc(stats_ready.sem, 1)
                dve.wait_ge(*stats_ready.now(b, 1))
                nc.vector.memset(pause[:, :], 0.0)
                for t in range(TT):
                    last = nc.vector.bn_aggr(mv[:, t, :], stats[:, t, :])
                last.then_inc(mv_ready.sem, 1)
                dve.wait_ge(*mv_ready.now(b, 1))
                nc.vector.tensor_scalar(veps[:, :], mv[:, :, 1], 1e-5, None, ALU.add).then_inc(var_ready.sem, 1)
                dve.wait_ge(*rstd_ready.now(b, 1))
                dve.wait_ge(*ring.product_before(("xT", KT - 1), b))
                for t in range(TT):
                    nc.vector.tensor_scalar(xn[:, t, :], x_tok[:, t, :], mv[:, t, 0:1], rstd[:, t:t + 1],
                                            ALU.subtract, ALU.mult).then_inc(xn_ready.sem, 1)

                for t in range(TT):
                    dve.wait_ge(*ring.product(("k", t), b))
                    nc.vector.tensor_tensor(biased[t % 2][:, :], ring.place(("k", t))[:, :], bkv["k"][:, :],
                                            ALU.add).then_inc(biased_ready.sem, 1)
                    dve.wait_ge(*biased_ready.now(b, t + 1))
                    nc.vector.tensor_scalar(expk[t % 2][:, :], biased[t % 2][:, :], 0.0, None,
                                            ALU.min).then_inc(mink_ready.sem, 1)
                    dve.wait_ge(*expk_ready.now(b, t + 1))
                    nc.vector.scalar_tensor_tensor(sk[:, t, :], biased[t % 2][:, :], 0.0, expk[t % 2][:, :], ALU.max,
                                                   ALU.add).then_inc(sk_ready.sem, 1)
                for t in range(TT):
                    dve.wait_ge(*ring.product(("v", t), b))
                    nc.vector.tensor_tensor(v[:, t, :], ring.place(("v", t))[:, :], bkv["v"][:, :],
                                            ALU.add).then_inc(v_ready.sem, 1)
                for h in range(QH + 1):
                    if h < QH:
                        dve.wait_ge(*reluq_ready.now(b, h + 1))
                        dve.wait_ge(*(sq_ready.now(b, h - 1) if h >= 2 else sq_ready.before(b, QH - 1 + h)))
                        nc.vector.tensor_scalar(expq[h % 2][:, :], ring.place(("q", h))[:, :], bq[:, h:h + 1], 0.0,
                                                ALU.add, ALU.min).then_inc(minq_ready.sem, 1)
                    if h > 0:
                        g = h - 1
                        dve.wait_ge(*ring.product(("norm", g), b))
                        dve.wait_ge(*(inv_ready.now(b, g - 1) if g >= 2 else inv_ready.before(b, QH - 1 + g)))
                        nc.vector.tensor_scalar(norm[g % 2][:, :], ring.place(("norm", g))[:, 0:TT], 1e-6, None,
                                                ALU.add).then_inc(norm_ready.sem, 1)
                        dve.wait_ge(*norm_ready.now(b, g + 1))
                        dve.wait_ge(*(acc_ready.now(b, (g - 1) * TT) if g >= 2 else
                                      acc_ready.before(b, (QH - 1 + g) * TT)))
                        nc.vector.reciprocal(inv[g % 2][:, :], norm[g % 2][:, :]).then_inc(inv_ready.sem, 1)
                        dve.wait_ge(*inv_ready.now(b, g + 1))
                        if g == 0:
                            dve.wait_ge(*s_stored.before(b, 1))
                        for t in range(TT):
                            dve.wait_ge(*ring.product(("head", g, t), b))
                            ps = ring.place(("head", g, t))[:, :]
                            if g == 0:
                                last = nc.vector.tensor_scalar(acc[:, t, :], ps, inv[0][:, t:t + 1], None, ALU.mult)
                            else:
                                dve.wait_ge(*acc_ready.now(b, (g - 1) * TT + t + 1))
                                last = nc.vector.scalar_tensor_tensor(acc[:, t, :], ps, inv[g % 2][:, t:t + 1],
                                                                      acc[:, t, :], ALU.mult, ALU.add)
                            last.then_inc(acc_ready.sem, 1)

        @block.scalar
        def _(act):
            act.wait_ge(w_loaded, 4 * 16)
            for s in (xT_ready, expk_ready, kvT_ready, ksum_ready, reluq_ready, expq_ready, M_ready):
                s.ahead(act)
            with act.Fori(0, B) as b:
                act.wait_ge(*ring.product_before(("q", QH - 1), b))
                act.wait_ge(*xT_stored.before(b, 1))
                for kt in range(KT):
                    act.wait_ge(*ring.product(("xT", kt), b))
                    nc.scalar.activation(xT[:, kt, :], ring.place(("xT", kt))[:, :], ACT.Copy).then_inc(xT_ready.sem, 1)
                for t in range(TT):
                    act.wait_ge(*mink_ready.now(b, t + 1))
                    nc.scalar.activation(expk[t % 2][:, :], expk[t % 2][:, :], ACT.Exp).then_inc(expk_ready.sem, 1)
                act.wait_ge(*ring.product(("kvT", 0), b))
                nc.scalar.activation(flat(kvT[:, :, :]), ring.place(("kvT", 0))[:, :], ACT.Copy).then_inc(kvT_ready.sem, 1)
                act.wait_ge(*ring.product(("ksum", 0), b))
                nc.scalar.activation(ksum[:, :], ring.place(("ksum", 0))[:, 0:KVH], ACT.Copy).then_inc(ksum_ready.sem, 1)
                for h in range(QH):
                    act.wait_ge(*ring.product(("q", h), b))
                    act.wait_ge(*(sq_ready.now(b, h - 1) if h >= 2 else sq_ready.before(b, QH - 1 + h)))
                    nc.scalar.activation(reluq[h % 2][:, :], ring.place(("q", h))[:, :], ACT.Relu,
                                         bias=bq[:, h:h + 1]).then_inc(reluq_ready.sem, 1)
                    act.wait_ge(*minq_ready.now(b, h + 1))
                    nc.scalar.activation(expq[h % 2][:, :], expq[h % 2][:, :], ACT.Exp).then_inc(expq_ready.sem, 1)
                    act.wait_ge(*ring.product(("M", h), b))
                    act.wait_ge(*(ring.product(("head", h - 2, TT - 1), b) if h >= 2 else
                                  ring.product_before(("head", QH - 2 + h, TT - 1), b)))
                    nc.scalar.activation(M[h % 2][:, :], ring.place(("M", h))[:, :], ACT.Copy).then_inc(M_ready.sem, 1)

        @block.tensor
        def _(pe):
            pe.wait_ge(w_loaded, 4 * 16)
            pe.wait_ge(const_set, 2)
            ring.done.ahead(pe)
            with pe.Fori(0, B) as b:
                for job in jobs:
                    kind, n = job[0], job[1]
                    place = ring.place(job)
                    pe.wait_ge(*ring.vacated(job, b))
                    if kind == "xT":
                        for t in range(TT):
                            pe.wait_ge(*xn_ready.now(b, t + 1))
                            last = nc.tensor.transpose(place[:, t * P:(t + 1) * P], xn[:, t, n * P:(n + 1) * P],
                                                       ident[:, :])
                    elif kind in "kv":
                        if n == 0:
                            pe.wait_ge(wkv_loaded, 2 * 16)
                        for kt in range(KT):
                            pe.wait_ge(*xT_ready.now(b, kt + 1))
                            last = nc.tensor.matmul(place[:, :], xT[:, kt, n * P:(n + 1) * P], Wkv[kind][:, kt, :],
                                                    start=(kt == 0), stop=(kt == KT - 1))
                    elif kind == "kvT":
                        pe.wait_ge(*sk_ready.now(b, TT))
                        pe.wait_ge(*v_ready.now(b, TT))
                        for g in range(KVH):
                            for t in range(TT):
                                last = nc.tensor.matmul(place[:, g * D:(g + 1) * D], v[:, t, g * D:(g + 1) * D],
                                                        sk[:, t, g * D:(g + 1) * D], start=(t == 0),
                                                        stop=(t == TT - 1))
                    elif kind == "ksum":
                        for g in range(KVH):
                            for t in range(TT):
                                last = nc.tensor.matmul(place[:, g:g + 1], sk[:, t, g * D:(g + 1) * D], ones[:, :],
                                                        start=(t == 0), stop=(t == TT - 1))
                    elif kind == "q":
                        if n % (QH // 4) == 0:
                            pe.wait_ge(wqo_loaded[n // (QH // 4)], 2 * 16)
                        for kt in range(KT):
                            last = nc.tensor.matmul(place[:, :], Wq[:, kt, n * D:(n + 1) * D], xT[:, kt, :],
                                                    start=(kt == 0), stop=(kt == KT - 1))
                    elif kind == "M":
                        pe.wait_ge(*kvT_ready.now(b, 1))
                        last = nc.tensor.matmul(place[:, :], kvT[:, n // GROUPS, :], Wo[:, n, :], start=True, stop=True)
                    elif kind == "norm":
                        pe.wait_ge(*sq_ready.now(b, n + 1))
                        pe.wait_ge(*ksum_ready.now(b, 1))
                        for t in range(TT):
                            last = nc.tensor.matmul(place[:, t:t + 1], sq[n % 2][:, t * P:(t + 1) * P],
                                                    ksum[:, n // GROUPS:n // GROUPS + 1], start=True, stop=True)
                    else:
                        t = job[2]
                        pe.wait_ge(*M_ready.now(b, n + 1))
                        last = nc.tensor.matmul(place[:, :], sq[n % 2][:, t * P:(t + 1) * P], M[n % 2][:, :],
                                                start=True, stop=True)
                    last.then_inc(ring.done.sem, 1)


def relu_gate(nc, w, x1, spill, out):
    with ExitStack() as ctx:
        def sb(name, shape, dt=F32):
            return ctx.enter_context(nc.sbuf_tensor("g_" + name, shape, dt))

        def signal(name, per, unit=1):
            return Signal(ctx, nc, "g_" + name, per, unit)

        Wup = sb("Wup", [P, KT, I1])
        Wdn = sb("Wdn", [P, UT, C])
        up_a, up_b = sb("up_a", [RANK, C]), sb("up_b", [RANK, I1])
        dn_a, dn_b = sb("dn_a", [RANK, I1]), sb("dn_b", [RANK, C])
        up_scale, dn_scale = sb("up_scale", [8, I1]), sb("dn_scale", [32, C])
        up_pick, dn_pick = sb("up_pick", [8, P]), sb("dn_pick", [32, UT, P])
        b_up = sb("b_up", [P, UT])
        b_dn = sb("b_dn", [P, C])
        xT = [sb(f"xT{i}", [P, KT, T]) for i in range(1)]
        x2 = [sb(f"x2{i}", [P, T]) for i in range(3)]
        z = sb("z", [P, TT, C])
        tanh_z = [sb(f"tanh_z{i}", [P, C]) for i in range(2)]
        s = sb("s", [P, TT, C])
        xs = sb("xs", [P, TT, C])
        banks = [ctx.enter_context(nc.psum_tensor(f"g_ps{i}", [P, 512], F32)) for i in range(8)]

        small_loaded = ctx.enter_context(nc.semaphore("g_small_loaded"))
        up_loaded = [ctx.enter_context(nc.semaphore(f"g_up_loaded{i}")) for i in range(4)]
        dn_loaded = [ctx.enter_context(nc.semaphore(f"g_dn_loaded{i}")) for i in range(4)]
        expansion = ctx.enter_context(nc.semaphore("g_expansion"))
        expanded = ctx.enter_context(nc.semaphore("g_expanded"))
        xT_loaded = signal("xT_loaded", 1, 16)
        s_loaded = signal("s_loaded", 1, 32)
        x2_ready = signal("x2_ready", UT)
        x2_used = signal("x2_used", UT - 1)
        z_ready = signal("z_ready", TT)
        tanh_z_ready = signal("tanh_z_ready", TT)
        u_ready = signal("u_ready", TT)
        sg_ready = signal("sg_ready", TT)
        out_ready = signal("out_ready", TT)
        out_stored = signal("out_stored", 1, 16)
        U = Ring(ctx, nc, "g_U", banks[0:4], [("up", j) for j in range(UT)],
                 {("up", j): (x2_ready, j + 1) for j in range(UT)})
        Y = Ring(ctx, nc, "g_Y", banks[4:8], [("down", t) for t in range(TT)],
                 {("down", t): (z_ready, t + 1) for t in range(TT)})

        OB = I1 // C
        items = []
        for ob in range(OB):
            items.append((("up_scale", ob), 8 * ob + 7))
            items += [(("up_lora", ob, kt), 8 * ob + 2 * kt + 2) for kt in range(KT)]
        for j in range(UT):
            items += [(("dn_scale", j), 8 * OB + 2 * j + 1), (("dn_lora", j), 8 * OB + 2 * j + 2)]
        at = {item: i for i, (item, _) in enumerate(items)}

        block = ctx.enter_context(nc.Block())

        @block.sync
        def _(sp):
            for dst, name in ((up_a, "up_a"), (up_b, "up_b"), (dn_a, "dn_a"), (dn_b, "dn_b"),
                              (up_scale, "up_scale"), (dn_scale, "dn1_scale"), (up_pick, "up_pick"),
                              (b_up, "b_up"), (b_dn, "b_dn")):
                sp.dma_start(dst[:, :], w[name]).then_inc(small_loaded, 16)
            sp.dma_start(flat(dn_pick[:, :, :]), w["dn_pick"]).then_inc(small_loaded, 16)
            for i in range(4):
                sp.dma_start(Wup[:, :, i * C:(i + 1) * C].bitcast(I32),
                             w["up_q"].rearrange("p (k c) -> p k c", k=KT)[:, :, i * C:(i + 1) * C]).then_inc(
                                 up_loaded[i], 16)
            for i in range(4):
                n = UT // 4
                sp.dma_start(flat(Wdn[:, i * n:(i + 1) * n, :]).bitcast(I32),
                             w["dn_q"][:, i * n * C:(i + 1) * n * C]).then_inc(dn_loaded[i], 16)
            for q in (xT_loaded, s_loaded, out_stored):
                q.ahead(sp)
            with sp.Fori(0, B) as b:
                sp.wait_ge(*U.product_before(("up", UT - 1), b))
                sp.dma_start(flat(xT[0][:, :, :]), slab(spill["x2"], b)).then_inc(xT_loaded.sem, 16)
                sp.wait_ge(*out_stored.before(b, 1))
                sp.dma_start(flat(s[:, :, :]), slab(spill["s"], b)).then_inc(s_loaded.sem, 16)
                sp.dma_start(xs[:, :, :], rows(x1, b)).then_inc(s_loaded.sem, 16)
                sp.wait_ge(*out_ready.now(b, TT))
                sp.dma_start(rows(out, b), xs[:, :, :]).then_inc(out_stored.sem, 16)
            sp.wait_ge(out_stored.sem, 16 * (B + 1))

        @block.gpsimd
        def _(pool):
            out_ready.ahead(pool)
            with pool.Fori(0, B) as b:
                for t in range(TT):
                    pool.wait_ge(*sg_ready.now(b, t + 1))
                    nc.gpsimd.tensor_tensor(xs[:, t, :], xs[:, t, :], s[:, t, :], ALU.add).then_inc(out_ready.sem, 1)

        @block.vector
        def _(dve):
            for q in (z_ready, u_ready, sg_ready):
                q.ahead(dve)
            step = 0
            for ob in range(OB):
                dve.wait_ge(up_loaded[ob], 16)
                cols = slice(ob * C, (ob + 1) * C)
                for kt in range(KT):
                    i = at["up_scale", ob]
                    dve.wait_ge(expansion, i + 1)
                    nc.vector.scalar_tensor_tensor(Wup[:, kt, cols], Wup[:, kt, cols].bitcast(I32), -7.5,
                                                   banks[i % 8][:, :], ALU.add, ALU.mult).then_inc(expanded, 1)
                    i = at["up_lora", ob, kt]
                    dve.wait_ge(expansion, i + 1)
                    dve.wait_ge(expanded, step + 1)
                    nc.vector.tensor_tensor(Wup[:, kt, cols], Wup[:, kt, cols], banks[i % 8][:, :],
                                            ALU.add).then_inc(expanded, 1)
                    step += 2
            for j in range(UT):
                dve.wait_ge(dn_loaded[j // 4], 16)
                i = at["dn_scale", j]
                dve.wait_ge(expansion, i + 1)
                nc.vector.scalar_tensor_tensor(Wdn[:, j, :], Wdn[:, j, :].bitcast(I32), -7.5, banks[i % 8][:, :],
                                               ALU.add, ALU.mult).then_inc(expanded, 1)
                i = at["dn_lora", j]
                dve.wait_ge(expansion, i + 1)
                dve.wait_ge(expanded, step + 1)
                nc.vector.tensor_tensor(Wdn[:, j, :], Wdn[:, j, :], banks[i % 8][:, :], ALU.add).then_inc(expanded, 1)
                step += 2
            with dve.Fori(0, B) as b:
                for t in range(TT):
                    dve.wait_ge(*Y.product(("down", t), b))
                    dve.wait_ge(*sg_ready.before(b, t + 1))
                    nc.vector.tensor_tensor(z[:, t, :], Y.place(("down", t))[:, :], b_dn[:, :],
                                            ALU.add).then_inc(z_ready.sem, 1)
                dve.wait_ge(*s_loaded.now(b, 1))
                for t in range(TT):
                    dve.wait_ge(*tanh_z_ready.now(b, t + 1))
                    nc.vector.scalar_tensor_tensor(z[:, t, :], tanh_z[t % 2][:, :], 1.0, z[:, t, :], ALU.add,
                                                   ALU.mult).then_inc(u_ready.sem, 1)
                    dve.wait_ge(*u_ready.now(b, t + 1))
                    nc.vector.scalar_tensor_tensor(s[:, t, :], s[:, t, :], 0.5, z[:, t, :], ALU.mult,
                                                   ALU.mult).then_inc(sg_ready.sem, 1)

        @block.scalar
        def _(act):
            act.wait_ge(small_loaded, 10 * 16)
            for q in (x2_ready, tanh_z_ready):
                q.ahead(act)
            with act.Fori(0, B) as b:
                for j in range(UT):
                    act.wait_ge(*U.product(("up", j), b))
                    act.wait_ge(*(x2_used.now(b, j - 2) if j >= 3 else Y.product_before(("down", TT - 1), b)))
                    nc.scalar.activation(x2[j % 3][:, :], U.place(("up", j))[:, :], ACT.Relu,
                                         bias=b_up[:, j:j + 1]).then_inc(x2_ready.sem, 1)
                for t in range(TT):
                    act.wait_ge(*z_ready.now(b, t + 1))
                    act.wait_ge(*(u_ready.now(b, t - 1) if t >= 2 else u_ready.before(b, TT - 1 + t)))
                    nc.scalar.activation(tanh_z[t % 2][:, :], z[:, t, :], ACT.Tanh,
                                         scale=0.5).then_inc(tanh_z_ready.sem, 1)

        @block.tensor
        def _(pe):
            pe.wait_ge(small_loaded, 10 * 16)
            for q in (U.done, Y.done, x2_used):
                q.ahead(pe)
            for i, (item, _) in enumerate(items):
                if i >= 8:
                    pe.wait_ge(expanded, items[i - 8][1])
                kind, n = item[0], item[1]
                if kind == "up_scale":
                    lhs, rhs = up_pick[:, :], up_scale[:, n * C:(n + 1) * C]
                elif kind == "up_lora":
                    lhs, rhs = up_a[:, item[2] * P:(item[2] + 1) * P], up_b[:, n * C:(n + 1) * C]
                elif kind == "dn_scale":
                    lhs, rhs = dn_pick[:, n, :], dn_scale[:, :]
                else:
                    lhs, rhs = dn_a[:, n * P:(n + 1) * P], dn_b[:, :]
                nc.tensor.matmul(banks[i % 8][:, :], lhs, rhs, start=True, stop=True).then_inc(expansion, 1)
            pe.wait_ge(expanded, 8 * OB + 2 * UT)
            with pe.Fori(0, B) as b:
                pe.wait_ge(*xT_loaded.now(b, 1))
                for j in range(UT + 1):
                    if j < UT:
                        pe.wait_ge(*U.vacated(("up", j), b))
                        for kt in range(KT):
                            last = nc.tensor.matmul(U.place(("up", j))[:, :], Wup[:, kt, j * P:(j + 1) * P],
                                                    xT[0][:, kt, :], start=(kt == 0), stop=(kt == KT - 1))
                        last.then_inc(U.done.sem, 1)
                    if j > 0:
                        i = j - 1
                        pe.wait_ge(*x2_ready.now(b, i + 1))
                        for t in range(TT):
                            if i == 0:
                                pe.wait_ge(*Y.vacated(("down", t), b))
                            last = nc.tensor.matmul(Y.place(("down", t))[:, :], x2[i % 3][:, t * P:(t + 1) * P],
                                                    Wdn[:, i, :], start=(i == 0), stop=(i == UT - 1))
                            if i == UT - 1:
                                last.then_inc(Y.done.sem, 1)
                        if i < UT - 1:
                            last.then_inc(x2_used.sem, 1)


SCRATCH = {"x": KT * T, "r": HH * T, "k": HH * T, "v": HH * T, "w": HH * T, "g": TT * KD,
           "x2": KT * T, "s": TT * C}


def layouts(inputs):
    a = {k: np.asarray(v) for k, v in inputs.items()}

    def tiles(m, order=None):
        m = m if order is None else m[order]
        n = m.shape[0] // P
        return m.reshape(n, P, -1).transpose(1, 0, 2).reshape(P, -1)

    def every(v):
        return np.broadcast_to(v, (P,) + v.shape)

    o = {}
    o["x"] = a["L0_attn_x"].reshape(B * T, C)[:, CHANNELS]
    o["ident"] = np.eye(P, dtype=np.float32)
    o["front"] = tiles(np.concatenate([a["L0_attn_Wx1"], a["L0_attn_Wr"], a["L0_attn_Wk"], a["L0_attn_Wv"],
                                       a["L0_attn_Ww_a"], a["L0_attn_Wg_a"]], axis=1), CHANNELS)
    x2 = a["L0_attn_Wx2"][CHANNELS].transpose(1, 2, 0)
    pad = np.concatenate([x2, x2[4:5]])
    o["Wx2"] = pad.reshape(3, 2 * LOW, C).transpose(1, 0, 2).reshape(P, -1)
    o["Wb"] = np.concatenate([a["L0_attn_Ww_b"], a["L0_attn_Wg_b"]], axis=1)
    o["front_col"] = np.concatenate([tiles(a["L0_attn_mu_x"][:, None], CHANNELS),
                                     a["L0_attn_x_bias"][:, CHANNELS].reshape(5 * KT, P).T,
                                     a["L0_attn_bw"].reshape(HH, P).T], axis=1)
    o["bg"] = every(a["L0_attn_bg"])
    hidden = np.concatenate([HIDDEN0, I0 + HIDDEN0])
    o["gu_words"] = np.tile(a["L0_ffn_gate_up_packed"][hidden].T, (2, 1))
    o["gu_scale"] = a["L0_ffn_gate_up_scales"][:, hidden][np.arange(P) % 64 // 16]
    words = a["L0_ffn_down_packed"][CHANNELS].T.reshape(JT, 16, C)
    words = np.concatenate([words, words[:B * DQ - JT]])
    o["dn_words"] = np.tile(words.transpose(1, 0, 2), (8, 1, 1)).reshape(P, -1)
    scale = a["L0_ffn_down_scales"][:, CHANNELS]
    o["dn_scale"] = every(np.concatenate([scale, scale[:B * DQ - JT]]).reshape(-1))
    nibble = [2 * jj + np.arange(P) // 64 for jj in range(2)] + [np.arange(P) // 16 % 4]
    o["shift"] = np.stack([12 - 4 * j for j in nibble], axis=1).astype(np.int32)
    key = np.arange(P)
    o["spread"] = np.stack([(key[:, None] // DK == key // DK) & (key[:, None] % DK == v) for v in range(DK)],
                           axis=1).astype(np.float32).reshape(P, -1)
    o["heads"] = (key[:, None] // DK == np.arange(HPT)).astype(np.float32)
    o["bonus"] = a["L0_attn_bonus"].reshape(HH, P).T
    o["lnw"] = every(np.tile(a["L0_attn_ln_w"], NH))
    o["lnb"] = every(np.tile(a["L0_attn_ln_b"], NH))
    o["Wo0"] = tiles(a["L0_attn_Wo"][:, CHANNELS])
    for s in "kv":
        o[f"W{s}1"] = tiles(a[f"L1_attn_W{s}"].T, CHANNELS)
        o["b" + s] = every(a["L1_attn_b" + s])
    o["Wq1"] = tiles(a["L1_attn_Wq"].T, CHANNELS)
    o["bq"] = a["L1_attn_bq"].reshape(QH, D).T
    o["Wo1"] = tiles(a["L1_attn_Wo"].T[:, CHANNELS])
    o["up_q"] = tiles(a["L1_ffn_w_up_q"].T, CHANNELS)
    o["up_a"] = a["L1_ffn_w_up_lora_a"][CHANNELS].T
    o["up_b"] = a["L1_ffn_w_up_lora_b"]
    o["dn_q"] = tiles(a["L1_ffn_w_down_q"][CHANNELS].T)
    o["dn_a"] = a["L1_ffn_w_down_lora_a"].T
    o["dn_b"] = a["L1_ffn_w_down_lora_b"][:, CHANNELS]
    o["up_scale"] = a["L1_ffn_w_up_scale"].T
    o["dn1_scale"] = a["L1_ffn_w_down_scale"][CHANNELS].T
    o["up_pick"] = (key % 64 // 8 == np.arange(8)[:, None]).astype(np.float32)
    o["dn_pick"] = np.stack([2 * j + key // 64 == np.arange(32)[:, None] for j in range(UT)],
                            axis=1).astype(np.float32).reshape(32, -1)
    o["b_up"] = a["L1_ffn_b_up"].reshape(UT, P).T
    o["b_dn"] = every(a["L1_ffn_b_down"][CHANNELS])
    return {k: np.ascontiguousarray(v) for k, v in o.items()}


def build(nc, w, out):
    def scratch(name, shape):
        return nc.dram_tensor("scratch_" + name, shape, F32, kind="Internal").ap()

    spill = {k: scratch(k, (B * P, n)) for k, n in SCRATCH.items()}
    x1 = scratch("x1", (B * T, C))
    with ExitStack() as ctx:
        Wgu = ctx.enter_context(nc.sbuf_tensor("Wgu", [P, KT, 2 * I0], F32))
        Wdn = ctx.enter_context(nc.sbuf_tensor("Wdn", [P, B * DQ, C], F32))
        front(nc, w, w["x"], spill, Wgu, Wdn)
        recurrence_and_gate(nc, w, w["x"], spill, Wgu, Wdn, x1)
    linear_attention(nc, w, x1, spill)
    relu_gate(nc, w, x1, spill, out)


def kernel(**inputs):
    import concourse.bacc as bacc
    from concourse.bass_utils import run_bass_kernel_spmd as run

    nc = bacc.Bacc("TRN2", target_bir_lowering=False, num_devices=1)
    arrays = {"in_" + k: v for k, v in layouts(inputs).items()}
    w = {k[3:]: nc.dram_tensor(k, v.shape, mybir.dt.from_np(v.dtype), kind="ExternalInput").ap()
         for k, v in arrays.items()}
    out = nc.dram_tensor("out", (B * T, C), F32, kind="ExternalOutput").ap()
    build(nc, w, out)
    r = run(nc, [arrays], core_ids=[0])
    return np.ascontiguousarray(r.results[0]["out"][:, np.argsort(CHANNELS)].reshape(B, T, C))
```

```python
import numpy as np
import concourse.bass as bass
from concourse import mybir
from contextlib import ExitStack

F32 = mybir.dt.float32
F32R = mybir.dt.float32r
F16 = mybir.dt.float16
I32 = mybir.dt.int32
U32 = mybir.dt.uint32
ALU = mybir.AluOpType
ACT = mybir.ActivationFunctionType
AX = mybir.AxisListType

P = 128
B = 4
T = 512
TT = T // P
C = 512
KT = C // P
NH, DK = 16, 16
KD = NH * DK
HH = KD // P
HPT = P // DK
LOW = 64
I0 = 1408
JT = I0 // P
QH, KVH, D = 16, 4, 128
GROUPS = QH // KVH
I1 = 2048
UT = I1 // P
RANK = 16

CHANNELS = np.array([8 * (p % 64) + 2 * kt + p // 64 for kt in range(KT) for p in range(P)])
HIDDEN0 = np.array([P * m + 8 * (p % 16) + p // 16 for m in range(JT) for p in range(P)])


GQ = 2 * I0 // B
DQ = -(-JT // B)
UNPACK_STEPS = 3 * (2 + DQ)


class Signal:

    def __init__(self, ctx, nc, name, per, unit=1):
        self.sem, self.per, self.unit = ctx.enter_context(nc.semaphore(name)), per, unit

    def ahead(self, eng):
        eng.sem_inc(self.sem, self.per * self.unit)

    def now(self, b, k):
        return self.sem, b * (self.per * self.unit) + (self.per + k) * self.unit

    def before(self, b, k):
        return self.sem, b * (self.per * self.unit) + k * self.unit


class Ring:

    def __init__(self, ctx, nc, name, places, jobs, reader):
        self.places, self.n, self.jobs, self.reader = places, len(places), jobs, reader
        self.index = {job: i for i, job in enumerate(jobs)}
        assert len(self.index) == len(jobs) >= self.n
        self.done = Signal(ctx, nc, name + "_product", len(jobs))

    def slot(self, job):
        return self.index[job] % self.n

    def place(self, job):
        return self.places[self.slot(job)]

    def product(self, job, b):
        return self.done.now(b, self.index[job] + 1)

    def product_before(self, job, b):
        return self.done.before(b, self.index[job] + 1)

    def vacated(self, job, b):
        i = self.index[job]
        if i >= self.n:
            signal, k = self.reader[self.jobs[i - self.n]]
            return signal.now(b, k)
        last = max(j for j in range(len(self.jobs)) if j % self.n == i)
        signal, k = self.reader[self.jobs[last]]
        return signal.before(b, k)


def rows(ap, b):
    return ap[bass.ds(b * T, T), :].rearrange("(t p) c -> p t c", p=P)


def slab(ap, b):
    return ap[bass.ds(b * P, P), :]


def flat(ap):
    return ap.rearrange("p a b -> p (a b)")


def front(nc, w, x, spill, Wgu, Wdn):
    MIX = ["r", "w", "k", "v", "g"]
    ORDER = [2, 0, 3, 1, 4]
    N_MIX = len(ORDER) * KT

    def mixes(n):
        return [("mix", n, kt) for kt in range(KT)]

    def projections(n):
        return [("proj", n, hh) for hh in range(HH)] if MIX[ORDER[n]] in "rkv" else [("down", n)]

    jobs = [("xT", kt) for kt in range(KT)] + [("low", m) for m in range(3)] + mixes(0)
    for n in range(1, len(ORDER)):
        jobs += mixes(n) + projections(n - 1)
    jobs += [("decay", hh) for hh in range(HH)] + projections(4) + [("gate", h) for h in range(2)]

    with ExitStack() as ctx:
        def sb(name, shape, dt=F32):
            return ctx.enter_context(nc.sbuf_tensor("f_" + name, shape, dt))

        def signal(name, per, unit=1):
            return Signal(ctx, nc, "f_" + name, per, unit)

        W = sb("W", [P, KT, 1216])
        Wx1 = W[:, :, 0:320]
        Wproj = {"r": W[:, :, 320:576], "k": W[:, :, 576:832], "v": W[:, :, 832:1088]}
        Wdown = {"w": W[:, :, 1088:1152], "g": W[:, :, 1152:1216]}
        Wx2 = sb("Wx2", [P, 3, C])
        Wb = sb("Wb", [LOW, 2, KD])
        col = sb("col", [P, 6 * KT + HH])
        mu_x = col[:, 0:KT]
        bias = col[:, KT:6 * KT]
        bw = col[:, 6 * KT:6 * KT + HH]
        bg = sb("bg", [P, KD])
        ident = sb("ident", [P, P])
        x_tok = sb("x_tok", [P, TT, C])
        stats = sb("stats", [P, TT, 6])
        mv = sb("mv", [P, TT, 2])
        veps = sb("veps", [P, TT])
        pause = sb("pause", [P, 1])
        half = sb("half", [P, TT])
        rstd = sb("rstd", [P, TT])
        xT = sb("xT", [P, KT, T + 2])
        delta = sb("delta", [P, KT, T])
        mixed = [sb(f"mixed{i}", [P, KT, T]) for i in range(2)]
        xn = mixed[1]
        low = sb("low", [P, 3, T])
        tlow = {s: sb("tlow" + s, [LOW, T]) for s in "wg"}
        out = {s: sb("out" + s, [P, HH, T]) for s in "rkvw"}
        expw = sb("expw", [P, T])
        gu_words = sb("gu_words", [P, GQ], U32)
        gu_scale = sb("gu_scale", [P, GQ], F16)
        dn_words = sb("dn_words", [P, DQ, C], U32)
        dn_scale = sb("dn_scale", [P, DQ, C], F16)
        shift = sb("shift", [P, 3], I32)
        shifted = sb("shifted", [P, GQ], U32)
        value = sb("value", [P, GQ], U32)
        g = sb("g", [P, TT, KD])
        tanhg = sb("tanhg", [P, TT, KD])
        gate = sb("gate", [P, TT, KD])
        banks = [ctx.enter_context(nc.psum_tensor(f"f_ps{i}", [P, 512], F32)) for i in range(8)]

        w_loaded = ctx.enter_context(nc.semaphore("f_w_loaded"))
        const_set = ctx.enter_context(nc.semaphore("f_const_set"))
        x_loaded = signal("x_loaded", 1, 16)
        stats_ready = signal("stats_ready", 1)
        mv_ready = signal("mv_ready", 1)
        var_ready = signal("var_ready", 1)
        rstd_ready = signal("rstd_ready", 1)
        xn_ready = signal("xn_ready", TT)
        xT_ready = signal("xT_ready", KT)
        delta_ready = signal("delta_ready", KT)
        x_mixed = signal("x_mixed", KT)
        part_ready = signal("part_ready", N_MIX)
        mix_ready = signal("mix_ready", N_MIX)
        low_ready = signal("low_ready", 3)
        tlow_ready = signal("tlow_ready", 2)
        out_ready = {s: signal("out_ready" + s, HH) for s in "rkvw"}
        expw_ready = signal("expw_ready", HH)
        g_ready = signal("g_ready", 2)
        tanhg_ready = signal("tanhg_ready", 2)
        gate_ready = signal("gate_ready", 2)
        packed_loaded = signal("packed_loaded", 1, 64)
        unpack_step = signal("unpack_step", UNPACK_STEPS)
        unpacked = signal("unpacked", 2 + DQ)
        stored = {s: signal("stored" + s, 1, 16) for s in "xrkvwg"}

        reader = {}
        for job in jobs:
            kind, n = job[0], job[1]
            if kind == "xT":
                reader[job] = (xT_ready, n + 1)
            elif kind == "low":
                reader[job] = (low_ready, n + 1)
            elif kind == "mix":
                reader[job] = (part_ready, n * KT + job[2] + 1)
            elif kind == "proj":
                reader[job] = (out_ready[MIX[ORDER[n]]], job[2] + 1)
            elif kind == "down":
                reader[job] = (tlow_ready, 1 if MIX[ORDER[n]] == "w" else 2)
            elif kind == "decay":
                reader[job] = (expw_ready, n + 1)
            else:
                reader[job] = (g_ready, n + 1)
        ring = Ring(ctx, nc, "f", banks, jobs, reader)

        def last_reader(use):
            return ("low", 2) if use == 0 else projections(use - 1)[-1]

        block = ctx.enter_context(nc.Block())

        @block.sync
        def _(sp):
            sp.dma_start(ident[:, :], w["ident"]).then_inc(w_loaded, 16)
            sp.dma_start(flat(W[:, :, :]), w["front"]).then_inc(w_loaded, 16)
            sp.dma_start(flat(Wx2[:, :, :]), w["Wx2"]).then_inc(w_loaded, 16)
            sp.dma_start(flat(Wb[:, :, :]), w["Wb"]).then_inc(w_loaded, 16)
            sp.dma_start(col[:, :], w["front_col"]).then_inc(w_loaded, 16)
            sp.dma_start(bg[:, :], w["bg"]).then_inc(w_loaded, 16)
            sp.dma_start(shift[:, :], w["shift"]).then_inc(w_loaded, 16)
            for s in [x_loaded, packed_loaded, *stored.values()]:
                s.ahead(sp)
            with sp.Fori(0, B) as b:
                sp.wait_ge(*xn_ready.before(b, TT))
                sp.dma_start(x_tok[:, :, :], rows(x, b)).then_inc(x_loaded.sem, 16)
                sp.wait_ge(*unpacked.before(b, 2 + DQ))
                sp.dma_start(gu_words[:, :].bitcast(I32), w["gu_words"][:, bass.ds(b * GQ, GQ)]).then_inc(packed_loaded.sem, 16)
                sp.dma_start(gu_scale[:, :], w["gu_scale"][:, bass.ds(b * GQ, GQ)]).then_inc(packed_loaded.sem, 16)
                sp.dma_start(flat(dn_words[:, :, :]).bitcast(I32),
                             w["dn_words"][:, bass.ds(b * (DQ * C), DQ * C)]).then_inc(packed_loaded.sem, 16)
                sp.dma_start(flat(dn_scale[:, :, :]),
                             w["dn_scale"][:, bass.ds(b * (DQ * C), DQ * C)]).then_inc(packed_loaded.sem, 16)
                sp.wait_ge(*xT_ready.now(b, KT))
                sp.dma_start(slab(spill["x"], b).rearrange("p (n t) -> p n t", n=KT),
                             xT[:, :, 2:T + 2]).then_inc(stored["x"].sem, 16)
                for s in "krvw":
                    sp.wait_ge(*out_ready[s].now(b, HH))
                    sp.dma_start(slab(spill[s], b), flat(out[s][:, :, :])).then_inc(stored[s].sem, 16)
                sp.wait_ge(*gate_ready.now(b, 2))
                sp.dma_start(slab(spill["g"], b), flat(gate[:, :, :])).then_inc(stored["g"].sem, 16)
            for s in stored.values():
                sp.wait_ge(s.sem, 16 * (B + 1))

        @block.gpsimd
        def _(pool):
            nc.gpsimd.memset(half[:, :], -0.5).then_inc(const_set, 1)
            nc.gpsimd.memset(xT[:, :, 0:2], 0.0).then_inc(const_set, 1)
            pool.wait_ge(const_set, 2)
            for s in (rstd_ready, delta_ready, mix_ready):
                s.ahead(pool)
            with pool.Fori(0, B) as b:
                pool.wait_ge(*var_ready.now(b, 1))
                nc.gpsimd.tensor_tensor(rstd[:, :], veps[:, :], half[:, :], ALU.pow).then_inc(rstd_ready.sem, 1)
                for kt in range(KT):
                    pool.wait_ge(*xT_ready.now(b, kt + 1))
                    nc.gpsimd.tensor_tensor(delta[:, kt, :], xT[:, kt, 1:T + 1], xT[:, kt, 2:T + 2],
                                            ALU.subtract).then_inc(delta_ready.sem, 1)
                for n in range(len(ORDER)):
                    for kt in range(KT):
                        m = mixed[(n + 1) % 2][:, kt, :]
                        pool.wait_ge(*part_ready.now(b, n * KT + kt + 1))
                        nc.gpsimd.tensor_tensor(m, m, xT[:, kt, 2:T + 2], ALU.add).then_inc(mix_ready.sem, 1)

        @block.vector
        def _(dve):
            dve.wait_ge(w_loaded, 7 * 16)
            for s in (stats_ready, mv_ready, var_ready, xn_ready, x_mixed, part_ready, g_ready, gate_ready,
                      unpack_step, unpacked):
                s.ahead(dve)

            def unpack(b, n, words, shift_by, width):
                if n > 0:
                    dve.wait_ge(*unpacked.now(b, n))
                nc.vector.tensor_scalar(shifted[:, 0:width], words, shift_by, None,
                                        ALU.logical_shift_left).then_inc(unpack_step.sem, 1)
                dve.wait_ge(*unpack_step.now(b, 3 * n + 1))
                nc.vector.tensor_scalar(value[:, 0:width], shifted[:, 0:width], 3, 0x0E000E00,
                                        ALU.logical_shift_right, ALU.bitwise_and).then_inc(unpack_step.sem, 1)
                dve.wait_ge(*unpack_step.now(b, 3 * n + 2))
                nc.vector.scalar_tensor_tensor(value[:, 0:width], shifted[:, 0:width], 0x80008000,
                                               value[:, 0:width], ALU.bitwise_and,
                                               ALU.bitwise_or).then_inc(unpack_step.sem, 1)
                dve.wait_ge(*unpack_step.now(b, 3 * n + 3))

            def unpack_gate_up(b, jj):
                if jj == 0:
                    dve.wait_ge(*packed_loaded.now(b, 1))
                unpack(b, jj, gu_words[:, :], shift[:, jj:jj + 1].bitcast(U32), GQ)
                pair = value[:, :].bitcast(F16).rearrange("p (c e) -> p e c", e=2)
                for e in range(2):
                    last = nc.vector.scalar_tensor_tensor(Wgu[:, jj + 2 * e, bass.ds(b * GQ, GQ)], pair[:, e, :],
                                                          2.0 ** 14, gu_scale[:, :], ALU.mult, ALU.mult)
                last.then_inc(unpacked.sem, 1)

            def unpack_down(b, m):
                unpack(b, 2 + m, dn_words[:, m, :], shift[:, 2:3].bitcast(U32), C)
                pair = value[:, 0:C].bitcast(F16).rearrange("p (c e) -> p e c", e=2)
                for e in range(2):
                    rows_e = slice(64 * e, 64 * e + 64)
                    last = nc.vector.scalar_tensor_tensor(Wdn[rows_e, bass.ds(b * DQ + m, 1), :],
                                                          pair[rows_e, e:e + 1, :], 2.0 ** 14,
                                                          dn_scale[rows_e, m:m + 1, :], ALU.mult, ALU.mult)
                last.then_inc(unpacked.sem, 1)

            with dve.Fori(0, B) as b:
                dve.wait_ge(*x_loaded.now(b, 1))
                for t in range(TT):
                    last = nc.vector.bn_stats(stats[:, t, :], x_tok[:, t, :])
                last.then_inc(stats_ready.sem, 1)
                dve.wait_ge(*stats_ready.now(b, 1))
                nc.vector.memset(pause[:, :], 0.0)
                for t in range(TT):
                    last = nc.vector.bn_aggr(mv[:, t, :], stats[:, t, :])
                last.then_inc(mv_ready.sem, 1)
                dve.wait_ge(*mv_ready.now(b, 1))
                nc.vector.tensor_scalar(veps[:, :], mv[:, :, 1], 1e-5, None, ALU.add).then_inc(var_ready.sem, 1)
                dve.wait_ge(*rstd_ready.now(b, 1))
                dve.wait_ge(*ring.product_before(last_reader(5), b))
                for t in range(TT):
                    nc.vector.tensor_scalar(xn[:, t, :], x_tok[:, t, :], mv[:, t, 0:1], rstd[:, t:t + 1],
                                            ALU.subtract, ALU.mult).then_inc(xn_ready.sem, 1)
                dve.wait_ge(*ring.product_before(last_reader(4), b))
                for kt in range(KT):
                    dve.wait_ge(*delta_ready.now(b, kt + 1))
                    nc.vector.scalar_tensor_tensor(mixed[0][:, kt, :], delta[:, kt, :], mu_x[:, kt:kt + 1],
                                                   xT[:, kt, 2:T + 2], ALU.mult, ALU.add).then_inc(x_mixed.sem, 1)
                for n, i in enumerate(ORDER):
                    use = n + 1
                    if use == 1:
                        dve.wait_ge(*ring.product(("xT", KT - 1), b))
                    else:
                        dve.wait_ge(*ring.product(last_reader(use - 2), b))
                    for kt in range(KT):
                        dve.wait_ge(*ring.product(("mix", n, kt), b))
                        nc.vector.scalar_tensor_tensor(mixed[use % 2][:, kt, :], ring.place(("mix", n, kt))[:, :],
                                                       bias[:, i * KT + kt:i * KT + kt + 1], delta[:, kt, :],
                                                       ALU.add, ALU.mult).then_inc(part_ready.sem, 1)
                    if n < 2:
                        unpack_gate_up(b, n)
                    else:
                        unpack_down(b, n - 2)
                for h in range(2):
                    dve.wait_ge(*ring.product(("gate", h), b))
                    for n in range(2):
                        last = nc.vector.tensor_tensor(g[:, 2 * h + n, :],
                                                       ring.place(("gate", h))[:, n * KD:(n + 1) * KD], bg[:, :],
                                                       ALU.add)
                    last.then_inc(g_ready.sem, 1)
                dve.wait_ge(*stored["g"].before(b, 1))
                for h in range(2):
                    dve.wait_ge(*tanhg_ready.now(b, h + 1))
                    nc.vector.scalar_tensor_tensor(flat(gate[:, 2 * h:2 * h + 2, :]), flat(tanhg[:, 2 * h:2 * h + 2, :]),
                                                   1.0, flat(g[:, 2 * h:2 * h + 2, :]), ALU.add,
                                                   ALU.mult).then_inc(gate_ready.sem, 1)

        @block.scalar
        def _(act):
            act.wait_ge(w_loaded, 7 * 16)
            for s in (xT_ready, low_ready, tlow_ready, expw_ready, tanhg_ready, *out_ready.values()):
                s.ahead(act)
            with act.Fori(0, B) as b:
                act.wait_ge(*mix_ready.before(b, N_MIX))
                act.wait_ge(*stored["x"].before(b, 1))
                for job in jobs:
                    kind, n = job[0], job[1]
                    place = ring.place(job)
                    if kind in ("mix", "gate"):
                        continue
                    act.wait_ge(*ring.product(job, b))
                    if kind == "xT":
                        nc.scalar.activation(xT[:, n, 2:T + 2], place[:, :], ACT.Copy).then_inc(xT_ready.sem, 1)
                    elif kind == "low":
                        h = P if n < 2 else LOW
                        nc.scalar.activation(low[0:h, n, :], place[0:h, :], ACT.Tanh).then_inc(low_ready.sem, 1)
                    elif kind == "proj":
                        s, hh = MIX[ORDER[n]], job[2]
                        act.wait_ge(*stored[s].before(b, 1))
                        nc.scalar.activation(out[s][:, hh, :], place[:, :], ACT.Copy).then_inc(out_ready[s].sem, 1)
                    elif kind == "down":
                        s = MIX[ORDER[n]]
                        nc.scalar.activation(tlow[s][:, :], place[0:LOW, :], ACT.Tanh).then_inc(tlow_ready.sem, 1)
                    elif kind == "decay":
                        if n == 1:
                            act.wait_ge(*out_ready["w"].now(b, 1))
                        nc.scalar.activation(expw[:, :], place[:, :], ACT.Exp,
                                             bias=bw[:, n:n + 1]).then_inc(expw_ready.sem, 1)
                        act.wait_ge(*expw_ready.now(b, n + 1))
                        act.wait_ge(*stored["w"].before(b, 1))
                        nc.scalar.activation(out["w"][:, n, :], expw[:, :], ACT.Exp,
                                             scale=-1.0).then_inc(out_ready["w"].sem, 1)
                for h in range(2):
                    act.wait_ge(*g_ready.now(b, h + 1))
                    act.wait_ge(*gate_ready.before(b, h + 1))
                    nc.scalar.activation(flat(tanhg[:, 2 * h:2 * h + 2, :]), flat(g[:, 2 * h:2 * h + 2, :]), ACT.Tanh,
                                         scale=0.5).then_inc(tanhg_ready.sem, 1)

        @block.tensor
        def _(pe):
            pe.wait_ge(w_loaded, 7 * 16)
            ring.done.ahead(pe)
            with pe.Fori(0, B) as b:
                for job in jobs:
                    kind, n = job[0], job[1]
                    place = ring.place(job)
                    pe.wait_ge(*ring.vacated(job, b))
                    if kind == "xT":
                        for t in range(TT):
                            pe.wait_ge(*xn_ready.now(b, t + 1))
                            last = nc.tensor.transpose(place[:, t * P:(t + 1) * P], xn[:, t, n * P:(n + 1) * P],
                                                       ident[:, :])
                    elif kind == "low":
                        h = P if n < 2 else LOW
                        for kt in range(KT):
                            pe.wait_ge(*x_mixed.now(b, kt + 1))
                            last = nc.tensor.matmul(place[0:h, :], Wx1[:, kt, n * P:n * P + h], mixed[0][:, kt, :],
                                                    start=(kt == 0), stop=(kt == KT - 1))
                    elif kind == "mix":
                        i, kt = ORDER[n], job[2]
                        pe.wait_ge(*low_ready.now(b, i // 2 + 1))
                        p = LOW * (i % 2)
                        last = nc.tensor.matmul(place[:, :], Wx2[p:p + LOW, i // 2, kt * P:(kt + 1) * P],
                                                low[p:p + LOW, i // 2, :], start=True, stop=True)
                    elif kind in ("proj", "down"):
                        s = MIX[ORDER[n]]
                        buf = mixed[(n + 1) % 2]
                        if kind == "proj":
                            h, weight = P, Wproj[s][:, :, job[2] * P:(job[2] + 1) * P]
                        else:
                            h, weight = LOW, Wdown[s]
                        for kt in range(KT):
                            pe.wait_ge(*mix_ready.now(b, n * KT + kt + 1))
                            last = nc.tensor.matmul(place[0:h, :], weight[:, kt, :], buf[:, kt, :],
                                                    start=(kt == 0), stop=(kt == KT - 1))
                    elif kind == "decay":
                        pe.wait_ge(*tlow_ready.now(b, 1))
                        last = nc.tensor.matmul(place[:, :], Wb[:, 0, n * P:(n + 1) * P], tlow["w"][:, :],
                                                start=True, stop=True)
                    else:
                        pe.wait_ge(*tlow_ready.now(b, 2))
                        for m in range(2):
                            t = 2 * n + m
                            last = nc.tensor.matmul(place[:, m * KD:(m + 1) * KD], tlow["g"][:, t * P:(t + 1) * P],
                                                    Wb[:, 1, :], start=True, stop=True)
                    last.then_inc(ring.done.sem, 1)


def product3(nc, out, left, right, start, stop):
    nc.tensor.matmul(out, left[1], right[0], start=start, stop=False)
    nc.tensor.matmul(out, left[0], right[1], start=False, stop=False)
    return nc.tensor.matmul(out, left[0], right[0], start=False, stop=stop)


def recurrence_and_gate(nc, w, x, spill, Wgu, Wdn, x1):
    UNITS = HH * DK
    LAG = 2
    A_jobs = ([("vtok", n) for n in range(2)] + [("spread", u) for u in range(UNITS)] + [("bonus", 0)]
              + [("oT", hh) for hh in range(HH)] + [("s", t) for t in range(TT)])
    DOWN = [(0, 1), (2,), (3,)]
    F_jobs = [("gu", j) for j in range(JT)] + [("down", n) for n in range(len(DOWN))]

    order = [("gu", 0), ("vtok", 0), ("vtok", 1)]
    gu = [("gu", j) for j in range(1, JT)]
    for u in range(UNITS):
        if u % 3 == 0 and u > 0:
            order.append(gu.pop(0))
        order.append(("spread", u))
        if u >= LAG:
            order.append(("sum", u - LAG))
    assert not gu
    order += [("sum", u) for u in range(UNITS - LAG, UNITS)]
    order += [("bonus", 0), ("down", 0), ("oT", 0), ("oT", 1), ("down", 1), ("down", 2)]
    order += [("s", t) for t in range(TT)]

    with ExitStack() as ctx:
        def sb(name, shape, dt=F32):
            return ctx.enter_context(nc.sbuf_tensor("r_" + name, shape, dt))

        def twins(name, shape, other, other_shape):
            with nc.sbuf_tensor("r_" + name, shape, F32R) as part:
                pass
            return part, sb(other, other_shape)

        def signal(name, per, unit=1):
            return Signal(ctx, nc, "r_" + name, per, unit)

        spread = sb("spread", [P, DK, P], F32R)
        ident32 = sb("ident32", [P, P])
        ident = sb("ident", [P, P], F32R)
        heads = sb("heads", [P, HPT])
        Wo = sb("Wo", [P, HH, C])
        bonus = sb("bonus", [P, HH])
        lnw = sb("lnw", [P, KD])
        lnb = sb("lnb", [P, KD])
        half = sb("half", [P, NH * TT])
        x_hi = sb("x_hi", [P, KT, T], F32R)
        x_lo, xT = twins("x_lo", [P, KT, T], "xT", [P, KT, T])
        rT = [sb(f"rT{i}", [P, T]) for i in range(HH)]
        kT = [sb(f"kT{i}", [P, T]) for i in range(HH)]
        dT = [sb(f"dT{i}", [P, T]) for i in range(HH)]
        v_hi = sb("v_hi", [P, HH, T], F32R)
        v_lo, vT = twins("v_lo", [P, HH, T], "vT", [P, HH, T])
        v_tok = sb("v_tok", [P, TT, KD])
        kv = [sb(f"kv{i}", [P, T]) for i in range(2)]
        S = [sb(f"S{i}", [P, T + 1]) for i in range(2)]
        rS = [sb(f"rS{i}", [P, T]) for i in range(3)]
        rkb = sb("rkb", [P, HH, T])
        gate = sb("gate", [P, TT, KD])
        vc = sb("vc", [P, TT, KD])
        o = sb("o", [P, TT, KD])
        small = {s: sb(s, [P, TT * NH]) for s in ("osum", "oss", "oveps", "orstd")}
        w_hi, w_lo = [None, None], [None, None]
        w_hi[0], tanh_y = twins("w_hi0", [P, KT, 2, P], "tanh_y", [P, 2, C])
        w_hi[1], oT = twins("w_hi1", [P, KT, 2, P], "oT", [P, HH, T])
        w_lo[0], u1_first = twins("w_lo0", [P, KT, 2, P], "u1_first", [P, 2, C])
        w_lo[1], u1_second = twins("w_lo1", [P, KT, 2, P], "u1_second", [P, 2, C])
        u1 = [pair[:, i, :] for pair in (u1_first, u1_second) for i in range(2)]
        h = sb("h", [P, JT, T])
        spread32 = flat(h[:, 0:DK * P // T, :])
        tanh_gate = [sb(f"tanh_gate{i}", [P, T]) for i in range(2)]
        hg = sb("hg", [P, T])
        ysq = hg
        yss = sb("yss", [P, TT])
        yveps = sb("yveps", [P, TT])
        yr = sb("yr", [P, TT])
        hyr = sb("hyr", [P, TT])
        xs = sb("xs", [P, TT, C])
        banks = [ctx.enter_context(nc.psum_tensor(f"r_ps{i}", [P, 512], F32)) for i in range(8)]

        w_loaded = ctx.enter_context(nc.semaphore("r_w_loaded"))
        spread_loaded = ctx.enter_context(nc.semaphore("r_spread_loaded"))
        const_set = ctx.enter_context(nc.semaphore("r_const_set"))
        rounded = ctx.enter_context(nc.semaphore("r_rounded"))
        xT_loaded = signal("xT_loaded", 1, 16)
        rkd_loaded = [signal(f"rkd_loaded{i}", 1, 48) for i in range(HH)]
        v_loaded = signal("v_loaded", 1, 16)
        g_loaded = signal("g_loaded", 1, 16)
        x_loaded = signal("x_loaded", 1, 16)
        x1_stored = signal("x1_stored", 1, 16)
        x_hi_ready = signal("x_hi_ready", KT)
        x_lo_ready = signal("x_lo_ready", KT)
        w_hi_ready = signal("w_hi_ready", JT)
        w_lo_ready = signal("w_lo_ready", JT)
        v_hi_ready = signal("v_hi_ready", 1)
        v_lo_ready = signal("v_lo_ready", 1)
        vtok_ready = signal("vtok_ready", 2)
        rk_ready = signal("rk_ready", HH)
        rkb_ready = signal("rkb_ready", HH)
        kv_ready = signal("kv_ready", UNITS)
        S_ready = signal("S_ready", UNITS)
        rS_ready = signal("rS_ready", UNITS)
        summed = signal("summed", UNITS)
        tanh_gate_ready = signal("tanh_gate_ready", JT)
        hg_ready = signal("hg_ready", JT)
        h_ready = signal("h_ready", JT)
        vc_ready = signal("vc_ready", 1)
        o_ready = signal("o_ready", TT)
        osum_ready = signal("osum_ready", 1)
        centred = signal("centred", 1)
        squared = signal("squared", 1)
        oss_ready = signal("oss_ready", 1)
        oveps_ready = signal("oveps_ready", 1)
        orstd_ready = signal("orstd_ready", 1)
        o_step = signal("o_step", 3)
        gated_ready = signal("gated_ready", 1)
        oT_ready = signal("oT_ready", HH)
        yss_ready = signal("yss_ready", TT)
        yveps_ready = signal("yveps_ready", len(DOWN))
        yr_ready = signal("yr_ready", len(DOWN))
        hyr_ready = signal("hyr_ready", len(DOWN))
        tanh_y_ready = signal("tanh_y_ready", TT)
        u1_ready = signal("u1_ready", TT)
        sg_ready = signal("sg_ready", TT)
        x1_ready = signal("x1_ready", TT)

        A = Ring(ctx, nc, "r_A", banks[0:2], A_jobs,
                 {**{("vtok", n): (vtok_ready, n + 1) for n in range(2)},
                  **{("spread", u): (kv_ready, u + 1) for u in range(UNITS)},
                  ("bonus", 0): (vc_ready, 1),
                  **{("oT", hh): (oT_ready, hh + 1) for hh in range(HH)},
                  **{("s", t): (sg_ready, t + 1) for t in range(TT)}})
        O = banks[2:4]
        F = Ring(ctx, nc, "r_F", [banks[4:6], banks[6:8]], F_jobs,
                 {**{("gu", j): (h_ready, j + 1) for j in range(JT)},
                  **{("down", n): (u1_ready, DOWN[n][-1] + 1) for n in range(len(DOWN))}})

        def tile_weights(j):
            return Wgu[:, :, :].rearrange("p k (s n) -> p k s n", s=2)[:, :, :, j * P:(j + 1) * P]

        block = ctx.enter_context(nc.Block())

        @block.sync
        def _(sp):
            for dst, name in ((ident32, "ident"), (heads, "heads"), (bonus, "bonus"), (lnw, "lnw"), (lnb, "lnb")):
                sp.dma_start(dst[:, :], w[name]).then_inc(w_loaded, 16)
            sp.dma_start(flat(Wo[:, :, :]), w["Wo0"]).then_inc(w_loaded, 16)
            sp.dma_start(spread32, w["spread"]).then_inc(spread_loaded, 16)
            for s in [xT_loaded, *rkd_loaded, v_loaded, g_loaded, x_loaded, x1_stored]:
                s.ahead(sp)

            def load(b):
                sp.wait_ge(*F.product_before(("gu", JT - 1), b))
                sp.dma_start(flat(xT[:, :, :]), slab(spill["x"], b)).then_inc(xT_loaded.sem, 16)
                sp.wait_ge(*A.product_before(("spread", UNITS - 1), b))
                sp.dma_start(flat(vT[:, :, :]), slab(spill["v"], b)).then_inc(v_loaded.sem, 16)
                for hh in range(HH):
                    sp.wait_ge(*rS_ready.before(b, DK * (hh + 1)))
                    for dst, s in ((rT, "r"), (kT, "k"), (dT, "w")):
                        sp.dma_start(dst[hh][:, :], slab(spill[s], b)[:, hh * T:(hh + 1) * T]).then_inc(
                            rkd_loaded[hh].sem, 16)
                sp.wait_ge(*gated_ready.before(b, 1))
                sp.dma_start(flat(gate[:, :, :]), slab(spill["g"], b)).then_inc(g_loaded.sem, 16)

            load(0)
            sp.dma_start(xs[:, :, :], rows(x, 0)).then_inc(x_loaded.sem, 16)
            with sp.Fori(1, B) as b:
                load(b)
                sp.wait_ge(*x1_ready.before(b, TT))
                sp.dma_start(rows(x1, b - 1), xs[:, :, :]).then_inc(x1_stored.sem, 16)
                sp.wait_ge(*x1_stored.before(b, 1))
                sp.dma_start(xs[:, :, :], rows(x, b)).then_inc(x_loaded.sem, 16)
            sp.wait_ge(*x1_ready.now(B - 1, TT))
            sp.dma_start(rows(x1, B - 1), xs[:, :, :]).then_inc(x1_stored.sem, 16)
            sp.wait_ge(x1_stored.sem, 16 * (B + 1))

        @block.gpsimd
        def _(pool):
            nc.gpsimd.memset(half[:, :], -0.5).then_inc(const_set, 1)
            for i in range(2):
                nc.gpsimd.memset(S[i][:, 0:1], 0.0).then_inc(const_set, 1)
            pool.wait_ge(const_set, 3)
            for s in (rS_ready, orstd_ready, yr_ready, x1_ready):
                s.ahead(pool)
            with pool.Fori(0, B) as b:
                for u in range(UNITS):
                    pool.wait_ge(*S_ready.now(b, u + 1))
                    if u >= 3:
                        pool.wait_ge(*summed.now(b, u - 2))
                    else:
                        pool.wait_ge(*summed.before(b, UNITS - (UNITS - 1 - u) % 3))
                    nc.gpsimd.tensor_tensor(rS[u % 3][:, :], S[u % 2][:, 0:T], rT[u // DK][:, :],
                                            ALU.mult).then_inc(rS_ready.sem, 1)
                pool.wait_ge(*oveps_ready.now(b, 1))
                nc.gpsimd.tensor_tensor(small["orstd"][:, :], small["oveps"][:, :], half[:, :],
                                        ALU.pow).then_inc(orstd_ready.sem, 1)
                for n, ts in enumerate(DOWN):
                    pool.wait_ge(*yveps_ready.now(b, n + 1))
                    cols = slice(ts[0], ts[-1] + 1)
                    nc.gpsimd.tensor_tensor(yr[:, cols], yveps[:, cols], half[:, cols],
                                            ALU.pow).then_inc(yr_ready.sem, 1)
                pool.wait_ge(*x_loaded.now(b, 1))
                for t in range(TT):
                    pool.wait_ge(*sg_ready.now(b, t + 1))
                    nc.gpsimd.tensor_tensor(xs[:, t, :], xs[:, t, :], u1[t], ALU.add).then_inc(x1_ready.sem, 1)

        @block.vector
        def _(dve):
            dve.wait_ge(w_loaded, 6 * 16)
            dve.wait_ge(const_set, 3)
            dve.wait_ge(rounded, 2)
            for s in (x_lo_ready, w_lo_ready, v_lo_ready, rk_ready, rkb_ready, kv_ready, S_ready, hg_ready, h_ready, vc_ready, o_ready,
                      osum_ready, centred, oss_ready, oveps_ready, o_step, gated_ready, yveps_ready, hyr_ready,
                      u1_ready, sg_ready):
                s.ahead(dve)
            with dve.Fori(0, B) as b:
                def split_weights(j):
                    dve.wait_ge(*w_hi_ready.now(b, j + 1))
                    if j >= 2:
                        dve.wait_ge(*F.product(("gu", j - 2), b))
                    else:
                        dve.wait_ge(*x1_ready.before(b, 2 * j + 2))
                    nc.vector.tensor_tensor(w_lo[j % 2][:, :, :, :], tile_weights(j),
                                            w_hi[j % 2][:, :, :, :].bitcast(F32),
                                            ALU.subtract).then_inc(w_lo_ready.sem, 1)

                for kt in range(KT):
                    dve.wait_ge(*x_hi_ready.now(b, kt + 1))
                    nc.vector.tensor_tensor(x_lo[:, kt, :], xT[:, kt, :],
                                            x_hi[:, kt, :].bitcast(F32), ALU.subtract).then_inc(x_lo_ready.sem, 1)
                split_weights(0)
                dve.wait_ge(*v_hi_ready.now(b, 1))
                nc.vector.tensor_tensor(flat(v_lo[:, :, :]), flat(vT[:, :, :]),
                                        flat(v_hi[:, :, :]).bitcast(F32), ALU.subtract).then_inc(v_lo_ready.sem, 1)
                split_weights(1)
                dve.wait_ge(*F.product_before(("down", len(DOWN) - 1), b))

                def hidden(j):
                    dve.wait_ge(*tanh_gate_ready.now(b, j + 1))
                    gate_ps, up_ps = F.place(("gu", j))
                    dve.wait_ge(*(h_ready.now(b, j) if j > 0 else h_ready.before(b, JT)))
                    nc.vector.scalar_tensor_tensor(hg[:, :], tanh_gate[j % 2][:, :], 1.0, gate_ps[:, :], ALU.add,
                                                   ALU.mult).then_inc(hg_ready.sem, 1)
                    dve.wait_ge(*hg_ready.now(b, j + 1))
                    nc.vector.scalar_tensor_tensor(h[:, j, :], hg[:, :], 0.5, up_ps[:, :], ALU.mult,
                                                   ALU.mult).then_inc(h_ready.sem, 1)

                for u in range(UNITS):
                    hh = u // DK
                    if u % DK == 0:
                        dve.wait_ge(*rkd_loaded[hh].now(b, 1))
                        nc.vector.scalar_tensor_tensor(rkb[:, hh, :], rT[hh][:, :], bonus[:, hh:hh + 1], kT[hh][:, :],
                                                       ALU.mult, ALU.mult).then_inc(rkb_ready.sem, 1)
                    dve.wait_ge(*A.product(("spread", u), b))
                    dve.wait_ge(*(S_ready.now(b, u - 1) if u >= 2 else S_ready.before(b, UNITS - 1 + u)))
                    nc.vector.tensor_tensor(kv[u % 2][:, :], kT[hh][:, :], A.place(("spread", u))[:, :],
                                            ALU.mult).then_inc(kv_ready.sem, 1)
                    dve.wait_ge(*kv_ready.now(b, u + 1))
                    dve.wait_ge(*(rS_ready.now(b, u - 1) if u >= 2 else rS_ready.before(b, UNITS - 1 + u)))
                    nc.vector.tensor_tensor_scan(S[u % 2][:, 1:T + 1], dT[hh][:, :], kv[u % 2][:, :], 0.0, ALU.mult,
                                                 ALU.add).then_inc(S_ready.sem, 1)
                    if u % 3 == 2:
                        hidden(u // 3)
                        if u // 3 + 2 < JT:
                            split_weights(u // 3 + 2)
                hidden(JT - 1)

                dve.wait_ge(*A.product(("bonus", 0), b))
                dve.wait_ge(*vtok_ready.now(b, 2))
                by_head = "p t (h v) -> p (t h) v"
                wide = [P, TT * NH, DK]
                nc.vector.tensor_tensor(vc[:, :, :].rearrange(by_head, v=DK), v_tok[:, :, :].rearrange(by_head, v=DK),
                                        A.place(("bonus", 0))[:, 0:TT * NH].unsqueeze(2).broadcast_to(wide),
                                        ALU.mult).then_inc(vc_ready.sem, 1)
                dve.wait_ge(*vc_ready.now(b, 1))
                dve.wait_ge(*summed.now(b, UNITS))
                for t in range(TT):
                    ps = O[t // 2][:, (t % 2) * KD:(t % 2 + 1) * KD]
                    nc.vector.tensor_tensor(o[:, t, :].rearrange("p (g h v) -> p g h v", g=HH, v=DK),
                                            vc[:, t, :].rearrange("p (g h v) -> p g h v", g=HH, v=DK),
                                            ps.rearrange("p (g v h) -> p g h v", g=HH, v=DK),
                                            ALU.add).then_inc(o_ready.sem, 1)
                dve.wait_ge(*o_ready.now(b, TT))
                o3 = o[:, :, :].rearrange(by_head, v=DK)
                nc.vector.tensor_reduce(small["osum"][:, :], o3, AX.X, ALU.add).then_inc(osum_ready.sem, 1)
                dve.wait_ge(*osum_ready.now(b, 1))
                nc.vector.scalar_tensor_tensor(o3, small["osum"][:, :].unsqueeze(2).broadcast_to(wide), -1.0 / DK, o3,
                                               ALU.mult, ALU.add).then_inc(centred.sem, 1)
                dve.wait_ge(*squared.now(b, 1))
                nc.vector.tensor_reduce(small["oss"][:, :], vc[:, :, :].rearrange(by_head, v=DK), AX.X,
                                        ALU.add).then_inc(oss_ready.sem, 1)
                dve.wait_ge(*oss_ready.now(b, 1))
                nc.vector.tensor_scalar(small["oveps"][:, :], small["oss"][:, :], 1.0 / DK, 1e-5, ALU.mult,
                                        ALU.add).then_inc(oveps_ready.sem, 1)
                dve.wait_ge(*orstd_ready.now(b, 1))
                nc.vector.tensor_tensor(o3, o3, small["orstd"][:, :].unsqueeze(2).broadcast_to(wide),
                                        ALU.mult).then_inc(o_step.sem, 1)
                dve.wait_ge(*o_step.now(b, 1))
                nc.vector.tensor_tensor(o[:, :, :], o[:, :, :], lnw[:, :].unsqueeze(1).broadcast_to([P, TT, KD]),
                                        ALU.mult).then_inc(o_step.sem, 1)
                dve.wait_ge(*o_step.now(b, 2))
                nc.vector.tensor_tensor(o[:, :, :], o[:, :, :], lnb[:, :].unsqueeze(1).broadcast_to([P, TT, KD]),
                                        ALU.add).then_inc(o_step.sem, 1)
                dve.wait_ge(*o_step.now(b, 3))
                dve.wait_ge(*g_loaded.now(b, 1))
                nc.vector.scalar_tensor_tensor(flat(o[:, :, :]), flat(gate[:, :, :]), 0.5, flat(o[:, :, :]), ALU.mult,
                                               ALU.mult).then_inc(gated_ready.sem, 1)
                for n, ts in enumerate(DOWN):
                    cols = slice(ts[0], ts[-1] + 1)
                    dve.wait_ge(*yss_ready.now(b, ts[-1] + 1))
                    nc.vector.tensor_scalar(yveps[:, cols], yss[:, cols], 1.0 / C, 1e-6, ALU.mult,
                                            ALU.add).then_inc(yveps_ready.sem, 1)
                    dve.wait_ge(*yr_ready.now(b, n + 1))
                    nc.vector.tensor_scalar(hyr[:, cols], yr[:, cols], 0.5, None, ALU.mult).then_inc(hyr_ready.sem, 1)
                    for i, t in enumerate(ts):
                        dve.wait_ge(*tanh_y_ready.now(b, t + 1))
                        dve.wait_ge(*x1_ready.before(b, t + 1))
                        nc.vector.scalar_tensor_tensor(u1[t], tanh_y[:, t % 2, :], 1.0,
                                                       F.place(("down", n))[i][:, :], ALU.add,
                                                       ALU.mult).then_inc(u1_ready.sem, 1)
                for t in range(TT):
                    dve.wait_ge(*A.product(("s", t), b))
                    dve.wait_ge(*u1_ready.now(b, t + 1))
                    nc.vector.scalar_tensor_tensor(u1[t], A.place(("s", t))[:, :], hyr[:, t:t + 1], u1[t],
                                                   ALU.mult, ALU.mult).then_inc(sg_ready.sem, 1)

        @block.scalar
        def _(act):
            act.wait_ge(w_loaded, 6 * 16)
            act.wait_ge(spread_loaded, 16)
            nc.scalar.activation(flat(spread[:, :, :]), spread32, ACT.Copy).then_inc(rounded, 1)
            nc.scalar.activation(ident[:, :], ident32[:, :], ACT.Copy).then_inc(rounded, 1)
            for s in (x_hi_ready, w_hi_ready, v_hi_ready, vtok_ready, tanh_gate_ready, squared, oT_ready, yss_ready, tanh_y_ready):
                s.ahead(act)
            with act.Fori(0, B) as b:
                def round_weights(j):
                    if j >= 2:
                        act.wait_ge(*F.product(("gu", j - 2), b))
                    elif j == 0:
                        act.wait_ge(*u1_ready.before(b, TT))
                    else:
                        act.wait_ge(*A.product_before(("s", TT - 1), b))
                    nc.scalar.activation(w_hi[j % 2][:, :, :, :], tile_weights(j), ACT.Copy).then_inc(w_hi_ready.sem, 1)

                act.wait_ge(*xT_loaded.now(b, 1))
                for kt in range(KT):
                    nc.scalar.activation(x_hi[:, kt, :], xT[:, kt, :],
                                         ACT.Copy).then_inc(x_hi_ready.sem, 1)
                round_weights(0)
                act.wait_ge(*v_loaded.now(b, 1))
                nc.scalar.activation(flat(v_hi[:, :, :]), flat(vT[:, :, :]),
                                     ACT.Copy).then_inc(v_hi_ready.sem, 1)
                round_weights(1)
                act.wait_ge(*vc_ready.before(b, 1))
                for n in range(2):
                    act.wait_ge(*A.product(("vtok", n), b))
                    nc.scalar.activation(flat(v_tok[:, 2 * n:2 * n + 2, :]), A.place(("vtok", n))[:, :],
                                         ACT.Copy).then_inc(vtok_ready.sem, 1)
                for j in range(JT):
                    act.wait_ge(*F.product(("gu", j), b))
                    act.wait_ge(*(h_ready.now(b, j - 1) if j >= 2 else h_ready.before(b, JT)))
                    nc.scalar.activation(tanh_gate[j % 2][:, :], F.place(("gu", j))[0][:, :], ACT.Tanh,
                                         scale=0.5).then_inc(tanh_gate_ready.sem, 1)
                    if j + 2 < JT:
                        round_weights(j + 2)
                act.wait_ge(*centred.now(b, 1))
                nc.scalar.activation(flat(vc[:, :, :]), flat(o[:, :, :]), ACT.Square).then_inc(squared.sem, 1)

                def squares(n):
                    act.wait_ge(*F.product(("down", n), b))
                    for i, t in enumerate(DOWN[n]):
                        act.wait_ge(*(yss_ready.now(b, t) if t > 0 else yss_ready.before(b, TT)))
                        nc.scalar.activation(ysq[:, :], F.place(("down", n))[i][:, :], ACT.Square,
                                             accum_out=yss[:, t:t + 1]).then_inc(yss_ready.sem, 1)

                def tanhs(n):
                    act.wait_ge(*hyr_ready.now(b, n + 1))
                    for i, t in enumerate(DOWN[n]):
                        act.wait_ge(*(u1_ready.now(b, t - 1) if t >= 2 else u1_ready.before(b, t + 3)))
                        nc.scalar.activation(tanh_y[:, t % 2, :], F.place(("down", n))[i][:, :], ACT.Tanh,
                                             scale=hyr[:, t:t + 1]).then_inc(tanh_y_ready.sem, 1)

                squares(0)
                for hh in range(HH):
                    act.wait_ge(*A.product(("oT", hh), b))
                    nc.scalar.activation(oT[:, hh, :], A.place(("oT", hh))[:, :], ACT.Copy).then_inc(oT_ready.sem, 1)
                tanhs(0)
                for n in (1, 2):
                    squares(n)
                    tanhs(n)

        @block.tensor
        def _(pe):
            pe.wait_ge(w_loaded, 6 * 16)
            pe.wait_ge(rounded, 2)
            for s in (A.done, F.done, summed):
                s.ahead(pe)
            with pe.Fori(0, B) as b:
                for job in order:
                    kind, n = job
                    if kind == "sum":
                        u, hh = n, n // DK
                        pe.wait_ge(*rS_ready.now(b, u + 1))
                        if u == 0:
                            pe.wait_ge(*o_ready.before(b, TT))
                        for t in range(TT):
                            at = (t % 2) * KD + hh * P + (u % DK) * HPT
                            last = nc.tensor.matmul(O[t // 2][:, at:at + HPT], rS[u % 3][:, t * P:(t + 1) * P],
                                                    heads[:, :], start=True, stop=True)
                        last.then_inc(summed.sem, 1)
                        continue
                    ring = F if kind in ("gu", "down") else A
                    place = ring.place(job)
                    pe.wait_ge(*ring.vacated(job, b))
                    if kind == "vtok":
                        pe.wait_ge(*v_lo_ready.now(b, 1))
                        for m in range(2):
                            t = 2 * n + m
                            for hh in range(HH):
                                at = m * KD + hh * P
                                for i, part in enumerate((v_hi, v_lo)):
                                    last = nc.tensor.matmul(place[:, at:at + P], part[:, hh, t * P:(t + 1) * P],
                                                            ident[:, :], start=(i == 0), stop=(i == 1))
                    elif kind == "spread":
                        for i, part in enumerate((v_hi, v_lo)):
                            last = nc.tensor.matmul(place[:, :], spread[:, n % DK, :], part[:, n // DK, :],
                                                    start=(i == 0), stop=(i == 1))
                    elif kind == "gu":
                        pe.wait_ge(*w_lo_ready.now(b, n + 1))
                        for side in range(2):
                            for kt in range(KT):
                                if n == 0 and side == 0:
                                    pe.wait_ge(*x_lo_ready.now(b, kt + 1))
                                last = product3(nc, place[side][:, :],
                                                (w_hi[n % 2][:, kt, side, :], w_lo[n % 2][:, kt, side, :]),
                                                (x_hi[:, kt, :], x_lo[:, kt, :]), kt == 0, kt == KT - 1)
                    elif kind == "down":
                        for i, t in enumerate(DOWN[n]):
                            for j in range(JT):
                                if n == 0 and i == 0:
                                    pe.wait_ge(*h_ready.now(b, j + 1))
                                last = nc.tensor.matmul(place[i][:, :], h[:, j, t * P:(t + 1) * P], Wdn[:, j, :],
                                                        start=(j == 0), stop=(j == JT - 1))
                    elif kind == "bonus":
                        pe.wait_ge(*rkb_ready.now(b, HH))
                        for t in range(TT):
                            for hh in range(HH):
                                at = t * NH + hh * HPT
                                last = nc.tensor.matmul(place[:, at:at + HPT], rkb[:, hh, t * P:(t + 1) * P],
                                                        heads[:, :], start=True, stop=True)
                    elif kind == "oT":
                        pe.wait_ge(*gated_ready.now(b, 1))
                        for t in range(TT):
                            last = nc.tensor.transpose(place[:, t * P:(t + 1) * P], o[:, t, n * P:(n + 1) * P],
                                                       ident32[:, :])
                    else:
                        if n == 0:
                            pe.wait_ge(*oT_ready.now(b, HH))
                        for hh in range(HH):
                            last = nc.tensor.matmul(place[:, :], oT[:, hh, n * P:(n + 1) * P], Wo[:, hh, :],
                                                    start=(hh == 0), stop=(hh == HH - 1))
                    last.then_inc(ring.done.sem, 1)


def linear_attention(nc, w, x1, spill):
    AHEAD = 2
    LN_HEAD = QH - 2
    jobs = ([("xT", kt) for kt in range(KT)] + [(s, t) for s in "kv" for t in range(TT)]
            + [("kvT", 0), ("ksum", 0)])
    for h in range(QH + 1):
        if h < QH:
            jobs += [("q", h), ("M", h)]
        if h > 0:
            jobs += [("norm", h - 1)] + [("head", h - 1, t) for t in range(TT)]

    with ExitStack() as ctx:
        def sb(name, shape, dt=F32):
            return ctx.enter_context(nc.sbuf_tensor("l_" + name, shape, dt))

        def signal(name, per, unit=1):
            return Signal(ctx, nc, "l_" + name, per, unit)

        Wkv = {s: sb("W" + s, [P, KT, KVH * D]) for s in "kv"}
        Wq = [sb(f"Wq{i}", [P, KT, QH * D], F32R) for i in range(2)]
        Wo = sb("Wo", [P, QH, C])
        bkv = {s: sb("b" + s, [P, KVH * D]) for s in "kv"}
        bq = sb("bq", [P, QH])
        ident = sb("ident", [P, P])
        ones = sb("ones", [P, 1])
        half = sb("half", [P, TT])
        x_tok = sb("x_tok", [P, TT, C])
        stats = sb("stats", [P, TT, 6])
        mv = sb("mv", [P, TT, 2])
        veps = sb("veps", [P, TT])
        pause = sb("pause", [P, 1])
        rstd = sb("rstd", [P, TT])
        xT = sb("xT", [P, KT, T])
        x_part = [sb(f"x_part{i}", [P, KT, T], F32R) for i in range(2)]
        sk = sb("sk", [P, TT, KVH * D])
        v = sb("v", [P, TT, KVH * D])
        kvT = sb("kvT", [P, KVH, D])
        ksum = sb("ksum", [P, KVH])
        expq = [sb(f"expq{i}", [P, T]) for i in range(2)]
        reluq = [sb(f"reluq{i}", [P, T]) for i in range(2)]
        biased, expk = reluq, expq
        sq = [sb(f"sq{i}", [P, T]) for i in range(2)]
        sq_part = [[sb(f"sq_part{i}{j}", [P, T], F32R) for i in range(2)] for j in range(2)]
        M_part = [[sb(f"M_part{i}{j}", [P, C], F32R) for i in range(2)] for j in range(2)]
        norm = [sb(f"norm{i}", [P, TT]) for i in range(2)]
        inv = [sb(f"inv{i}", [P, TT]) for i in range(2)]
        acc = sb("acc", [P, TT, C])
        banks = [ctx.enter_context(nc.psum_tensor(f"l_ps{i}", [P, 512], F32)) for i in range(8)]

        w_loaded = ctx.enter_context(nc.semaphore("l_w_loaded"))
        wkv_loaded = ctx.enter_context(nc.semaphore("l_wkv_loaded"))
        wo_loaded = ctx.enter_context(nc.semaphore("l_wo_loaded"))
        wq_loaded = [ctx.enter_context(nc.semaphore(f"l_wq_loaded{i}")) for i in range(TT)]
        wq_hi_ready = ctx.enter_context(nc.semaphore("l_wq_hi_ready"))
        wq_lo_ready = ctx.enter_context(nc.semaphore("l_wq_lo_ready"))
        const_set = ctx.enter_context(nc.semaphore("l_const_set"))
        x_loaded = signal("x_loaded", 1, 16)
        stats_ready = signal("stats_ready", 1)
        mv_ready = signal("mv_ready", 1)
        var_ready = signal("var_ready", 1)
        rstd_ready = signal("rstd_ready", 1)
        xn_ready = signal("xn_ready", TT)
        xT_ready = signal("xT_ready", KT)
        biased_ready = signal("biased_ready", TT)
        expk_ready = signal("expk_ready", TT)
        mink_ready = signal("mink_ready", TT)
        sk_ready = signal("sk_ready", TT)
        v_ready = signal("v_ready", TT)
        kvT_ready = signal("kvT_ready", 1)
        ksum_ready = signal("ksum_ready", 1)
        expq_ready = signal("expq_ready", QH)
        reluq_ready = signal("reluq_ready", QH)
        minq_ready = signal("minq_ready", QH)
        sq_ready = signal("sq_ready", QH)
        M_hi_ready = signal("M_hi_ready", QH)
        M_lo_ready = signal("M_lo_ready", QH)
        x_hi_ready = signal("x_hi_ready", KT)
        x_lo_ready = signal("x_lo_ready", KT)
        sq_hi_ready = signal("sq_hi_ready", QH)
        sq_lo_ready = signal("sq_lo_ready", QH)
        norm_ready = signal("norm_ready", QH)
        inv_ready = signal("inv_ready", QH)
        acc_ready = signal("acc_ready", QH * TT)
        xT_stored = signal("xT_stored", 1, 16)
        s_stored = signal("s_stored", 1, 16)

        reader = {("kvT", 0): (kvT_ready, 1), ("ksum", 0): (ksum_ready, 1)}
        for kt in range(KT):
            reader["xT", kt] = (xT_ready, kt + 1)
        for t in range(TT):
            reader["k", t] = (biased_ready, t + 1)
            reader["v", t] = (v_ready, t + 1)
        for h in range(QH):
            reader["q", h] = (minq_ready, h + 1)
            reader["M", h] = (M_lo_ready, h + 1)
            reader["norm", h] = (norm_ready, h + 1)
            for t in range(TT):
                reader["head", h, t] = (acc_ready, h * TT + t + 1)
        ring = Ring(ctx, nc, "l", banks, jobs, reader)

        block = ctx.enter_context(nc.Block())

        @block.sync
        def _(sp):
            for dst, name in ((ident, "ident"), (bkv["k"], "bk"), (bkv["v"], "bv"), (bq, "bq")):
                sp.dma_start(dst[:, :], w[name]).then_inc(w_loaded, 16)
            for s in [x_loaded, xT_stored, s_stored]:
                s.ahead(sp)

            def load_x(b):
                if not isinstance(b, int) or b > 0:
                    sp.wait_ge(*ring.product(("xT", KT - 1), b - 1))
                sp.dma_start(x_tok[:, :, :], rows(x1, b)).then_inc(x_loaded.sem, 16)

            def store_xT(b):
                sp.wait_ge(*xT_ready.now(b, KT))
                sp.dma_start(slab(spill["x2"], b), flat(xT[:, :, :])).then_inc(xT_stored.sem, 16)

            def store_s(b):
                sp.wait_ge(*acc_ready.now(b, QH * TT))
                sp.dma_start(slab(spill["s"], b), flat(acc[:, :, :])).then_inc(s_stored.sem, 16)

            load_x(0)
            for s in "kv":
                sp.dma_start(flat(Wkv[s][:, :, :]), w["W" + s + "1"]).then_inc(wkv_loaded, 16)
            sp.wait_ge(*ring.product(("xT", KT - 1), 0))
            for h in range(QH):
                if h >= TT:
                    sp.wait_ge(wq_lo_ready, h - TT + 1)
                sp.dma_start(x_tok[:, h % TT, :].rearrange("p (k c) -> p k c", k=KT),
                             w["Wq1"].rearrange("p (k c) -> p k c", k=KT)[:, :, h * D:(h + 1) * D]).then_inc(
                                 wq_loaded[h % TT], 16)
                if h == 3:
                    sp.dma_start(flat(Wo[:, :, :]), w["Wo1"]).then_inc(wo_loaded, 16)
                if h == TT:
                    store_xT(0)
            sp.wait_ge(wq_lo_ready, QH)
            load_x(1)
            store_s(0)
            with sp.Fori(1, B - 1) as b:
                store_xT(b)
                load_x(b + 1)
                store_s(b)
            store_xT(B - 1)
            store_s(B - 1)
            sp.wait_ge(xT_stored.sem, 16 * (B + 1))
            sp.wait_ge(s_stored.sem, 16 * (B + 1))

        @block.gpsimd
        def _(pool):
            nc.gpsimd.memset(half[:, :], -0.5).then_inc(const_set, 1)
            nc.gpsimd.memset(ones[:, :], 1.0).then_inc(const_set, 1)
            pool.wait_ge(const_set, 2)
            rstd_ready.ahead(pool)
            sq_ready.ahead(pool)

            def rsqrt(b):
                pool.wait_ge(*var_ready.now(b, 1))
                nc.gpsimd.tensor_tensor(rstd[:, :], veps[:, :], half[:, :], ALU.pow).then_inc(rstd_ready.sem, 1)

            def low(h):
                cols = slice(h * D, (h + 1) * D)
                pool.wait_ge(wq_hi_ready, h + 1)
                nc.gpsimd.tensor_tensor(Wq[1][:, :, cols], x_tok[:, h % TT, :].rearrange("p (k c) -> p k c", k=KT),
                                        Wq[0][:, :, cols].bitcast(F32), ALU.subtract).then_inc(wq_lo_ready, 1)

            def sequence(b, first, last):
                for h in range(QH):
                    if first and h + AHEAD < QH:
                        low(h + AHEAD)
                    if h == LN_HEAD and not last:
                        rsqrt(b + 1)
                    pool.wait_ge(*expq_ready.now(b, h + 1))
                    pool.wait_ge(*(sq_lo_ready.now(b, h - 1) if h >= 2 else sq_lo_ready.before(b, QH - 1 + h)))
                    pool.wait_ge(*(ring.product(("norm", h - 2), b) if h >= 2 else
                                   ring.product_before(("norm", QH - 2 + h), b)))
                    nc.gpsimd.tensor_tensor(sq[h % 2][:, :], expq[h % 2][:, :], reluq[h % 2][:, :],
                                            ALU.add).then_inc(sq_ready.sem, 1)

            rsqrt(0)
            for h in range(AHEAD):
                low(h)
            sequence(0, True, False)
            with pool.Fori(1, B - 1) as b:
                sequence(b, False, False)
            sequence(B - 1, False, True)

        @block.vector
        def _(dve):
            dve.wait_ge(w_loaded, 4 * 16)
            for s in (stats_ready, mv_ready, var_ready, xn_ready, biased_ready, mink_ready, sk_ready, v_ready,
                      minq_ready, norm_ready, inv_ready, acc_ready, M_lo_ready, x_hi_ready, x_lo_ready, sq_hi_ready,
                      sq_lo_ready):
                s.ahead(dve)

            def layer_norm(b):
                dve.wait_ge(*x_loaded.now(b, 1))
                for t in range(TT):
                    last = nc.vector.bn_stats(stats[:, t, :], x_tok[:, t, :])
                last.then_inc(stats_ready.sem, 1)
                dve.wait_ge(*stats_ready.now(b, 1))
                nc.vector.memset(pause[:, :], 0.0)
                for t in range(TT):
                    last = nc.vector.bn_aggr(mv[:, t, :], stats[:, t, :])
                last.then_inc(mv_ready.sem, 1)
                dve.wait_ge(*mv_ready.now(b, 1))
                nc.vector.tensor_scalar(veps[:, :], mv[:, :, 1], 1e-5, None, ALU.add).then_inc(var_ready.sem, 1)
                dve.wait_ge(*rstd_ready.now(b, 1))
                for t in range(TT):
                    nc.vector.tensor_scalar(x_tok[:, t, :], x_tok[:, t, :], mv[:, t, 0:1], rstd[:, t:t + 1],
                                            ALU.subtract, ALU.mult).then_inc(xn_ready.sem, 1)

            def sequence(b, last_one):
                for t in range(TT):
                    dve.wait_ge(*ring.product(("k", t), b))
                    if t < 2:
                        dve.wait_ge(*sq_ready.before(b, QH - 1 + t))
                    nc.vector.tensor_tensor(biased[t % 2][:, :], ring.place(("k", t))[:, :], bkv["k"][:, :],
                                            ALU.add).then_inc(biased_ready.sem, 1)
                    dve.wait_ge(*biased_ready.now(b, t + 1))
                    nc.vector.tensor_scalar(expk[t % 2][:, :], biased[t % 2][:, :], 0.0, None,
                                            ALU.min).then_inc(mink_ready.sem, 1)
                    dve.wait_ge(*expk_ready.now(b, t + 1))
                    nc.vector.scalar_tensor_tensor(sk[:, t, :], biased[t % 2][:, :], 0.0, expk[t % 2][:, :], ALU.max,
                                                   ALU.add).then_inc(sk_ready.sem, 1)
                for t in range(TT):
                    dve.wait_ge(*ring.product(("v", t), b))
                    nc.vector.tensor_tensor(v[:, t, :], ring.place(("v", t))[:, :], bkv["v"][:, :],
                                            ALU.add).then_inc(v_ready.sem, 1)
                dve.wait_ge(*ring.product_before(("q", QH - 1), b))
                for kt in range(KT):
                    dve.wait_ge(*xT_ready.now(b, kt + 1))
                    nc.vector.tensor_copy(x_part[0][:, kt, :], xT[:, kt, :]).then_inc(x_hi_ready.sem, 1)
                    dve.wait_ge(*x_hi_ready.now(b, kt + 1))
                    nc.vector.tensor_tensor(x_part[1][:, kt, :], xT[:, kt, :], x_part[0][:, kt, :].bitcast(F32),
                                            ALU.subtract).then_inc(x_lo_ready.sem, 1)
                for h in range(QH + 1):
                    if h < QH:
                        dve.wait_ge(*reluq_ready.now(b, h + 1))
                        dve.wait_ge(*(sq_ready.now(b, h - 1) if h >= 2 else sq_ready.before(b, QH - 1 + h)))
                        nc.vector.tensor_scalar(expq[h % 2][:, :], ring.place(("q", h))[:, :], bq[:, h:h + 1], 0.0,
                                                ALU.add, ALU.min).then_inc(minq_ready.sem, 1)
                    if h == LN_HEAD and not last_one:
                        layer_norm(b + 1)
                    if h > 0:
                        g = h - 1
                        dve.wait_ge(*ring.product(("norm", g), b))
                        dve.wait_ge(*(inv_ready.now(b, g - 1) if g >= 2 else inv_ready.before(b, QH - 1 + g)))
                        nc.vector.tensor_scalar(norm[g % 2][:, :], ring.place(("norm", g))[:, 0:TT], 1e-6, None,
                                                ALU.add).then_inc(norm_ready.sem, 1)
                        dve.wait_ge(*norm_ready.now(b, g + 1))
                        dve.wait_ge(*(acc_ready.now(b, (g - 1) * TT) if g >= 2 else
                                      acc_ready.before(b, (QH - 1 + g) * TT)))
                        nc.vector.reciprocal(inv[g % 2][:, :], norm[g % 2][:, :]).then_inc(inv_ready.sem, 1)
                        dve.wait_ge(*inv_ready.now(b, g + 1))
                        if g == 0:
                            dve.wait_ge(*s_stored.before(b, 1))
                        for t in range(TT):
                            dve.wait_ge(*ring.product(("head", g, t), b))
                            ps = ring.place(("head", g, t))[:, :]
                            if g == 0:
                                last = nc.vector.tensor_scalar(acc[:, t, :], ps, inv[0][:, t:t + 1], None, ALU.mult)
                            else:
                                dve.wait_ge(*acc_ready.now(b, (g - 1) * TT + t + 1))
                                last = nc.vector.scalar_tensor_tensor(acc[:, t, :], ps, inv[g % 2][:, t:t + 1],
                                                                      acc[:, t, :], ALU.mult, ALU.add)
                            last.then_inc(acc_ready.sem, 1)
                    if h < QH:
                        dve.wait_ge(*(ring.product(("head", h - 2, TT - 1), b) if h >= 2 else
                                      ring.product_before(("head", QH - 2 + h, TT - 1), b)))
                        dve.wait_ge(*M_hi_ready.now(b, h + 1))
                        nc.vector.tensor_tensor(M_part[h % 2][1][:, :], ring.place(("M", h))[:, :],
                                                M_part[h % 2][0][:, :].bitcast(F32),
                                                ALU.subtract).then_inc(M_lo_ready.sem, 1)
                        dve.wait_ge(*sq_ready.now(b, h + 1))
                        hi, lo = sq_part[h % 2]
                        nc.vector.tensor_copy(hi[:, :], sq[h % 2][:, :]).then_inc(sq_hi_ready.sem, 1)
                        dve.wait_ge(*sq_hi_ready.now(b, h + 1))
                        nc.vector.tensor_tensor(lo[:, :], sq[h % 2][:, :], hi[:, :].bitcast(F32),
                                                ALU.subtract).then_inc(sq_lo_ready.sem, 1)

            layer_norm(0)
            sequence(0, False)
            with dve.Fori(1, B - 1) as b:
                sequence(b, False)
            sequence(B - 1, True)

        @block.scalar
        def _(act):
            act.wait_ge(w_loaded, 4 * 16)
            for s in (xT_ready, expk_ready, kvT_ready, ksum_ready, reluq_ready, expq_ready, M_hi_ready):
                s.ahead(act)

            def high(h):
                cols = slice(h * D, (h + 1) * D)
                act.wait_ge(wq_loaded[h % TT], 16 * (h // TT + 1))
                nc.scalar.activation(Wq[0][:, :, cols], x_tok[:, h % TT, :].rearrange("p (k c) -> p k c", k=KT),
                                     ACT.Copy).then_inc(wq_hi_ready, 1)

            def sequence(b, first):
                act.wait_ge(*x_lo_ready.before(b, KT))
                act.wait_ge(*xT_stored.before(b, 1))
                for kt in range(KT):
                    act.wait_ge(*ring.product(("xT", kt), b))
                    nc.scalar.activation(xT[:, kt, :], ring.place(("xT", kt))[:, :], ACT.Copy).then_inc(xT_ready.sem, 1)
                for t in range(TT):
                    act.wait_ge(*mink_ready.now(b, t + 1))
                    nc.scalar.activation(expk[t % 2][:, :], expk[t % 2][:, :], ACT.Exp).then_inc(expk_ready.sem, 1)
                if first:
                    for h in range(AHEAD):
                        high(h)
                act.wait_ge(*ring.product(("kvT", 0), b))
                nc.scalar.activation(flat(kvT[:, :, :]), ring.place(("kvT", 0))[:, :], ACT.Copy).then_inc(kvT_ready.sem, 1)
                act.wait_ge(*ring.product(("ksum", 0), b))
                nc.scalar.activation(ksum[:, :], ring.place(("ksum", 0))[:, 0:KVH], ACT.Copy).then_inc(ksum_ready.sem, 1)
                act.wait_ge(*sk_ready.now(b, TT))
                for h in range(QH):
                    if first and h + AHEAD < QH:
                        high(h + AHEAD)
                    act.wait_ge(*ring.product(("q", h), b))
                    act.wait_ge(*(sq_ready.now(b, h - 1) if h >= 2 else sq_ready.before(b, QH - 1 + h)))
                    nc.scalar.activation(reluq[h % 2][:, :], ring.place(("q", h))[:, :], ACT.Relu,
                                         bias=bq[:, h:h + 1]).then_inc(reluq_ready.sem, 1)
                    act.wait_ge(*minq_ready.now(b, h + 1))
                    nc.scalar.activation(expq[h % 2][:, :], expq[h % 2][:, :], ACT.Exp).then_inc(expq_ready.sem, 1)
                    act.wait_ge(*ring.product(("M", h), b))
                    act.wait_ge(*(ring.product(("head", h - 2, TT - 1), b) if h >= 2 else
                                  ring.product_before(("head", QH - 2 + h, TT - 1), b)))
                    nc.scalar.activation(M_part[h % 2][0][:, :], ring.place(("M", h))[:, :],
                                         ACT.Copy).then_inc(M_hi_ready.sem, 1)

            sequence(0, True)
            with act.Fori(1, B) as b:
                sequence(b, False)

        @block.tensor
        def _(pe):
            pe.wait_ge(w_loaded, 4 * 16)
            pe.wait_ge(const_set, 2)
            ring.done.ahead(pe)

            def sequence(b, first):
                for job in jobs:
                    kind, n = job[0], job[1]
                    place = ring.place(job)
                    pe.wait_ge(*ring.vacated(job, b))
                    if kind == "xT":
                        for t in range(TT):
                            pe.wait_ge(*xn_ready.now(b, t + 1))
                            last = nc.tensor.transpose(place[:, t * P:(t + 1) * P], x_tok[:, t, n * P:(n + 1) * P],
                                                       ident[:, :])
                    elif kind in "kv":
                        if n == 0:
                            pe.wait_ge(wkv_loaded, 2 * 16)
                        for kt in range(KT):
                            pe.wait_ge(*xT_ready.now(b, kt + 1))
                            last = nc.tensor.matmul(place[:, :], xT[:, kt, n * P:(n + 1) * P], Wkv[kind][:, kt, :],
                                                    start=(kt == 0), stop=(kt == KT - 1))
                    elif kind == "kvT":
                        pe.wait_ge(*sk_ready.now(b, TT))
                        pe.wait_ge(*v_ready.now(b, TT))
                        for g in range(KVH):
                            for t in range(TT):
                                last = nc.tensor.matmul(place[:, g * D:(g + 1) * D], v[:, t, g * D:(g + 1) * D],
                                                        sk[:, t, g * D:(g + 1) * D], start=(t == 0),
                                                        stop=(t == TT - 1))
                    elif kind == "ksum":
                        for g in range(KVH):
                            for t in range(TT):
                                last = nc.tensor.matmul(place[:, g:g + 1], sk[:, t, g * D:(g + 1) * D], ones[:, :],
                                                        start=(t == 0), stop=(t == TT - 1))
                    elif kind == "q":
                        if first:
                            pe.wait_ge(wq_lo_ready, n + 1)
                        if n == 0:
                            pe.wait_ge(*x_lo_ready.now(b, KT))
                        for kt in range(KT):
                            last = product3(nc, place[:, :], [q[:, kt, n * D:(n + 1) * D] for q in Wq],
                                            [q[:, kt, :] for q in x_part], kt == 0, kt == KT - 1)
                    elif kind == "M":
                        pe.wait_ge(*kvT_ready.now(b, 1))
                        if first and n == 0:
                            pe.wait_ge(wo_loaded, 16)
                        last = nc.tensor.matmul(place[:, :], kvT[:, n // GROUPS, :], Wo[:, n, :], start=True, stop=True)
                    elif kind == "norm":
                        pe.wait_ge(*sq_ready.now(b, n + 1))
                        pe.wait_ge(*ksum_ready.now(b, 1))
                        for t in range(TT):
                            last = nc.tensor.matmul(place[:, t:t + 1], sq[n % 2][:, t * P:(t + 1) * P],
                                                    ksum[:, n // GROUPS:n // GROUPS + 1], start=True, stop=True)
                    else:
                        t = job[2]
                        pe.wait_ge(*M_lo_ready.now(b, n + 1))
                        pe.wait_ge(*sq_lo_ready.now(b, n + 1))
                        last = product3(nc, place[:, :], [q[:, t * P:(t + 1) * P] for q in sq_part[n % 2]],
                                        [q[:, :] for q in M_part[n % 2]], True, True)
                    last.then_inc(ring.done.sem, 1)

            sequence(0, True)
            with pe.Fori(1, B) as b:
                sequence(b, False)


def relu_gate(nc, w, x1, spill, out):
    LAG = 2
    OB = I1 // C
    first_tiles = [("up", 0, kt) for kt in range(KT)]

    def tiles_at(j):
        return ([("up", j // 4 + 1, j % 4)] if j // 4 + 1 < OB else []) + [("dn", j)]

    order = first_tiles + [x for j in range(UT) for x in tiles_at(j)]
    number = {x: i for i, x in enumerate(order)}
    items = []
    for x in order:
        if x[0] == "dn" or x[2] == 0:
            items.append(("scale", x))
        items.append(("lora", x))
    made = {item: i + 1 for i, item in enumerate(items)}

    with ExitStack() as ctx:
        def sb(name, shape, dt=F32):
            return ctx.enter_context(nc.sbuf_tensor("g_" + name, shape, dt))

        def signal(name, per, unit=1):
            return Signal(ctx, nc, "g_" + name, per, unit)

        Wup = [sb(f"Wup{i}", [P, KT, I1], F32R) for i in range(2)]
        Wdn = [sb(f"Wdn{i}", [P, UT, C], F32R) for i in range(2)]
        wide = sb("wide", [P, I1])
        narrow = sb("narrow", [P, C])
        b_up = sb("b_up", [P, UT])
        b_dn = sb("b_dn", [P, C])
        xT = sb("xT", [P, KT, T])
        x_part = [sb(f"x_part{i}", [P, KT, T], F32R) for i in range(2)]
        whole = [sb(f"whole{i}", [P, C]) for i in range(2)]
        x2 = [sb(f"x2{i}", [P, T]) for i in range(2)]
        x2_part = [[sb(f"x2_part{i}{j}", [P, T], F32R) for i in range(2)] for j in range(3)]
        z = [sb(f"z{i}", [P, C]) for i in range(2)]
        tanh_z = [sb(f"tanh_z{i}", [P, C]) for i in range(2)]
        s = sb("s", [P, TT, C])
        xs = sb("xs", [P, 2, C])
        up_q, dn_q = s[:, :, :].bitcast(I32), xs[:, :, :].bitcast(I32)
        banks = [ctx.enter_context(nc.psum_tensor(f"g_ps{i}", [P, 512], F32)) for i in range(8)]
        scale_ps, pre_ps = banks[0], banks[1]

        small_loaded = ctx.enter_context(nc.semaphore("g_small_loaded"))
        up_loaded = ctx.enter_context(nc.semaphore("g_up_loaded"))
        dn_loaded = ctx.enter_context(nc.semaphore("g_dn_loaded"))
        expansion = ctx.enter_context(nc.semaphore("g_expansion"))
        expanded = ctx.enter_context(nc.semaphore("g_expanded"))
        w_hi_ready = ctx.enter_context(nc.semaphore("g_w_hi_ready"))
        w_lo_ready = ctx.enter_context(nc.semaphore("g_w_lo_ready"))
        xT_loaded = signal("xT_loaded", 1, 16)
        s_loaded = signal("s_loaded", 1, 16)
        x1_loaded = [signal(f"x1_loaded{i}", TT // 2, 16) for i in range(2)]
        x_hi_ready = signal("x_hi_ready", KT)
        x_lo_ready = signal("x_lo_ready", KT)
        x2_ready = signal("x2_ready", UT)
        x2_hi_ready = signal("x2_hi_ready", UT)
        x2_lo_ready = signal("x2_lo_ready", UT)
        x2_used = signal("x2_used", UT - 1)
        z_ready = signal("z_ready", TT)
        tanh_z_ready = signal("tanh_z_ready", TT)
        u_ready = signal("u_ready", TT)
        sg_ready = signal("sg_ready", TT)
        out_ready = signal("out_ready", TT)
        out_stored = [signal(f"out_stored{i}", TT // 2, 16) for i in range(2)]
        U = Ring(ctx, nc, "g_U", banks[2:4], [("up", j) for j in range(UT)],
                 {("up", j): (x2_ready, j + 1) for j in range(UT)})
        Y = Ring(ctx, nc, "g_Y", banks[4:8], [("down", t) for t in range(TT)],
                 {("down", t): (z_ready, t + 1) for t in range(TT)})

        block = ctx.enter_context(nc.Block())

        @block.sync
        def _(sp):
            for q in (xT_loaded, s_loaded, *x1_loaded, *out_stored):
                q.ahead(sp)

            def load_up(ob):
                if ob > 0:
                    sp.wait_ge(expanded, 2 * number["up", ob - 1, KT - 1] + 1)
                sp.dma_start(up_q, w["up_q"].rearrange("p (k c) -> p k c", k=KT)[:, :, ob * C:(ob + 1) * C]).then_inc(
                    up_loaded, 16)

            def load_down(c):
                if c > 0:
                    sp.wait_ge(expanded, 2 * number["dn", 2 * c - 1] + 1)
                sp.dma_start(dn_q.rearrange("p a b -> p (a b)"), w["dn_q"][:, c * 2 * C:(c + 1) * 2 * C]).then_inc(
                    dn_loaded, 16)

            def load_x(b):
                sp.wait_ge(*x_lo_ready.before(b, KT))
                sp.dma_start(flat(xT[:, :, :]), slab(spill["x2"], b)).then_inc(xT_loaded.sem, 16)

            def finish(b):
                sp.wait_ge(*out_ready.before(b, TT))
                sp.dma_start(flat(s[:, :, :]), slab(spill["s"], b)).then_inc(s_loaded.sem, 16)

                def load(t):
                    stored = out_stored[t % 2]
                    sp.wait_ge(*(stored.now(b, t // 2) if t >= 2 else stored.before(b, TT // 2)))
                    sp.dma_start(xs[:, t % 2, :], x1[bass.ds(b * T + t * P, P), :]).then_inc(x1_loaded[t % 2].sem, 16)

                load(0)
                load(1)
                for t in range(TT):
                    sp.wait_ge(*out_ready.now(b, t + 1))
                    sp.dma_start(out[bass.ds(b * T + t * P, P), :], xs[:, t % 2, :]).then_inc(out_stored[t % 2].sem, 16)
                    if t + 2 < TT:
                        load(t + 2)

            load_up(0)
            sp.dma_start(wide[:, :], w["g_wide"]).then_inc(small_loaded, 16)
            sp.dma_start(narrow[:, :], w["g_narrow"]).then_inc(small_loaded, 16)
            sp.dma_start(b_up[:, :], w["b_up"]).then_inc(small_loaded, 16)
            sp.dma_start(b_dn[:, :], w["b_dn"]).then_inc(small_loaded, 16)
            load_x(0)
            load_down(0)
            for j in range(0, UT, 2):
                if j % 4 == 0 and j // 4 + 1 < OB:
                    load_up(j // 4 + 1)
                if j + 2 < UT:
                    load_down(j // 2 + 1)
            sp.wait_ge(expanded, 2 * len(order))
            with sp.Fori(1, B) as b:
                load_x(b)
                finish(b - 1)
            finish(B - 1)
            for q in out_stored:
                sp.wait_ge(q.sem, 16 * (TT // 2) * (B + 1))

        @block.gpsimd
        def _(pool):
            out_ready.ahead(pool)
            for i, x in enumerate(order):
                part = Wup[1][:, x[2], x[1] * C:(x[1] + 1) * C] if x[0] == "up" else Wdn[1][:, x[1], :]
                high = Wup[0][:, x[2], x[1] * C:(x[1] + 1) * C] if x[0] == "up" else Wdn[0][:, x[1], :]
                pool.wait_ge(w_hi_ready, i + 1)
                nc.gpsimd.tensor_tensor(part, whole[i % 2][:, :], high.bitcast(F32), ALU.subtract).then_inc(
                    w_lo_ready, 1)

            def finish(b):
                for t in range(TT):
                    pool.wait_ge(*sg_ready.now(b, t + 1))
                    pool.wait_ge(*x1_loaded[t % 2].now(b, t // 2 + 1))
                    nc.gpsimd.tensor_tensor(xs[:, t % 2, :], xs[:, t % 2, :], s[:, t, :], ALU.add).then_inc(
                        out_ready.sem, 1)

            with pool.Fori(1, B) as b:
                finish(b - 1)
            finish(B - 1)

        @block.vector
        def _(dve):
            dve.wait_ge(small_loaded, 4 * 16)
            for q in (x_lo_ready, x2_hi_ready, x2_lo_ready, z_ready, u_ready, sg_ready):
                q.ahead(dve)

            def expand(x):
                i = number[x]
                if x[0] == "up":
                    dve.wait_ge(up_loaded, 16 * (x[1] + 1))
                    q, scale, before = up_q[:, x[2], :], scale_ps, ("scale", ("up", x[1], 0))
                else:
                    dve.wait_ge(dn_loaded, 16 * (x[1] // 2 + 1))
                    q, scale, before = dn_q[:, x[1] % 2, :], pre_ps, ("scale", x)
                dve.wait_ge(expansion, made[before])
                if i >= 2:
                    dve.wait_ge(w_lo_ready, i - 1)
                nc.vector.scalar_tensor_tensor(whole[i % 2][:, :], q, -7.5, scale[:, :], ALU.add,
                                               ALU.mult).then_inc(expanded, 1)
                dve.wait_ge(expanded, 2 * i + 1)
                dve.wait_ge(expansion, made["lora", x])
                nc.vector.tensor_tensor(whole[i % 2][:, :], whole[i % 2][:, :], pre_ps[:, :], ALU.add).then_inc(
                    expanded, 1)

            def finish(b):
                dve.wait_ge(*s_loaded.now(b, 1))
                for t in range(TT):
                    dve.wait_ge(*Y.product(("down", t), b))
                    dve.wait_ge(*(sg_ready.now(b, t - 1) if t >= 2 else sg_ready.before(b, TT - 1 + t)))
                    nc.vector.tensor_tensor(z[t % 2][:, :], Y.place(("down", t))[:, :], b_dn[:, :],
                                            ALU.add).then_inc(z_ready.sem, 1)
                    dve.wait_ge(*tanh_z_ready.now(b, t + 1))
                    nc.vector.scalar_tensor_tensor(z[t % 2][:, :], tanh_z[t % 2][:, :], 1.0, z[t % 2][:, :], ALU.add,
                                                   ALU.mult).then_inc(u_ready.sem, 1)
                    dve.wait_ge(*u_ready.now(b, t + 1))
                    nc.vector.scalar_tensor_tensor(s[:, t, :], s[:, t, :], 0.5, z[t % 2][:, :], ALU.mult,
                                                   ALU.mult).then_inc(sg_ready.sem, 1)

            def sequence(b, first):
                dve.wait_ge(*U.product_before(("up", UT - 1), b))
                for kt in range(KT):
                    dve.wait_ge(*x_hi_ready.now(b, kt + 1))
                    nc.vector.tensor_tensor(x_part[1][:, kt, :], xT[:, kt, :], x_part[0][:, kt, :].bitcast(F32),
                                            ALU.subtract).then_inc(x_lo_ready.sem, 1)
                if not first:
                    finish(b - 1)
                for j in range(UT):
                    if first:
                        for x in tiles_at(j):
                            expand(x)
                    dve.wait_ge(*x2_ready.now(b, j + 1))
                    dve.wait_ge(*(x2_used.now(b, j - 2) if j >= 3 else Y.product_before(("down", TT - 1), b)))
                    hi, lo = x2_part[j % 3]
                    nc.vector.tensor_copy(hi[:, :], x2[j % 2][:, :]).then_inc(x2_hi_ready.sem, 1)
                    dve.wait_ge(*x2_hi_ready.now(b, j + 1))
                    nc.vector.tensor_tensor(lo[:, :], x2[j % 2][:, :], hi[:, :].bitcast(F32), ALU.subtract).then_inc(
                        x2_lo_ready.sem, 1)

            for x in first_tiles:
                expand(x)
            sequence(0, True)
            with dve.Fori(1, B) as b:
                sequence(b, False)
            finish(B - 1)

        @block.scalar
        def _(act):
            act.wait_ge(small_loaded, 4 * 16)
            for q in (x_hi_ready, x2_ready, tanh_z_ready):
                q.ahead(act)

            def high(x):
                part = Wup[0][:, x[2], x[1] * C:(x[1] + 1) * C] if x[0] == "up" else Wdn[0][:, x[1], :]
                act.wait_ge(expanded, 2 * number[x] + 2)
                nc.scalar.activation(part, whole[number[x] % 2][:, :], ACT.Copy).then_inc(w_hi_ready, 1)

            def finish(b):
                for t in range(TT):
                    act.wait_ge(*z_ready.now(b, t + 1))
                    act.wait_ge(*(u_ready.now(b, t - 1) if t >= 2 else u_ready.before(b, TT - 1 + t)))
                    nc.scalar.activation(tanh_z[t % 2][:, :], z[t % 2][:, :], ACT.Tanh, scale=0.5).then_inc(
                        tanh_z_ready.sem, 1)

            def sequence(b, first):
                act.wait_ge(*xT_loaded.now(b, 1))
                act.wait_ge(*U.product_before(("up", UT - 1), b))
                for kt in range(KT):
                    nc.scalar.activation(x_part[0][:, kt, :], xT[:, kt, :], ACT.Copy).then_inc(x_hi_ready.sem, 1)
                if not first:
                    finish(b - 1)
                for j in range(UT):
                    if first:
                        for x in tiles_at(j):
                            high(x)
                    act.wait_ge(*U.product(("up", j), b))
                    act.wait_ge(*(x2_lo_ready.now(b, j - 1) if j >= 2 else x2_lo_ready.before(b, UT - 1 + j)))
                    nc.scalar.activation(x2[j % 2][:, :], U.place(("up", j))[:, :], ACT.Relu,
                                         bias=b_up[:, j:j + 1]).then_inc(x2_ready.sem, 1)

            for x in first_tiles:
                high(x)
            sequence(0, True)
            with act.Fori(1, B) as b:
                sequence(b, False)
            finish(B - 1)

        @block.tensor
        def _(pe):
            pe.wait_ge(small_loaded, 4 * 16)
            for q in (U.done, Y.done, x2_used):
                q.ahead(pe)

            def make(item):
                what, x = item
                i = number[x]
                if what == "scale" and x[0] == "up":
                    if x[1] > 0:
                        pe.wait_ge(expanded, 2 * number["up", x[1] - 1, KT - 1] + 1)
                    place, lhs, rhs = scale_ps, narrow[64:72, 0:P], wide[64:72, x[1] * C:(x[1] + 1) * C]
                else:
                    if what == "scale":
                        pe.wait_ge(expanded, 2 * i)
                    elif i > 0:
                        pe.wait_ge(expanded, 2 * i + 1 if x[0] == "dn" else 2 * i)
                    place = pre_ps
                    if what == "scale":
                        lhs, rhs = wide[96:128, x[1] * P:(x[1] + 1) * P], narrow[96:128, :]
                    elif x[0] == "up":
                        lhs, rhs = narrow[0:RANK, x[2] * P:(x[2] + 1) * P], wide[0:RANK, x[1] * C:(x[1] + 1) * C]
                    else:
                        lhs, rhs = wide[32:32 + RANK, x[1] * P:(x[1] + 1) * P], narrow[32:32 + RANK, :]
                nc.tensor.matmul(place[:, :], lhs, rhs, start=True, stop=True).then_inc(expansion, 1)

            def sequence(b, first):
                for n in range(UT + LAG):
                    pre = [item for item in items if first and n < UT and item[1] in tiles_at(n)]
                    while len(pre) > 2:
                        make(pre.pop(0))
                    if n < UT:
                        pe.wait_ge(*U.vacated(("up", n), b))
                        if first and n % 4 == 0:
                            pe.wait_ge(w_lo_ready, number["up", n // 4, KT - 1] + 1)
                        cols = slice(n * P, (n + 1) * P)
                        for kt in range(KT):
                            if n == 0:
                                pe.wait_ge(*x_lo_ready.now(b, kt + 1))
                            last = product3(nc, U.place(("up", n))[:, :], [q[:, kt, cols] for q in Wup],
                                            [q[:, kt, :] for q in x_part], kt == 0, kt == KT - 1)
                        last.then_inc(U.done.sem, 1)
                    if pre:
                        make(pre.pop(0))
                    i = n - LAG
                    if i >= 0:
                        pe.wait_ge(*x2_lo_ready.now(b, i + 1))
                        if first:
                            pe.wait_ge(w_lo_ready, number["dn", i] + 1)
                        for t in range(TT):
                            if t == 2 and pre:
                                make(pre.pop(0))
                            if i == 0:
                                pe.wait_ge(*Y.vacated(("down", t), b))
                            last = product3(nc, Y.place(("down", t))[:, :],
                                            [q[:, t * P:(t + 1) * P] for q in x2_part[i % 3]],
                                            [q[:, i, :] for q in Wdn], i == 0, i == UT - 1)
                            if i == UT - 1:
                                last.then_inc(Y.done.sem, 1)
                        if i < UT - 1:
                            last.then_inc(x2_used.sem, 1)
                    elif pre:
                        make(pre.pop(0))

            for item in items:
                if item[1] in first_tiles:
                    make(item)
            sequence(0, True)
            with pe.Fori(1, B) as b:
                sequence(b, False)


SCRATCH = {"x": KT * T, "r": HH * T, "k": HH * T, "v": HH * T, "w": HH * T, "g": TT * KD,
           "x2": KT * T, "s": TT * C}


def layouts(inputs):
    a = {k: np.asarray(v) for k, v in inputs.items()}

    def tiles(m, order=None):
        m = m if order is None else m[order]
        n = m.shape[0] // P
        return m.reshape(n, P, -1).transpose(1, 0, 2).reshape(P, -1)

    def every(v):
        return np.broadcast_to(v, (P,) + v.shape)

    o = {}
    o["x"] = a["L0_attn_x"].reshape(B * T, C)[:, CHANNELS]
    o["ident"] = np.eye(P, dtype=np.float32)
    o["front"] = tiles(np.concatenate([a["L0_attn_Wx1"], a["L0_attn_Wr"], a["L0_attn_Wk"], a["L0_attn_Wv"],
                                       a["L0_attn_Ww_a"], a["L0_attn_Wg_a"]], axis=1), CHANNELS)
    x2 = a["L0_attn_Wx2"][CHANNELS].transpose(1, 2, 0)
    pad = np.concatenate([x2, x2[4:5]])
    o["Wx2"] = pad.reshape(3, 2 * LOW, C).transpose(1, 0, 2).reshape(P, -1)
    o["Wb"] = np.concatenate([a["L0_attn_Ww_b"], a["L0_attn_Wg_b"]], axis=1)
    o["front_col"] = np.concatenate([tiles(a["L0_attn_mu_x"][:, None], CHANNELS),
                                     a["L0_attn_x_bias"][:, CHANNELS].reshape(5 * KT, P).T,
                                     a["L0_attn_bw"].reshape(HH, P).T], axis=1)
    o["bg"] = every(a["L0_attn_bg"])
    hidden = np.concatenate([HIDDEN0, I0 + HIDDEN0])
    o["gu_words"] = np.tile(a["L0_ffn_gate_up_packed"][hidden].T, (2, 1))
    o["gu_scale"] = a["L0_ffn_gate_up_scales"][:, hidden][np.arange(P) % 64 // 16]
    words = a["L0_ffn_down_packed"][CHANNELS].T.reshape(JT, 16, C)
    words = np.concatenate([words, words[:B * DQ - JT]])
    o["dn_words"] = np.tile(words.transpose(1, 0, 2), (8, 1, 1)).reshape(P, -1)
    scale = a["L0_ffn_down_scales"][:, CHANNELS]
    o["dn_scale"] = every(np.concatenate([scale, scale[:B * DQ - JT]]).reshape(-1))
    nibble = [2 * jj + np.arange(P) // 64 for jj in range(2)] + [np.arange(P) // 16 % 4]
    o["shift"] = np.stack([12 - 4 * j for j in nibble], axis=1).astype(np.int32)
    key = np.arange(P)
    o["spread"] = np.stack([(key[:, None] // DK == key // DK) & (key[:, None] % DK == v) for v in range(DK)],
                           axis=1).astype(np.float32).reshape(P, -1)
    o["heads"] = (key[:, None] // DK == np.arange(HPT)).astype(np.float32)
    o["bonus"] = a["L0_attn_bonus"].reshape(HH, P).T
    o["lnw"] = every(np.tile(a["L0_attn_ln_w"], NH))
    o["lnb"] = every(np.tile(a["L0_attn_ln_b"], NH))
    o["Wo0"] = tiles(a["L0_attn_Wo"][:, CHANNELS])
    for s in "kv":
        o[f"W{s}1"] = tiles(a[f"L1_attn_W{s}"].T, CHANNELS)
        o["b" + s] = every(a["L1_attn_b" + s])
    o["Wq1"] = tiles(a["L1_attn_Wq"].T, CHANNELS)
    o["bq"] = a["L1_attn_bq"].reshape(QH, D).T
    o["Wo1"] = tiles(a["L1_attn_Wo"].T[:, CHANNELS])
    o["up_q"] = tiles(a["L1_ffn_w_up_q"].T, CHANNELS)
    o["dn_q"] = tiles(a["L1_ffn_w_down_q"][CHANNELS].T)
    up_pick = (key % 64 // 8 == np.arange(8)[:, None]).astype(np.float32)
    dn_pick = np.stack([2 * j + key // 64 == np.arange(32)[:, None] for j in range(UT)],
                       axis=1).astype(np.float32).reshape(32, -1)
    wide, narrow = np.zeros((P, I1), np.float32), np.zeros((P, C), np.float32)
    wide[0:RANK], narrow[0:RANK] = a["L1_ffn_w_up_lora_b"], a["L1_ffn_w_up_lora_a"][CHANNELS].T
    wide[32:32 + RANK], narrow[32:32 + RANK] = a["L1_ffn_w_down_lora_a"].T, a["L1_ffn_w_down_lora_b"][:, CHANNELS]
    wide[64:72], narrow[64:72, 0:P] = a["L1_ffn_w_up_scale"].T, up_pick
    wide[96:128], narrow[96:128] = dn_pick, a["L1_ffn_w_down_scale"][CHANNELS].T
    o["g_wide"], o["g_narrow"] = wide, narrow
    o["b_up"] = a["L1_ffn_b_up"].reshape(UT, P).T
    o["b_dn"] = every(a["L1_ffn_b_down"][CHANNELS])
    return {k: np.ascontiguousarray(v) for k, v in o.items()}


def build(nc, w, out):
    def scratch(name, shape):
        return nc.dram_tensor("scratch_" + name, shape, F32, kind="Internal").ap()

    spill = {k: scratch(k, (B * P, n)) for k, n in SCRATCH.items()}
    x1 = scratch("x1", (B * T, C))
    with ExitStack() as ctx:
        Wgu = ctx.enter_context(nc.sbuf_tensor("Wgu", [P, KT, 2 * I0], F32))
        Wdn = ctx.enter_context(nc.sbuf_tensor("Wdn", [P, B * DQ, C], F32))
        front(nc, w, w["x"], spill, Wgu, Wdn)
        recurrence_and_gate(nc, w, w["x"], spill, Wgu, Wdn, x1)
    linear_attention(nc, w, x1, spill)
    relu_gate(nc, w, x1, spill, out)


def kernel(**inputs):
    import concourse.bacc as bacc
    from concourse.bass_utils import run_bass_kernel_spmd as run

    nc = bacc.Bacc("TRN2", target_bir_lowering=False, num_devices=1)
    arrays = {"in_" + k: v for k, v in layouts(inputs).items()}
    w = {k[3:]: nc.dram_tensor(k, v.shape, mybir.dt.from_np(v.dtype), kind="ExternalInput").ap()
         for k, v in arrays.items()}
    out = nc.dram_tensor("out", (B * T, C), F32, kind="ExternalOutput").ap()
    build(nc, w, out)
    r = run(nc, [arrays], core_ids=[0])
    return np.ascontiguousarray(r.results[0]["out"][:, np.argsort(CHANNELS)].reshape(B, T, C))
```

```python
import numpy as np
import concourse.bass as bass
from concourse import mybir
from contextlib import ExitStack

F32 = mybir.dt.float32
F32R = mybir.dt.float32r
F16 = mybir.dt.float16
I32 = mybir.dt.int32
U32 = mybir.dt.uint32
ALU = mybir.AluOpType
ACT = mybir.ActivationFunctionType
AX = mybir.AxisListType

P = 128
B = 4
T = 512
TT = T // P
C = 512
KT = C // P
NH, DK = 16, 16
KD = NH * DK
HH = KD // P
HPT = P // DK
LOW = 64
I0 = 1408
JT = I0 // P
QH, KVH, D = 16, 4, 128
GROUPS = QH // KVH
I1 = 2048
UT = I1 // P
RANK = 16

CHANNELS = np.array([8 * (p % 64) + 2 * kt + p // 64 for kt in range(KT) for p in range(P)])
HIDDEN0 = np.array([P * m + 8 * (p % 16) + p // 16 for m in range(JT) for p in range(P)])


GQ = 2 * I0 // B
DQ = -(-JT // B)
UNPACK_STEPS = 3 * (2 + DQ)


class Signal:

    def __init__(self, ctx, nc, name, per, unit=1):
        self.sem, self.per, self.unit = ctx.enter_context(nc.semaphore(name)), per, unit

    def ahead(self, eng):
        eng.sem_inc(self.sem, self.per * self.unit)

    def now(self, b, k):
        return self.sem, b * (self.per * self.unit) + (self.per + k) * self.unit

    def before(self, b, k):
        return self.sem, b * (self.per * self.unit) + k * self.unit


class Ring:

    def __init__(self, ctx, nc, name, places, jobs, reader):
        self.places, self.n, self.jobs, self.reader = places, len(places), jobs, reader
        self.index = {job: i for i, job in enumerate(jobs)}
        assert len(self.index) == len(jobs) >= self.n
        self.done = Signal(ctx, nc, name + "_product", len(jobs))

    def slot(self, job):
        return self.index[job] % self.n

    def place(self, job):
        return self.places[self.slot(job)]

    def product(self, job, b):
        return self.done.now(b, self.index[job] + 1)

    def product_before(self, job, b):
        return self.done.before(b, self.index[job] + 1)

    def vacated(self, job, b):
        i = self.index[job]
        if i >= self.n:
            signal, k = self.reader[self.jobs[i - self.n]]
            return signal.now(b, k)
        last = max(j for j in range(len(self.jobs)) if j % self.n == i)
        signal, k = self.reader[self.jobs[last]]
        return signal.before(b, k)


def rows(ap, b):
    return ap[bass.ds(b * T, T), :].rearrange("(t p) c -> p t c", p=P)


def slab(ap, b):
    return ap[bass.ds(b * P, P), :]


def flat(ap):
    return ap.rearrange("p a b -> p (a b)")


def front(nc, w, x, spill, Wgu, Wdn, relay, hand):
    MIX = ["r", "w", "k", "v", "g"]
    ORDER = [2, 0, 3, 1, 4]
    N_MIX = len(ORDER) * KT

    def mixes(n):
        return [("mix", n, kt) for kt in range(KT)]

    def projections(n):
        return [("proj", n, hh) for hh in range(HH)] if MIX[ORDER[n]] in "rkv" else [("down", n)]

    jobs = [("xT", kt) for kt in range(KT)] + [("low", m) for m in range(3)] + mixes(0)
    for n in range(1, len(ORDER)):
        jobs += mixes(n) + projections(n - 1)
    jobs += [("decay", hh) for hh in range(HH)] + projections(4) + [("gate", h) for h in range(2)]

    with ExitStack() as ctx:
        def sb(name, shape, dt=F32):
            return ctx.enter_context(nc.sbuf_tensor("f_" + name, shape, dt))

        def signal(name, per, unit=1):
            return Signal(ctx, nc, "f_" + name, per, unit)

        W = sb("W", [P, KT, 1216])
        Wx1 = W[:, :, 0:320]
        Wproj = {"r": W[:, :, 320:576], "k": W[:, :, 576:832], "v": W[:, :, 832:1088]}
        Wdown = {"w": W[:, :, 1088:1152], "g": W[:, :, 1152:1216]}
        Wx2 = sb("Wx2", [P, 3, C])
        Wb = sb("Wb", [LOW, 2, KD])
        col = sb("col", [P, 6 * KT + HH])
        mu_x = col[:, 0:KT]
        bias = col[:, KT:6 * KT]
        bw = col[:, 6 * KT:6 * KT + HH]
        bg = sb("bg", [P, KD])
        ident = sb("ident", [P, P])
        x_tok, delta = relay[0:2]
        stats = sb("stats", [P, TT, 6])
        mv = sb("mv", [P, TT, 2])
        veps = sb("veps", [P, TT])
        pause = sb("pause", [P, 1])
        half = sb("half", [P, TT])
        rstd = sb("rstd", [P, TT])
        xT = sb("xT", [P, KT, T + 2])
        mixed = [relay[2], sb("mixed", [P, KT, T])]
        xn = mixed[1]
        low = sb("low", [P, 3, T])
        tlow = {s: sb("tlow" + s, [LOW, T]) for s in "wg"}
        out = {s: sb("out" + s, [P, HH, T]) for s in "rkvw"}
        expw = sb("expw", [P, T])
        gu_words = sb("gu_words", [P, GQ], U32)
        gu_scale = sb("gu_scale", [P, GQ], F16)
        dn_words = sb("dn_words", [P, DQ, C], U32)
        dn_scale = sb("dn_scale", [P, DQ, C], F16)
        shift = sb("shift", [P, 3], I32)
        shifted = sb("shifted", [P, GQ], U32)
        value = sb("value", [P, GQ], U32)
        g = sb("g", [P, TT, KD])
        tanhg = sb("tanhg", [P, TT, KD])
        gate = sb("gate", [P, TT, KD])
        banks = [ctx.enter_context(nc.psum_tensor(f"f_ps{i}", [P, 512], F32)) for i in range(8)]

        small_loaded = ctx.enter_context(nc.semaphore("f_small_loaded"))
        Wx1_loaded = ctx.enter_context(nc.semaphore("f_Wx1_loaded"))
        w_loaded = ctx.enter_context(nc.semaphore("f_w_loaded"))
        const_set = ctx.enter_context(nc.semaphore("f_const_set"))
        x_loaded = signal("x_loaded", 1, 16)
        stats_ready = signal("stats_ready", 1)
        mv_ready = signal("mv_ready", 1)
        var_ready = signal("var_ready", 1)
        rstd_ready = signal("rstd_ready", 1)
        xn_ready = signal("xn_ready", TT)
        xT_ready = signal("xT_ready", KT)
        delta_ready = signal("delta_ready", KT)
        x_mixed = signal("x_mixed", KT)
        part_ready = signal("part_ready", N_MIX)
        mix_ready = signal("mix_ready", N_MIX)
        low_ready = signal("low_ready", 3)
        tlow_ready = signal("tlow_ready", 2)
        out_ready = {s: signal("out_ready" + s, HH) for s in "rkvw"}
        expw_ready = signal("expw_ready", HH)
        g_ready = signal("g_ready", 2)
        tanhg_ready = signal("tanhg_ready", 2)
        gate_ready = signal("gate_ready", 2)
        packed_loaded = signal("packed_loaded", 1, 64)
        unpack_step = signal("unpack_step", UNPACK_STEPS)
        unpacked = signal("unpacked", 2 + DQ)
        stored = {s: signal("stored" + s, 1, 16) for s in "xrkvwg"}

        reader = {}
        for job in jobs:
            kind, n = job[0], job[1]
            if kind == "xT":
                reader[job] = (xT_ready, n + 1)
            elif kind == "low":
                reader[job] = (low_ready, n + 1)
            elif kind == "mix":
                reader[job] = (part_ready, n * KT + job[2] + 1)
            elif kind == "proj":
                reader[job] = (out_ready[MIX[ORDER[n]]], job[2] + 1)
            elif kind == "down":
                reader[job] = (tlow_ready, 1 if MIX[ORDER[n]] == "w" else 2)
            elif kind == "decay":
                reader[job] = (expw_ready, n + 1)
            else:
                reader[job] = (g_ready, n + 1)
        ring = Ring(ctx, nc, "f", banks, jobs, reader)

        def last_reader(use):
            return ("low", 2) if use == 0 else projections(use - 1)[-1]

        block = ctx.enter_context(nc.Block())

        @block.sync
        def _(sp):
            def load_x(b):
                sp.wait_ge(*xn_ready.before(b, TT))
                sp.dma_start(x_tok[:, :, :], rows(x, b)).then_inc(x_loaded.sem, 16)

            def load_packed(b):
                sp.wait_ge(*unpacked.before(b, 2 + DQ))
                sp.dma_start(gu_words[:, :].bitcast(I32), w["gu_words"][:, bass.ds(b * GQ, GQ)]).then_inc(packed_loaded.sem, 16)
                sp.dma_start(gu_scale[:, :], w["gu_scale"][:, bass.ds(b * GQ, GQ)]).then_inc(packed_loaded.sem, 16)
                sp.dma_start(flat(dn_words[:, :, :]).bitcast(I32),
                             w["dn_words"][:, bass.ds(b * (DQ * C), DQ * C)]).then_inc(packed_loaded.sem, 16)
                sp.dma_start(flat(dn_scale[:, :, :]),
                             w["dn_scale"][:, bass.ds(b * (DQ * C), DQ * C)]).then_inc(packed_loaded.sem, 16)

            def sequence(b, last=False):
                load_packed(b)
                sp.wait_ge(*xT_ready.now(b, KT))
                sp.dma_start(slab(spill["x"], b).rearrange("p (n t) -> p n t", n=KT),
                             xT[:, :, 2:T + 2]).then_inc(stored["x"].sem, 16)
                if not last:
                    load_x(b + 1)
                for s in "krvw":
                    sp.wait_ge(*out_ready[s].now(b, HH))
                    sp.dma_start(slab(spill[s], b), flat(out[s][:, :, :])).then_inc(stored[s].sem, 16)
                if last:
                    sp.wait_ge(*stored["x"].before(b, 1))
                    sp.dma_start(flat(relay[0][:, :, :]), slab(spill["x"], 0)).then_inc(hand, 16)
                    sp.wait_ge(*ring.product(last_reader(4), b))
                    sp.wait_ge(*stored["v"].before(b, 1))
                    sp.dma_start(flat(relay[2][:, HH:, :]), slab(spill["v"], 0)).then_inc(hand, 16)
                sp.wait_ge(*gate_ready.now(b, 2))
                sp.dma_start(slab(spill["g"], b), flat(gate[:, :, :])).then_inc(stored["g"].sem, 16)

            for s in [x_loaded, packed_loaded, *stored.values()]:
                s.ahead(sp)
            load_x(0)
            for dst, name in ((ident, "ident"), (col, "front_col"), (bg, "bg"), (shift, "shift")):
                sp.dma_start(dst[:, :], w[name]).then_inc(small_loaded, 16)
            front_w = w["front"].rearrange("p (k n) -> p k n", k=KT)
            sp.dma_start(Wx1, front_w[:, :, 0:320]).then_inc(Wx1_loaded, 16)
            sp.dma_start(flat(Wx2[:, :, :]), w["Wx2"]).then_inc(Wx1_loaded, 16)
            sp.dma_start(W[:, :, 320:], front_w[:, :, 320:]).then_inc(w_loaded, 16)
            sp.dma_start(flat(Wb[:, :, :]), w["Wb"]).then_inc(w_loaded, 16)
            with sp.Fori(0, B - 1) as b:
                sequence(b)
            sequence(B - 1, last=True)
            for s in stored.values():
                sp.wait_ge(s.sem, 16 * (B + 1))

        @block.gpsimd
        def _(pool):
            nc.gpsimd.memset(half[:, :], -0.5).then_inc(const_set, 1)
            nc.gpsimd.memset(xT[:, :, 0:2], 0.0).then_inc(const_set, 1)
            pool.wait_ge(const_set, 2)
            for s in (rstd_ready, delta_ready, mix_ready):
                s.ahead(pool)

            def deviations(b):
                pool.wait_ge(*var_ready.now(b, 1))
                nc.gpsimd.tensor_tensor(rstd[:, :], veps[:, :], half[:, :], ALU.pow).then_inc(rstd_ready.sem, 1)

            def sequence(b, last=False):
                for kt in range(KT):
                    pool.wait_ge(*xT_ready.now(b, kt + 1))
                    nc.gpsimd.tensor_tensor(delta[:, kt, :], xT[:, kt, 1:T + 1], xT[:, kt, 2:T + 2],
                                            ALU.subtract).then_inc(delta_ready.sem, 1)
                for n in range(len(ORDER)):
                    if n == 3 and not last:
                        deviations(b + 1)
                    for kt in range(KT):
                        m = mixed[(n + 1) % 2][:, kt, :]
                        pool.wait_ge(*part_ready.now(b, n * KT + kt + 1))
                        nc.gpsimd.tensor_tensor(m, m, xT[:, kt, 2:T + 2], ALU.add).then_inc(mix_ready.sem, 1)

            deviations(0)
            with pool.Fori(0, B - 1) as b:
                sequence(b)
            sequence(B - 1, last=True)

        @block.vector
        def _(dve):
            for s in (stats_ready, mv_ready, var_ready, xn_ready, x_mixed, part_ready, g_ready, gate_ready,
                      unpack_step, unpacked):
                s.ahead(dve)

            def unpack(b, n, words, shift_by, width):
                if n > 0:
                    dve.wait_ge(*unpacked.now(b, n))
                nc.vector.tensor_scalar(shifted[:, 0:width], words, shift_by, None,
                                        ALU.logical_shift_left).then_inc(unpack_step.sem, 1)
                dve.wait_ge(*unpack_step.now(b, 3 * n + 1))
                nc.vector.tensor_scalar(value[:, 0:width], shifted[:, 0:width], 3, 0x0E000E00,
                                        ALU.logical_shift_right, ALU.bitwise_and).then_inc(unpack_step.sem, 1)
                dve.wait_ge(*unpack_step.now(b, 3 * n + 2))
                nc.vector.scalar_tensor_tensor(value[:, 0:width], shifted[:, 0:width], 0x80008000,
                                               value[:, 0:width], ALU.bitwise_and,
                                               ALU.bitwise_or).then_inc(unpack_step.sem, 1)
                dve.wait_ge(*unpack_step.now(b, 3 * n + 3))

            def unpack_gate_up(b, jj):
                if jj == 0:
                    dve.wait_ge(*packed_loaded.now(b, 1))
                unpack(b, jj, gu_words[:, :], shift[:, jj:jj + 1].bitcast(U32), GQ)
                pair = value[:, :].bitcast(F16).rearrange("p (c e) -> p e c", e=2)
                for e in range(2):
                    last = nc.vector.scalar_tensor_tensor(Wgu[:, jj + 2 * e, bass.ds(b * GQ, GQ)], pair[:, e, :],
                                                          2.0 ** 14, gu_scale[:, :], ALU.mult, ALU.mult)
                last.then_inc(unpacked.sem, 1)

            def unpack_down(b, m):
                unpack(b, 2 + m, dn_words[:, m, :], shift[:, 2:3].bitcast(U32), C)
                pair = value[:, 0:C].bitcast(F16).rearrange("p (c e) -> p e c", e=2)
                for e in range(2):
                    rows_e = slice(64 * e, 64 * e + 64)
                    last = nc.vector.scalar_tensor_tensor(Wdn[rows_e, bass.ds(b * DQ + m, 1), :],
                                                          pair[rows_e, e:e + 1, :], 2.0 ** 14,
                                                          dn_scale[rows_e, m:m + 1, :], ALU.mult, ALU.mult)
                last.then_inc(unpacked.sem, 1)

            def statistics(b):
                dve.wait_ge(*x_loaded.now(b, 1))
                for t in range(TT):
                    last = nc.vector.bn_stats(stats[:, t, :], x_tok[:, t, :])
                last.then_inc(stats_ready.sem, 1)
                dve.wait_ge(*stats_ready.now(b, 1))
                nc.vector.memset(pause[:, :], 0.0)
                for t in range(TT):
                    last = nc.vector.bn_aggr(mv[:, t, :], stats[:, t, :])
                last.then_inc(mv_ready.sem, 1)
                dve.wait_ge(*mv_ready.now(b, 1))
                nc.vector.tensor_scalar(veps[:, :], mv[:, :, 1], 1e-5, None, ALU.add).then_inc(var_ready.sem, 1)

            def normalise(b):
                dve.wait_ge(*rstd_ready.now(b, 1))
                dve.wait_ge(*ring.product_before(last_reader(5), b))
                for t in range(TT):
                    nc.vector.tensor_scalar(xn[:, t, :], x_tok[:, t, :], mv[:, t, 0:1], rstd[:, t:t + 1],
                                            ALU.subtract, ALU.mult).then_inc(xn_ready.sem, 1)

            def sequence(b, last=False):
                dve.wait_ge(*ring.product_before(last_reader(4), b))
                for kt in range(KT):
                    dve.wait_ge(*delta_ready.now(b, kt + 1))
                    nc.vector.scalar_tensor_tensor(mixed[0][:, kt, :], delta[:, kt, :], mu_x[:, kt:kt + 1],
                                                   xT[:, kt, 2:T + 2], ALU.mult, ALU.add).then_inc(x_mixed.sem, 1)
                for n, i in enumerate(ORDER):
                    use = n + 1
                    if use == 1:
                        dve.wait_ge(*ring.product(("xT", KT - 1), b))
                    else:
                        dve.wait_ge(*ring.product(last_reader(use - 2), b))
                    for kt in range(KT):
                        dve.wait_ge(*ring.product(("mix", n, kt), b))
                        nc.vector.scalar_tensor_tensor(mixed[use % 2][:, kt, :], ring.place(("mix", n, kt))[:, :],
                                                       bias[:, i * KT + kt:i * KT + kt + 1], delta[:, kt, :],
                                                       ALU.add, ALU.mult).then_inc(part_ready.sem, 1)
                    if n < 2:
                        unpack_gate_up(b, n)
                    else:
                        unpack_down(b, n - 2)
                    if n == 2 and not last:
                        statistics(b + 1)
                if not last:
                    normalise(b + 1)
                for h in range(2):
                    dve.wait_ge(*ring.product(("gate", h), b))
                    for n in range(2):
                        sums = nc.vector.tensor_tensor(g[:, 2 * h + n, :],
                                                       ring.place(("gate", h))[:, n * KD:(n + 1) * KD], bg[:, :],
                                                       ALU.add)
                    sums.then_inc(g_ready.sem, 1)
                dve.wait_ge(*stored["g"].before(b, 1))
                for h in range(2):
                    dve.wait_ge(*tanhg_ready.now(b, h + 1))
                    nc.vector.scalar_tensor_tensor(flat(gate[:, 2 * h:2 * h + 2, :]), flat(tanhg[:, 2 * h:2 * h + 2, :]),
                                                   1.0, flat(g[:, 2 * h:2 * h + 2, :]), ALU.add,
                                                   ALU.mult).then_inc(gate_ready.sem, 1)

            statistics(0)
            normalise(0)
            dve.wait_ge(small_loaded, 4 * 16)
            with dve.Fori(0, B - 1) as b:
                sequence(b)
            sequence(B - 1, last=True)

        @block.scalar
        def _(act):
            act.wait_ge(small_loaded, 4 * 16)
            for s in (xT_ready, low_ready, tlow_ready, expw_ready, tanhg_ready, *out_ready.values()):
                s.ahead(act)
            with act.Fori(0, B) as b:
                act.wait_ge(*mix_ready.before(b, N_MIX))
                act.wait_ge(*stored["x"].before(b, 1))
                for job in jobs:
                    kind, n = job[0], job[1]
                    place = ring.place(job)
                    if kind in ("mix", "gate"):
                        continue
                    act.wait_ge(*ring.product(job, b))
                    if kind == "xT":
                        nc.scalar.activation(xT[:, n, 2:T + 2], place[:, :], ACT.Copy).then_inc(xT_ready.sem, 1)
                    elif kind == "low":
                        h = P if n < 2 else LOW
                        nc.scalar.activation(low[0:h, n, :], place[0:h, :], ACT.Tanh).then_inc(low_ready.sem, 1)
                    elif kind == "proj":
                        s, hh = MIX[ORDER[n]], job[2]
                        act.wait_ge(*stored[s].before(b, 1))
                        nc.scalar.activation(out[s][:, hh, :], place[:, :], ACT.Copy).then_inc(out_ready[s].sem, 1)
                    elif kind == "down":
                        s = MIX[ORDER[n]]
                        nc.scalar.activation(tlow[s][:, :], place[0:LOW, :], ACT.Tanh).then_inc(tlow_ready.sem, 1)
                    elif kind == "decay":
                        if n == 1:
                            act.wait_ge(*out_ready["w"].now(b, 1))
                        nc.scalar.activation(expw[:, :], place[:, :], ACT.Exp,
                                             bias=bw[:, n:n + 1]).then_inc(expw_ready.sem, 1)
                        act.wait_ge(*expw_ready.now(b, n + 1))
                        act.wait_ge(*stored["w"].before(b, 1))
                        nc.scalar.activation(out["w"][:, n, :], expw[:, :], ACT.Exp,
                                             scale=-1.0).then_inc(out_ready["w"].sem, 1)
                for h in range(2):
                    act.wait_ge(*g_ready.now(b, h + 1))
                    act.wait_ge(*gate_ready.before(b, h + 1))
                    nc.scalar.activation(flat(tanhg[:, 2 * h:2 * h + 2, :]), flat(g[:, 2 * h:2 * h + 2, :]), ACT.Tanh,
                                         scale=0.5).then_inc(tanhg_ready.sem, 1)

        @block.tensor
        def _(pe):
            pe.wait_ge(small_loaded, 4 * 16)
            ring.done.ahead(pe)
            with pe.Fori(0, B) as b:
                for job in jobs:
                    kind, n = job[0], job[1]
                    place = ring.place(job)
                    pe.wait_ge(*ring.vacated(job, b))
                    if kind == "xT":
                        for t in range(TT):
                            pe.wait_ge(*xn_ready.now(b, t + 1))
                            last = nc.tensor.transpose(place[:, t * P:(t + 1) * P], xn[:, t, n * P:(n + 1) * P],
                                                       ident[:, :])
                    elif kind == "low":
                        h = P if n < 2 else LOW
                        for kt in range(KT):
                            pe.wait_ge(*x_mixed.now(b, kt + 1))
                            if n == 0 and kt == 0:
                                pe.wait_ge(Wx1_loaded, 2 * 16)
                            last = nc.tensor.matmul(place[0:h, :], Wx1[:, kt, n * P:n * P + h], mixed[0][:, kt, :],
                                                    start=(kt == 0), stop=(kt == KT - 1))
                    elif kind == "mix":
                        i, kt = ORDER[n], job[2]
                        pe.wait_ge(*low_ready.now(b, i // 2 + 1))
                        p = LOW * (i % 2)
                        last = nc.tensor.matmul(place[:, :], Wx2[p:p + LOW, i // 2, kt * P:(kt + 1) * P],
                                                low[p:p + LOW, i // 2, :], start=True, stop=True)
                    elif kind in ("proj", "down"):
                        s = MIX[ORDER[n]]
                        buf = mixed[(n + 1) % 2]
                        if kind == "proj":
                            h, weight = P, Wproj[s][:, :, job[2] * P:(job[2] + 1) * P]
                        else:
                            h, weight = LOW, Wdown[s]
                        if n == 0:
                            pe.wait_ge(w_loaded, 2 * 16)
                        for kt in range(KT):
                            pe.wait_ge(*mix_ready.now(b, n * KT + kt + 1))
                            last = nc.tensor.matmul(place[0:h, :], weight[:, kt, :], buf[:, kt, :],
                                                    start=(kt == 0), stop=(kt == KT - 1))
                    elif kind == "decay":
                        pe.wait_ge(*tlow_ready.now(b, 1))
                        last = nc.tensor.matmul(place[:, :], Wb[:, 0, n * P:(n + 1) * P], tlow["w"][:, :],
                                                start=True, stop=True)
                    else:
                        pe.wait_ge(*tlow_ready.now(b, 2))
                        for m in range(2):
                            t = 2 * n + m
                            last = nc.tensor.matmul(place[:, m * KD:(m + 1) * KD], tlow["g"][:, t * P:(t + 1) * P],
                                                    Wb[:, 1, :], start=True, stop=True)
                    last.then_inc(ring.done.sem, 1)


def product3(nc, out, left, right, start, stop):
    nc.tensor.matmul(out, left[1], right[0], start=start, stop=False)
    nc.tensor.matmul(out, left[0], right[1], start=False, stop=False)
    return nc.tensor.matmul(out, left[0], right[0], start=False, stop=stop)


def recurrence_and_gate(nc, w, x, spill, Wgu, Wdn, x1, relay, parts, handed, hand):
    UNITS = HH * DK
    LAG = 2
    A_jobs = ([("vtok", n) for n in range(2)] + [("spread", u) for u in range(UNITS)] + [("bonus", 0)]
              + [("oT", hh) for hh in range(HH)] + [("s", t) for t in range(TT)])
    DOWN = [(0, 1), (2,), (3,)]
    F_jobs = [("gu", j) for j in range(JT)] + [("down", n) for n in range(len(DOWN))]

    PIECES = [(side, kt) for side in range(2) for kt in range(KT)]
    order = [("gu", 0, PIECES), ("vtok", 0), ("vtok", 1)]
    for u in range(UNITS):
        if u // 3 + 1 < JT:
            order.append(("gu", u // 3 + 1, PIECES[3 * (u % 3):3 * (u % 3) + 3]))
        order.append(("spread", u))
        if u >= LAG:
            order.append(("sum", u - LAG))
    order += [("sum", u) for u in range(UNITS - LAG, UNITS)]
    order += [("bonus", 0), ("down", 0), ("oT", 0), ("oT", 1), ("down", 1), ("down", 2)]
    order += [("s", t) for t in range(TT)]

    with ExitStack() as ctx:
        def sb(name, shape, dt=F32):
            return ctx.enter_context(nc.sbuf_tensor("r_" + name, shape, dt))

        def twins(name, shape, other, other_shape):
            with nc.sbuf_tensor("r_" + name, shape, F32R) as part:
                pass
            return part, sb(other, other_shape)

        def signal(name, per, unit=1):
            return Signal(ctx, nc, "r_" + name, per, unit)

        spread = sb("spread", [P, DK, P], F32R)
        ident32 = sb("ident32", [P, P])
        ident = sb("ident", [P, P], F32R)
        heads = sb("heads", [P, HPT])
        Wo = sb("Wo", [P, HH, C])
        bonus = sb("bonus", [P, HH])
        lnw = sb("lnw", [P, KD])
        lnb = sb("lnb", [P, KD])
        half = sb("half", [P, NH * TT])
        x_lo, x_hi, xT = parts[0], parts[1], relay[0]
        v_hi, v_lo, vT = parts[2][:, 0:HH, :], parts[2][:, HH:, :], relay[2][:, HH:, :]
        rT = [sb(f"rT{i}", [P, T]) for i in range(HH)]
        kT = [sb(f"kT{i}", [P, T]) for i in range(HH)]
        dT = [sb(f"dT{i}", [P, T]) for i in range(HH)]
        v_tok = sb("v_tok", [P, TT, KD])
        kv = [sb(f"kv{i}", [P, T]) for i in range(2)]
        S = [sb(f"S{i}", [P, T + 1]) for i in range(2)]
        rS = [sb(f"rS{i}", [P, T]) for i in range(3)]
        rkb = sb("rkb", [P, HH, T])
        gate = sb("gate", [P, TT, KD])
        vc = sb("vc", [P, TT, KD])
        o = sb("o", [P, TT, KD])
        small = {s: sb(s, [P, TT * NH]) for s in ("osum", "oss", "oveps", "orstd")}
        w_hi, w_lo = [None, None], [None, None]
        w_hi[0], tanh_y = twins("w_hi0", [P, KT, 2, P], "tanh_y", [P, 2, C])
        w_hi[1], oT = twins("w_hi1", [P, KT, 2, P], "oT", [P, HH, T])
        w_lo[0], u1_first = twins("w_lo0", [P, KT, 2, P], "u1_first", [P, 2, C])
        w_lo[1], u1_second = twins("w_lo1", [P, KT, 2, P], "u1_second", [P, 2, C])
        u1 = [pair[:, i, :] for pair in (u1_first, u1_second) for i in range(2)]
        h = sb("h", [P, JT, T])
        spread32 = flat(h[:, 0:DK * P // T, :])
        tanh_gate = [sb(f"tanh_gate{i}", [P, T]) for i in range(2)]
        hg = sb("hg", [P, T])
        ysq = hg
        yss = sb("yss", [P, TT])
        yveps = sb("yveps", [P, TT])
        yr = sb("yr", [P, TT])
        hyr = sb("hyr", [P, TT])
        xs = sb("xs", [P, TT, C])
        banks = [ctx.enter_context(nc.psum_tensor(f"r_ps{i}", [P, 512], F32)) for i in range(8)]

        w_loaded = ctx.enter_context(nc.semaphore("r_w_loaded"))
        wo_loaded = ctx.enter_context(nc.semaphore("r_wo_loaded"))
        spread_loaded = ctx.enter_context(nc.semaphore("r_spread_loaded"))
        const_set = ctx.enter_context(nc.semaphore("r_const_set"))
        rounded = ctx.enter_context(nc.semaphore("r_rounded"))
        xT_loaded = signal("xT_loaded", 1, 16)
        rkd_loaded = [signal(f"rkd_loaded{i}", 1, 48) for i in range(HH)]
        v_loaded = signal("v_loaded", 1, 16)
        g_loaded = signal("g_loaded", 1, 16)
        x_loaded = signal("x_loaded", 1, 16)
        x1_stored = signal("x1_stored", 1, 16)
        x_hi_ready = signal("x_hi_ready", KT)
        x_lo_ready = signal("x_lo_ready", KT)
        w_hi_ready = signal("w_hi_ready", JT)
        w_lo_ready = signal("w_lo_ready", JT)
        v_hi_ready = signal("v_hi_ready", 1)
        v_lo_ready = signal("v_lo_ready", 1)
        vtok_ready = signal("vtok_ready", 2)
        rkb_ready = signal("rkb_ready", HH)
        kv_ready = signal("kv_ready", UNITS)
        S_ready = signal("S_ready", UNITS)
        rS_ready = signal("rS_ready", UNITS)
        summed = signal("summed", UNITS)
        tanh_gate_ready = signal("tanh_gate_ready", JT)
        hg_ready = signal("hg_ready", JT)
        h_ready = signal("h_ready", JT)
        vc_ready = signal("vc_ready", 1)
        o_ready = signal("o_ready", TT)
        osum_ready = signal("osum_ready", 1)
        centred = signal("centred", 1)
        squared = signal("squared", 1)
        oss_ready = signal("oss_ready", 1)
        oveps_ready = signal("oveps_ready", 1)
        orstd_ready = signal("orstd_ready", 1)
        o_step = signal("o_step", 3)
        gated_ready = signal("gated_ready", 1)
        oT_ready = signal("oT_ready", HH)
        yss_ready = signal("yss_ready", TT)
        yveps_ready = signal("yveps_ready", len(DOWN))
        yr_ready = signal("yr_ready", len(DOWN))
        hyr_ready = signal("hyr_ready", len(DOWN))
        tanh_y_ready = signal("tanh_y_ready", TT)
        u1_ready = signal("u1_ready", TT)
        sg_ready = signal("sg_ready", TT)
        x1_ready = signal("x1_ready", TT)

        A = Ring(ctx, nc, "r_A", banks[0:2], A_jobs,
                 {**{("vtok", n): (vtok_ready, n + 1) for n in range(2)},
                  **{("spread", u): (kv_ready, u + 1) for u in range(UNITS)},
                  ("bonus", 0): (vc_ready, 1),
                  **{("oT", hh): (oT_ready, hh + 1) for hh in range(HH)},
                  **{("s", t): (sg_ready, t + 1) for t in range(TT)}})
        O = banks[2:4]
        F = Ring(ctx, nc, "r_F", [banks[4:6], banks[6:8]], F_jobs,
                 {**{("gu", j): (h_ready, j + 1) for j in range(JT)},
                  **{("down", n): (u1_ready, DOWN[n][-1] + 1) for n in range(len(DOWN))}})

        def tile_weights(j):
            return Wgu[:, :, :].rearrange("p k (s n) -> p k s n", s=2)[:, :, :, j * P:(j + 1) * P]

        block = ctx.enter_context(nc.Block())

        @block.sync
        def _(sp):
            for s in [xT_loaded, *rkd_loaded, v_loaded, g_loaded, x_loaded, x1_stored]:
                s.ahead(sp)

            def load_x(b):
                if isinstance(b, int):
                    sp.wait_ge(handed, 2 * 16)
                    sp.sem_inc(xT_loaded.sem, 16)
                    sp.sem_inc(v_loaded.sem, 16)
                    return
                sp.wait_ge(*F.product_before(("gu", JT - 1), b))
                sp.dma_start(flat(xT[:, :, :]), slab(spill["x"], b)).then_inc(xT_loaded.sem, 16)

            def load(b):
                if not isinstance(b, int):
                    sp.wait_ge(*A.product_before(("spread", UNITS - 1), b))
                    sp.dma_start(flat(vT[:, :, :]), slab(spill["v"], b)).then_inc(v_loaded.sem, 16)
                for hh in range(HH):
                    sp.wait_ge(*rS_ready.before(b, DK * (hh + 1)))
                    for dst, s in ((rT, "r"), (kT, "k"), (dT, "w")):
                        sp.dma_start(dst[hh][:, :], slab(spill[s], b)[:, hh * T:(hh + 1) * T]).then_inc(
                            rkd_loaded[hh].sem, 16)
                sp.wait_ge(*gated_ready.before(b, 1))
                sp.dma_start(flat(gate[:, :, :]), slab(spill["g"], b)).then_inc(g_loaded.sem, 16)

            load_x(0)
            sp.dma_start(ident32[:, :], w["ident"]).then_inc(spread_loaded, 16)
            sp.dma_start(spread32, w["spread"]).then_inc(spread_loaded, 16)
            for dst, name in ((heads, "heads"), (bonus, "bonus"), (lnw, "lnw"), (lnb, "lnb")):
                sp.dma_start(dst[:, :], w[name]).then_inc(w_loaded, 16)
            load(0)
            sp.dma_start(flat(Wo[:, :, :]), w["Wo0"]).then_inc(wo_loaded, 16)
            sp.dma_start(xs[:, :, :], rows(x, 0)).then_inc(x_loaded.sem, 16)
            with sp.Fori(1, B) as b:
                load_x(b)
                load(b)
                sp.wait_ge(*x1_ready.before(b, TT))
                sp.dma_start(rows(x1, b - 1), xs[:, :, :]).then_inc(x1_stored.sem, 16)
                sp.wait_ge(*x1_stored.before(b, 1))
                sp.dma_start(xs[:, :, :], rows(x, b)).then_inc(x_loaded.sem, 16)
            sp.wait_ge(*F.product(("gu", JT - 1), B - 1))
            sp.dma_start(relay[0][:, :, :], rows(x1, 0)).then_inc(hand, 16)
            sp.dma_start(flat(relay[1][:, :, :]), w["Wk1"]).then_inc(hand, 16)
            sp.wait_ge(*A.product(("spread", UNITS - 1), B - 1))
            sp.dma_start(flat(relay[2][:, :, :]), w["Wv1"]).then_inc(hand, 16)
            for t in range(TT):
                sp.wait_ge(*x1_ready.now(B - 1, t + 1))
                sp.dma_start(x1[(B - 1) * T + t * P:(B - 1) * T + (t + 1) * P, :], xs[:, t, :]).then_inc(
                    x1_stored.sem, 16)
            sp.wait_ge(x1_stored.sem, 16 * (B + TT))

        @block.gpsimd
        def _(pool):
            nc.gpsimd.memset(half[:, :], -0.5).then_inc(const_set, 1)
            for i in range(2):
                nc.gpsimd.memset(S[i][:, 0:1], 0.0).then_inc(const_set, 1)
            pool.wait_ge(const_set, 3)
            for s in (rS_ready, orstd_ready, yr_ready, x1_ready):
                s.ahead(pool)
            pool.wait_ge(spread_loaded, 2 * 16)
            nc.gpsimd.tensor_copy(ident[:, :], ident32[:, :]).then_inc(rounded, 1)
            nc.gpsimd.tensor_copy(flat(spread[:, :, :]), spread32).then_inc(rounded, 1)
            with pool.Fori(0, B) as b:
                for u in range(UNITS):
                    pool.wait_ge(*S_ready.now(b, u + 1))
                    if u >= 3:
                        pool.wait_ge(*summed.now(b, u - 2))
                    else:
                        pool.wait_ge(*summed.before(b, UNITS - (UNITS - 1 - u) % 3))
                    nc.gpsimd.tensor_tensor(rS[u % 3][:, :], S[u % 2][:, 0:T], rT[u // DK][:, :],
                                            ALU.mult).then_inc(rS_ready.sem, 1)
                pool.wait_ge(*oveps_ready.now(b, 1))
                nc.gpsimd.tensor_tensor(small["orstd"][:, :], small["oveps"][:, :], half[:, :],
                                        ALU.pow).then_inc(orstd_ready.sem, 1)
                for n, ts in enumerate(DOWN):
                    pool.wait_ge(*yveps_ready.now(b, n + 1))
                    cols = slice(ts[0], ts[-1] + 1)
                    nc.gpsimd.tensor_tensor(yr[:, cols], yveps[:, cols], half[:, cols],
                                            ALU.pow).then_inc(yr_ready.sem, 1)
                pool.wait_ge(*x_loaded.now(b, 1))
                for t in range(TT):
                    pool.wait_ge(*sg_ready.now(b, t + 1))
                    nc.gpsimd.tensor_tensor(xs[:, t, :], xs[:, t, :], u1[t], ALU.add).then_inc(x1_ready.sem, 1)

        @block.vector
        def _(dve):
            dve.wait_ge(const_set, 3)
            for s in (x_lo_ready, w_lo_ready, v_lo_ready, rkb_ready, kv_ready, S_ready, hg_ready, h_ready, vc_ready, o_ready,
                      osum_ready, centred, oss_ready, oveps_ready, o_step, gated_ready, yveps_ready, hyr_ready,
                      u1_ready, sg_ready):
                s.ahead(dve)
            with dve.Fori(0, B) as b:
                def split_weights(j):
                    dve.wait_ge(*w_hi_ready.now(b, j + 1))
                    if j >= 2:
                        dve.wait_ge(*F.product(("gu", j - 2), b))
                    else:
                        dve.wait_ge(*x1_ready.before(b, 2 * j + 2))
                    nc.vector.tensor_tensor(w_lo[j % 2][:, :, :, :], tile_weights(j),
                                            w_hi[j % 2][:, :, :, :].bitcast(F32),
                                            ALU.subtract).then_inc(w_lo_ready.sem, 1)

                for kt in range(KT):
                    dve.wait_ge(*x_hi_ready.now(b, kt + 1))
                    nc.vector.tensor_tensor(x_lo[:, kt, :], xT[:, kt, :],
                                            x_hi[:, kt, :].bitcast(F32), ALU.subtract).then_inc(x_lo_ready.sem, 1)
                    if kt == 0:
                        split_weights(0)
                dve.wait_ge(*v_hi_ready.now(b, 1))
                nc.vector.tensor_tensor(flat(v_lo[:, :, :]), flat(vT[:, :, :]),
                                        flat(v_hi[:, :, :]).bitcast(F32), ALU.subtract).then_inc(v_lo_ready.sem, 1)
                split_weights(1)
                dve.wait_ge(w_loaded, 4 * 16)
                dve.wait_ge(rounded, 2)
                dve.wait_ge(*F.product_before(("down", len(DOWN) - 1), b))

                def hidden(j):
                    dve.wait_ge(*tanh_gate_ready.now(b, j + 1))
                    gate_ps, up_ps = F.place(("gu", j))
                    dve.wait_ge(*(h_ready.now(b, j) if j > 0 else h_ready.before(b, JT)))
                    nc.vector.scalar_tensor_tensor(hg[:, :], tanh_gate[j % 2][:, :], 1.0, gate_ps[:, :], ALU.add,
                                                   ALU.mult).then_inc(hg_ready.sem, 1)
                    dve.wait_ge(*hg_ready.now(b, j + 1))
                    nc.vector.scalar_tensor_tensor(h[:, j, :], hg[:, :], 0.5, up_ps[:, :], ALU.mult,
                                                   ALU.mult).then_inc(h_ready.sem, 1)

                for u in range(UNITS):
                    hh = u // DK
                    if u % DK == 0:
                        dve.wait_ge(*rkd_loaded[hh].now(b, 1))
                        nc.vector.scalar_tensor_tensor(rkb[:, hh, :], rT[hh][:, :], bonus[:, hh:hh + 1], kT[hh][:, :],
                                                       ALU.mult, ALU.mult).then_inc(rkb_ready.sem, 1)
                    dve.wait_ge(*A.product(("spread", u), b))
                    dve.wait_ge(*(S_ready.now(b, u - 1) if u >= 2 else S_ready.before(b, UNITS - 1 + u)))
                    nc.vector.tensor_tensor(kv[u % 2][:, :], kT[hh][:, :], A.place(("spread", u))[:, :],
                                            ALU.mult).then_inc(kv_ready.sem, 1)
                    dve.wait_ge(*kv_ready.now(b, u + 1))
                    dve.wait_ge(*(rS_ready.now(b, u - 1) if u >= 2 else rS_ready.before(b, UNITS - 1 + u)))
                    nc.vector.tensor_tensor_scan(S[u % 2][:, 1:T + 1], dT[hh][:, :], kv[u % 2][:, :], 0.0, ALU.mult,
                                                 ALU.add).then_inc(S_ready.sem, 1)
                    if u % 3 == 0 and u // 3 + 2 < JT:
                        split_weights(u // 3 + 2)
                    elif u % 3 == 1:
                        hidden(u // 3)

                dve.wait_ge(*A.product(("bonus", 0), b))
                dve.wait_ge(*vtok_ready.now(b, 2))
                by_head = "p t (h v) -> p (t h) v"
                wide = [P, TT * NH, DK]
                nc.vector.tensor_tensor(vc[:, :, :].rearrange(by_head, v=DK), v_tok[:, :, :].rearrange(by_head, v=DK),
                                        A.place(("bonus", 0))[:, 0:TT * NH].unsqueeze(2).broadcast_to(wide),
                                        ALU.mult).then_inc(vc_ready.sem, 1)
                dve.wait_ge(*vc_ready.now(b, 1))
                dve.wait_ge(*summed.now(b, UNITS))
                for t in range(TT):
                    ps = O[t // 2][:, (t % 2) * KD:(t % 2 + 1) * KD]
                    nc.vector.tensor_tensor(o[:, t, :].rearrange("p (g h v) -> p g h v", g=HH, v=DK),
                                            vc[:, t, :].rearrange("p (g h v) -> p g h v", g=HH, v=DK),
                                            ps.rearrange("p (g v h) -> p g h v", g=HH, v=DK),
                                            ALU.add).then_inc(o_ready.sem, 1)
                dve.wait_ge(*o_ready.now(b, TT))
                o3 = o[:, :, :].rearrange(by_head, v=DK)
                nc.vector.tensor_reduce(small["osum"][:, :], o3, AX.X, ALU.add).then_inc(osum_ready.sem, 1)
                dve.wait_ge(*osum_ready.now(b, 1))
                nc.vector.scalar_tensor_tensor(o3, small["osum"][:, :].unsqueeze(2).broadcast_to(wide), -1.0 / DK, o3,
                                               ALU.mult, ALU.add).then_inc(centred.sem, 1)
                dve.wait_ge(*squared.now(b, 1))
                nc.vector.tensor_reduce(small["oss"][:, :], vc[:, :, :].rearrange(by_head, v=DK), AX.X,
                                        ALU.add).then_inc(oss_ready.sem, 1)
                dve.wait_ge(*oss_ready.now(b, 1))
                nc.vector.tensor_scalar(small["oveps"][:, :], small["oss"][:, :], 1.0 / DK, 1e-5, ALU.mult,
                                        ALU.add).then_inc(oveps_ready.sem, 1)
                dve.wait_ge(*orstd_ready.now(b, 1))
                nc.vector.tensor_tensor(o3, o3, small["orstd"][:, :].unsqueeze(2).broadcast_to(wide),
                                        ALU.mult).then_inc(o_step.sem, 1)
                dve.wait_ge(*o_step.now(b, 1))
                nc.vector.tensor_tensor(o[:, :, :], o[:, :, :], lnw[:, :].unsqueeze(1).broadcast_to([P, TT, KD]),
                                        ALU.mult).then_inc(o_step.sem, 1)
                dve.wait_ge(*o_step.now(b, 2))
                nc.vector.tensor_tensor(o[:, :, :], o[:, :, :], lnb[:, :].unsqueeze(1).broadcast_to([P, TT, KD]),
                                        ALU.add).then_inc(o_step.sem, 1)
                dve.wait_ge(*o_step.now(b, 3))
                dve.wait_ge(*g_loaded.now(b, 1))
                nc.vector.scalar_tensor_tensor(flat(o[:, :, :]), flat(gate[:, :, :]), 0.5, flat(o[:, :, :]), ALU.mult,
                                               ALU.mult).then_inc(gated_ready.sem, 1)
                for n, ts in enumerate(DOWN):
                    cols = slice(ts[0], ts[-1] + 1)
                    dve.wait_ge(*yss_ready.now(b, ts[-1] + 1))
                    nc.vector.tensor_scalar(yveps[:, cols], yss[:, cols], 1.0 / C, 1e-6, ALU.mult,
                                            ALU.add).then_inc(yveps_ready.sem, 1)
                    dve.wait_ge(*yr_ready.now(b, n + 1))
                    nc.vector.tensor_scalar(hyr[:, cols], yr[:, cols], 0.5, None, ALU.mult).then_inc(hyr_ready.sem, 1)
                    for i, t in enumerate(ts):
                        dve.wait_ge(*tanh_y_ready.now(b, t + 1))
                        dve.wait_ge(*x1_ready.before(b, t + 1))
                        nc.vector.scalar_tensor_tensor(u1[t], tanh_y[:, t % 2, :], 1.0,
                                                       F.place(("down", n))[i][:, :], ALU.add,
                                                       ALU.mult).then_inc(u1_ready.sem, 1)
                for t in range(TT):
                    dve.wait_ge(*A.product(("s", t), b))
                    dve.wait_ge(*u1_ready.now(b, t + 1))
                    nc.vector.scalar_tensor_tensor(u1[t], A.place(("s", t))[:, :], hyr[:, t:t + 1], u1[t],
                                                   ALU.mult, ALU.mult).then_inc(sg_ready.sem, 1)

        @block.scalar
        def _(act):
            for s in (x_hi_ready, w_hi_ready, v_hi_ready, vtok_ready, tanh_gate_ready, squared, oT_ready, yss_ready, tanh_y_ready):
                s.ahead(act)
            with act.Fori(0, B) as b:
                def round_weights(j):
                    if j >= 2:
                        act.wait_ge(*F.product(("gu", j - 2), b))
                    elif j == 0:
                        act.wait_ge(*u1_ready.before(b, TT))
                    else:
                        act.wait_ge(*A.product_before(("s", TT - 1), b))
                    nc.scalar.activation(w_hi[j % 2][:, :, :, :], tile_weights(j), ACT.Copy).then_inc(w_hi_ready.sem, 1)

                act.wait_ge(*xT_loaded.now(b, 1))
                for kt in range(KT):
                    nc.scalar.activation(x_hi[:, kt, :], xT[:, kt, :],
                                         ACT.Copy).then_inc(x_hi_ready.sem, 1)
                    if kt == 0:
                        round_weights(0)
                act.wait_ge(*v_loaded.now(b, 1))
                nc.scalar.activation(flat(v_hi[:, :, :]), flat(vT[:, :, :]),
                                     ACT.Copy).then_inc(v_hi_ready.sem, 1)
                round_weights(1)
                act.wait_ge(*vc_ready.before(b, 1))
                for n in range(2):
                    act.wait_ge(*A.product(("vtok", n), b))
                    nc.scalar.activation(flat(v_tok[:, 2 * n:2 * n + 2, :]), A.place(("vtok", n))[:, :],
                                         ACT.Copy).then_inc(vtok_ready.sem, 1)
                for j in range(JT):
                    act.wait_ge(*F.product(("gu", j), b))
                    act.wait_ge(*(h_ready.now(b, j - 1) if j >= 2 else h_ready.before(b, JT)))
                    nc.scalar.activation(tanh_gate[j % 2][:, :], F.place(("gu", j))[0][:, :], ACT.Tanh,
                                         scale=0.5).then_inc(tanh_gate_ready.sem, 1)
                    if j + 2 < JT:
                        round_weights(j + 2)
                act.wait_ge(*centred.now(b, 1))
                nc.scalar.activation(flat(vc[:, :, :]), flat(o[:, :, :]), ACT.Square).then_inc(squared.sem, 1)

                def squares(n):
                    act.wait_ge(*F.product(("down", n), b))
                    for i, t in enumerate(DOWN[n]):
                        act.wait_ge(*(yss_ready.now(b, t) if t > 0 else yss_ready.before(b, TT)))
                        nc.scalar.activation(ysq[:, :], F.place(("down", n))[i][:, :], ACT.Square,
                                             accum_out=yss[:, t:t + 1]).then_inc(yss_ready.sem, 1)

                def tanhs(n):
                    act.wait_ge(*hyr_ready.now(b, n + 1))
                    for i, t in enumerate(DOWN[n]):
                        act.wait_ge(*(u1_ready.now(b, t - 1) if t >= 2 else u1_ready.before(b, t + 3)))
                        nc.scalar.activation(tanh_y[:, t % 2, :], F.place(("down", n))[i][:, :], ACT.Tanh,
                                             scale=hyr[:, t:t + 1]).then_inc(tanh_y_ready.sem, 1)

                squares(0)
                for hh in range(HH):
                    act.wait_ge(*A.product(("oT", hh), b))
                    nc.scalar.activation(oT[:, hh, :], A.place(("oT", hh))[:, :], ACT.Copy).then_inc(oT_ready.sem, 1)
                tanhs(0)
                for n in (1, 2):
                    squares(n)
                    tanhs(n)

        @block.tensor
        def _(pe):
            for s in (A.done, F.done, summed):
                s.ahead(pe)
            with pe.Fori(0, B) as b:
                for step in order:
                    kind, n = job = step[:2]
                    if kind == "sum":
                        u, hh = n, n // DK
                        pe.wait_ge(*rS_ready.now(b, u + 1))
                        if u == 0:
                            pe.wait_ge(*o_ready.before(b, TT))
                        for t in range(TT):
                            at = (t % 2) * KD + hh * P + (u % DK) * HPT
                            last = nc.tensor.matmul(O[t // 2][:, at:at + HPT], rS[u % 3][:, t * P:(t + 1) * P],
                                                    heads[:, :], start=True, stop=True)
                        last.then_inc(summed.sem, 1)
                        continue
                    ring = F if kind in ("gu", "down") else A
                    place = ring.place(job)
                    if kind != "gu" or step[2][0] == PIECES[0]:
                        pe.wait_ge(*ring.vacated(job, b))
                    if job == ("vtok", 0):
                        pe.wait_ge(rounded, 2)
                        pe.wait_ge(w_loaded, 4 * 16)
                    if kind == "vtok":
                        pe.wait_ge(*v_lo_ready.now(b, 1))
                        for m in range(2):
                            t = 2 * n + m
                            for hh in range(HH):
                                at = m * KD + hh * P
                                for i, part in enumerate((v_hi, v_lo)):
                                    last = nc.tensor.matmul(place[:, at:at + P], part[:, hh, t * P:(t + 1) * P],
                                                            ident[:, :], start=(i == 0), stop=(i == 1))
                    elif kind == "spread":
                        for i, part in enumerate((v_hi, v_lo)):
                            last = nc.tensor.matmul(place[:, :], spread[:, n % DK, :], part[:, n // DK, :],
                                                    start=(i == 0), stop=(i == 1))
                    elif kind == "gu":
                        if step[2][0] == PIECES[0]:
                            pe.wait_ge(*w_lo_ready.now(b, n + 1))
                        for side, kt in step[2]:
                            if n == 0 and side == 0:
                                pe.wait_ge(*x_lo_ready.now(b, kt + 1))
                            last = product3(nc, place[side][:, :],
                                            (w_hi[n % 2][:, kt, side, :], w_lo[n % 2][:, kt, side, :]),
                                            (x_hi[:, kt, :], x_lo[:, kt, :]), kt == 0, kt == KT - 1)
                        if step[2][-1] != PIECES[-1]:
                            continue
                    elif kind == "down":
                        for i, t in enumerate(DOWN[n]):
                            for j in range(JT):
                                if n == 0 and i == 0:
                                    pe.wait_ge(*h_ready.now(b, j + 1))
                                last = nc.tensor.matmul(place[i][:, :], h[:, j, t * P:(t + 1) * P], Wdn[:, j, :],
                                                        start=(j == 0), stop=(j == JT - 1))
                    elif kind == "bonus":
                        pe.wait_ge(*rkb_ready.now(b, HH))
                        for t in range(TT):
                            for hh in range(HH):
                                at = t * NH + hh * HPT
                                last = nc.tensor.matmul(place[:, at:at + HPT], rkb[:, hh, t * P:(t + 1) * P],
                                                        heads[:, :], start=True, stop=True)
                    elif kind == "oT":
                        pe.wait_ge(*gated_ready.now(b, 1))
                        for t in range(TT):
                            last = nc.tensor.transpose(place[:, t * P:(t + 1) * P], o[:, t, n * P:(n + 1) * P],
                                                       ident32[:, :])
                    else:
                        if n == 0:
                            pe.wait_ge(*oT_ready.now(b, HH))
                            pe.wait_ge(wo_loaded, 16)
                        for hh in range(HH):
                            last = nc.tensor.matmul(place[:, :], oT[:, hh, n * P:(n + 1) * P], Wo[:, hh, :],
                                                    start=(hh == 0), stop=(hh == HH - 1))
                    last.then_inc(ring.done.sem, 1)


def linear_attention(nc, w, x1, spill, relay, handed, hand):
    AHEAD = 2
    LN_HEAD = QH - 2
    LN_STEPS = {QH - 9 + t: ("stats", t) for t in range(TT)}
    LN_STEPS.update({QH - 5: ("aggregate", 0)})
    LN_STEPS.update({QH - 4 + t: ("normalise", t) for t in range(TT)})
    RSQRT_HEAD = QH - 5
    jobs = ([("xT", kt) for kt in range(KT)] + [(s, t) for s in "kv" for t in range(TT)]
            + [("kvT", 0), ("ksum", 0)])
    for h in range(QH + 1):
        if h < QH:
            jobs += [("q", h), ("M", h)]
        if h > 0:
            jobs += [("norm", h - 1)] + [("head", h - 1, t) for t in range(TT)]

    with ExitStack() as ctx:
        def sb(name, shape, dt=F32):
            return ctx.enter_context(nc.sbuf_tensor("l_" + name, shape, dt))

        def signal(name, per, unit=1):
            return Signal(ctx, nc, "l_" + name, per, unit)

        Wkv = dict(k=relay[1], v=relay[2])
        Wq = [sb(f"Wq{i}", [P, KT, QH * D], F32R) for i in range(2)]
        Wo = sb("Wo", [P, QH, C])
        bkv = {s: sb("b" + s, [P, KVH * D]) for s in "kv"}
        bq = sb("bq", [P, QH])
        ident = sb("ident", [P, P])
        ones = sb("ones", [P, 1])
        half = sb("half", [P, TT])
        x_tok = relay[0]
        stats = sb("stats", [P, TT, 6])
        mv = sb("mv", [P, TT, 2])
        veps = sb("veps", [P, TT])
        pause = sb("pause", [P, 1])
        rstd = sb("rstd", [P, TT])
        xT = sb("xT", [P, KT, T])
        x_part = [sb(f"x_part{i}", [P, KT, T], F32R) for i in range(2)]
        sk = sb("sk", [P, TT, KVH * D])
        v = sb("v", [P, TT, KVH * D])
        kvT = sb("kvT", [P, KVH, D])
        ksum = sb("ksum", [P, KVH])
        expq = [sb(f"expq{i}", [P, T]) for i in range(2)]
        reluq = [sb(f"reluq{i}", [P, T]) for i in range(2)]
        biased, expk = reluq, expq
        sq = [sb(f"sq{i}", [P, T]) for i in range(2)]
        sq_part = [[sb(f"sq_part{i}{j}", [P, T], F32R) for i in range(2)] for j in range(2)]
        M_part = [[sb(f"M_part{i}{j}", [P, C], F32R) for i in range(2)] for j in range(2)]
        norm = [sb(f"norm{i}", [P, TT]) for i in range(2)]
        inv = [sb(f"inv{i}", [P, TT]) for i in range(2)]
        acc = sb("acc", [P, TT, C])
        banks = [ctx.enter_context(nc.psum_tensor(f"l_ps{i}", [P, 512], F32)) for i in range(8)]

        w_loaded = ctx.enter_context(nc.semaphore("l_w_loaded"))
        ident_loaded = ctx.enter_context(nc.semaphore("l_ident_loaded"))
        wo_loaded = ctx.enter_context(nc.semaphore("l_wo_loaded"))
        wq_loaded = [ctx.enter_context(nc.semaphore(f"l_wq_loaded{i}")) for i in range(TT)]
        wq_hi_ready = ctx.enter_context(nc.semaphore("l_wq_hi_ready"))
        wq_lo_ready = ctx.enter_context(nc.semaphore("l_wq_lo_ready"))
        const_set = ctx.enter_context(nc.semaphore("l_const_set"))
        x_loaded = signal("x_loaded", 1, 16)
        stats_ready = signal("stats_ready", 1)
        mv_ready = signal("mv_ready", 1)
        var_ready = signal("var_ready", 1)
        rstd_ready = signal("rstd_ready", 1)
        xn_ready = signal("xn_ready", TT)
        xT_ready = signal("xT_ready", KT)
        biased_ready = signal("biased_ready", TT)
        expk_ready = signal("expk_ready", TT)
        mink_ready = signal("mink_ready", TT)
        sk_ready = signal("sk_ready", TT)
        v_ready = signal("v_ready", TT)
        kvT_ready = signal("kvT_ready", 1)
        ksum_ready = signal("ksum_ready", 1)
        expq_ready = signal("expq_ready", QH)
        reluq_ready = signal("reluq_ready", QH)
        minq_ready = signal("minq_ready", QH)
        sq_ready = signal("sq_ready", QH)
        M_hi_ready = signal("M_hi_ready", QH)
        M_lo_ready = signal("M_lo_ready", QH)
        x_hi_ready = signal("x_hi_ready", KT)
        x_lo_ready = signal("x_lo_ready", KT)
        sq_hi_ready = signal("sq_hi_ready", QH)
        sq_lo_ready = signal("sq_lo_ready", QH)
        norm_ready = signal("norm_ready", QH)
        inv_ready = signal("inv_ready", QH)
        acc_ready = signal("acc_ready", QH * TT)
        xT_stored = signal("xT_stored", 1, 16)
        s_stored = signal("s_stored", 1, 16)

        reader = {("kvT", 0): (kvT_ready, 1), ("ksum", 0): (ksum_ready, 1)}
        for kt in range(KT):
            reader["xT", kt] = (xT_ready, kt + 1)
        for t in range(TT):
            reader["k", t] = (biased_ready, t + 1)
            reader["v", t] = (v_ready, t + 1)
        for h in range(QH):
            reader["q", h] = (minq_ready, h + 1)
            reader["M", h] = (M_lo_ready, h + 1)
            reader["norm", h] = (norm_ready, h + 1)
            for t in range(TT):
                reader["head", h, t] = (acc_ready, h * TT + t + 1)
        ring = Ring(ctx, nc, "l", banks, jobs, reader)

        block = ctx.enter_context(nc.Block())

        @block.sync
        def _(sp):
            for s in [x_loaded, xT_stored, s_stored]:
                s.ahead(sp)

            def load_x(b):
                sp.wait_ge(*ring.product(("xT", KT - 1), b - 1))
                sp.dma_start(x_tok[:, :, :], rows(x1, b)).then_inc(x_loaded.sem, 16)

            def store_xT(b):
                sp.wait_ge(*xT_ready.now(b, KT))
                sp.dma_start(slab(spill["x2"], b), flat(xT[:, :, :])).then_inc(xT_stored.sem, 16)

            def store_s(b):
                sp.wait_ge(*acc_ready.now(b, QH * TT))
                sp.dma_start(slab(spill["s"], b), flat(acc[:, :, :])).then_inc(s_stored.sem, 16)

            sp.wait_ge(handed, 3 * 16)
            sp.sem_inc(x_loaded.sem, 16)
            sp.dma_start(ident[:, :], w["ident"]).then_inc(ident_loaded, 16)
            for dst, name in ((bkv["k"], "bk"), (bkv["v"], "bv"), (bq, "bq")):
                sp.dma_start(dst[:, :], w[name]).then_inc(w_loaded, 16)
            sp.wait_ge(*ring.product(("xT", KT - 1), 0))
            for h in range(QH):
                if h >= TT:
                    sp.wait_ge(wq_lo_ready, h - TT + 1)
                sp.dma_start(x_tok[:, h % TT, :].rearrange("p (k c) -> p k c", k=KT),
                             w["Wq1"].rearrange("p (k c) -> p k c", k=KT)[:, :, h * D:(h + 1) * D]).then_inc(
                                 wq_loaded[h % TT], 16)
                if h == 3:
                    sp.dma_start(flat(Wo[:, :, :]), w["Wo1"]).then_inc(wo_loaded, 16)
                if h == TT:
                    store_xT(0)
            sp.wait_ge(wq_lo_ready, QH)
            load_x(1)
            store_s(0)
            with sp.Fori(1, B - 1) as b:
                store_xT(b)
                load_x(b + 1)
                store_s(b)
            store_xT(B - 1)
            sp.wait_ge(*ring.product(("xT", KT - 1), B - 1))
            sp.dma_start(relay[0][:, :, :].bitcast(I32), w["up_q"].rearrange("p (k c) -> p k c", k=KT)[:, :, 0:C]).then_inc(
                hand, 16)
            sp.wait_ge(*ring.product(("v", TT - 1), B - 1))
            sp.dma_start(flat(relay[1][:, :, :]), w["g_wide"]).then_inc(hand, 16)
            sp.wait_ge(*xT_stored.now(B - 1, 1))
            sp.dma_start(flat(relay[2][:, :, :]), slab(spill["x2"], 0)).then_inc(hand, 16)
            for t in range(TT):
                sp.wait_ge(*acc_ready.now(B - 1, (QH - 1) * TT + t + 1))
                sp.dma_start(slab(spill["s"], B - 1)[:, t * C:(t + 1) * C], acc[:, t, :]).then_inc(s_stored.sem, 16)
            sp.wait_ge(xT_stored.sem, 16 * (B + 1))
            sp.wait_ge(s_stored.sem, 16 * (B + TT))

        @block.gpsimd
        def _(pool):
            nc.gpsimd.memset(half[:, :], -0.5).then_inc(const_set, 1)
            nc.gpsimd.memset(ones[:, :], 1.0).then_inc(const_set, 1)
            pool.wait_ge(const_set, 2)
            rstd_ready.ahead(pool)
            sq_ready.ahead(pool)

            def rsqrt(b):
                pool.wait_ge(*var_ready.now(b, 1))
                nc.gpsimd.tensor_tensor(rstd[:, :], veps[:, :], half[:, :], ALU.pow).then_inc(rstd_ready.sem, 1)

            def low(h):
                cols = slice(h * D, (h + 1) * D)
                pool.wait_ge(wq_hi_ready, h + 1)
                nc.gpsimd.tensor_tensor(Wq[1][:, :, cols], x_tok[:, h % TT, :].rearrange("p (k c) -> p k c", k=KT),
                                        Wq[0][:, :, cols].bitcast(F32), ALU.subtract).then_inc(wq_lo_ready, 1)

            def sequence(b, first, last):
                for h in range(QH):
                    if first and h + AHEAD < QH:
                        low(h + AHEAD)
                    if h == (LN_HEAD if first else RSQRT_HEAD) and not last:
                        rsqrt(b + 1)
                    pool.wait_ge(*expq_ready.now(b, h + 1))
                    pool.wait_ge(*(sq_lo_ready.now(b, h - 1) if h >= 2 else sq_lo_ready.before(b, QH - 1 + h)))
                    pool.wait_ge(*(ring.product(("norm", h - 2), b) if h >= 2 else
                                   ring.product_before(("norm", QH - 2 + h), b)))
                    nc.gpsimd.tensor_tensor(sq[h % 2][:, :], expq[h % 2][:, :], reluq[h % 2][:, :],
                                            ALU.add).then_inc(sq_ready.sem, 1)

            rsqrt(0)
            for h in range(AHEAD):
                low(h)
            sequence(0, True, False)
            with pool.Fori(1, B - 1) as b:
                sequence(b, False, False)
            sequence(B - 1, False, True)

        @block.vector
        def _(dve):
            for s in (stats_ready, mv_ready, var_ready, xn_ready, biased_ready, mink_ready, sk_ready, v_ready,
                      minq_ready, norm_ready, inv_ready, acc_ready, M_lo_ready, x_hi_ready, x_lo_ready, sq_hi_ready,
                      sq_lo_ready):
                s.ahead(dve)

            def layer_norm_step(b, kind, t):
                if kind == "stats":
                    if t == 0:
                        dve.wait_ge(*x_loaded.now(b, 1))
                    last = nc.vector.bn_stats(stats[:, t, :], x_tok[:, t, :])
                    if t == TT - 1:
                        last.then_inc(stats_ready.sem, 1)
                elif kind == "aggregate":
                    dve.wait_ge(*stats_ready.now(b, 1))
                    nc.vector.memset(pause[:, :], 0.0)
                    for n in range(TT):
                        last = nc.vector.bn_aggr(mv[:, n, :], stats[:, n, :])
                    last.then_inc(mv_ready.sem, 1)
                    dve.wait_ge(*mv_ready.now(b, 1))
                    nc.vector.tensor_scalar(veps[:, :], mv[:, :, 1], 1e-5, None, ALU.add).then_inc(var_ready.sem, 1)
                else:
                    if t == 0:
                        dve.wait_ge(*rstd_ready.now(b, 1))
                    nc.vector.tensor_scalar(x_tok[:, t, :], x_tok[:, t, :], mv[:, t, 0:1], rstd[:, t:t + 1],
                                            ALU.subtract, ALU.mult).then_inc(xn_ready.sem, 1)

            def layer_norm(b):
                for step in LN_STEPS.values():
                    layer_norm_step(b, *step)

            def sequence(b, first, final):
                for t in range(TT):
                    dve.wait_ge(*ring.product(("k", t), b))
                    if t < 2:
                        dve.wait_ge(*sq_ready.before(b, QH - 1 + t))
                    nc.vector.tensor_tensor(biased[t % 2][:, :], ring.place(("k", t))[:, :], bkv["k"][:, :],
                                            ALU.add).then_inc(biased_ready.sem, 1)
                    dve.wait_ge(*biased_ready.now(b, t + 1))
                    nc.vector.tensor_scalar(expk[t % 2][:, :], biased[t % 2][:, :], 0.0, None,
                                            ALU.min).then_inc(mink_ready.sem, 1)
                    dve.wait_ge(*expk_ready.now(b, t + 1))
                    nc.vector.scalar_tensor_tensor(sk[:, t, :], biased[t % 2][:, :], 0.0, expk[t % 2][:, :], ALU.max,
                                                   ALU.add).then_inc(sk_ready.sem, 1)
                for t in range(TT):
                    dve.wait_ge(*ring.product(("v", t), b))
                    nc.vector.tensor_tensor(v[:, t, :], ring.place(("v", t))[:, :], bkv["v"][:, :],
                                            ALU.add).then_inc(v_ready.sem, 1)
                dve.wait_ge(*ring.product_before(("q", QH - 1), b))
                for kt in range(KT):
                    dve.wait_ge(*xT_ready.now(b, kt + 1))
                    nc.vector.tensor_copy(x_part[0][:, kt, :], xT[:, kt, :]).then_inc(x_hi_ready.sem, 1)
                    dve.wait_ge(*x_hi_ready.now(b, kt + 1))
                    nc.vector.tensor_tensor(x_part[1][:, kt, :], xT[:, kt, :], x_part[0][:, kt, :].bitcast(F32),
                                            ALU.subtract).then_inc(x_lo_ready.sem, 1)
                for h in range(QH + 1):
                    if h < QH:
                        dve.wait_ge(*reluq_ready.now(b, h + 1))
                        dve.wait_ge(*(sq_ready.now(b, h - 1) if h >= 2 else sq_ready.before(b, QH - 1 + h)))
                        nc.vector.tensor_scalar(expq[h % 2][:, :], ring.place(("q", h))[:, :], bq[:, h:h + 1], 0.0,
                                                ALU.add, ALU.min).then_inc(minq_ready.sem, 1)
                    if first and h == LN_HEAD:
                        layer_norm(b + 1)
                    elif not first and not final and h in LN_STEPS:
                        layer_norm_step(b + 1, *LN_STEPS[h])
                    if h > 0:
                        g = h - 1
                        dve.wait_ge(*ring.product(("norm", g), b))
                        dve.wait_ge(*(inv_ready.now(b, g - 1) if g >= 2 else inv_ready.before(b, QH - 1 + g)))
                        nc.vector.tensor_scalar(norm[g % 2][:, :], ring.place(("norm", g))[:, 0:TT], 1e-6, None,
                                                ALU.add).then_inc(norm_ready.sem, 1)
                        dve.wait_ge(*norm_ready.now(b, g + 1))
                        dve.wait_ge(*(acc_ready.now(b, (g - 1) * TT) if g >= 2 else
                                      acc_ready.before(b, (QH - 1 + g) * TT)))
                        nc.vector.reciprocal(inv[g % 2][:, :], norm[g % 2][:, :]).then_inc(inv_ready.sem, 1)
                        dve.wait_ge(*inv_ready.now(b, g + 1))
                        if g == 0:
                            dve.wait_ge(*s_stored.before(b, 1))
                        for t in range(TT):
                            dve.wait_ge(*ring.product(("head", g, t), b))
                            ps = ring.place(("head", g, t))[:, :]
                            if g == 0:
                                last = nc.vector.tensor_scalar(acc[:, t, :], ps, inv[0][:, t:t + 1], None, ALU.mult)
                            else:
                                dve.wait_ge(*acc_ready.now(b, (g - 1) * TT + t + 1))
                                last = nc.vector.scalar_tensor_tensor(acc[:, t, :], ps, inv[g % 2][:, t:t + 1],
                                                                      acc[:, t, :], ALU.mult, ALU.add)
                            last.then_inc(acc_ready.sem, 1)
                    if h < QH:
                        dve.wait_ge(*(ring.product(("head", h - 2, TT - 1), b) if h >= 2 else
                                      ring.product_before(("head", QH - 2 + h, TT - 1), b)))
                        dve.wait_ge(*M_hi_ready.now(b, h + 1))
                        nc.vector.tensor_tensor(M_part[h % 2][1][:, :], ring.place(("M", h))[:, :],
                                                M_part[h % 2][0][:, :].bitcast(F32),
                                                ALU.subtract).then_inc(M_lo_ready.sem, 1)
                        dve.wait_ge(*sq_ready.now(b, h + 1))
                        hi, lo = sq_part[h % 2]
                        nc.vector.tensor_copy(hi[:, :], sq[h % 2][:, :]).then_inc(sq_hi_ready.sem, 1)
                        dve.wait_ge(*sq_hi_ready.now(b, h + 1))
                        nc.vector.tensor_tensor(lo[:, :], sq[h % 2][:, :], hi[:, :].bitcast(F32),
                                                ALU.subtract).then_inc(sq_lo_ready.sem, 1)

            layer_norm(0)
            dve.wait_ge(w_loaded, 3 * 16)
            sequence(0, True, False)
            with dve.Fori(1, B - 1) as b:
                sequence(b, False, False)
            sequence(B - 1, False, True)

        @block.scalar
        def _(act):
            for s in (xT_ready, expk_ready, kvT_ready, ksum_ready, reluq_ready, expq_ready, M_hi_ready):
                s.ahead(act)

            def high(h):
                cols = slice(h * D, (h + 1) * D)
                act.wait_ge(wq_loaded[h % TT], 16 * (h // TT + 1))
                nc.scalar.activation(Wq[0][:, :, cols], x_tok[:, h % TT, :].rearrange("p (k c) -> p k c", k=KT),
                                     ACT.Copy).then_inc(wq_hi_ready, 1)

            def sequence(b, first):
                act.wait_ge(*x_lo_ready.before(b, KT))
                act.wait_ge(*xT_stored.before(b, 1))
                for kt in range(KT):
                    act.wait_ge(*ring.product(("xT", kt), b))
                    nc.scalar.activation(xT[:, kt, :], ring.place(("xT", kt))[:, :], ACT.Copy).then_inc(xT_ready.sem, 1)
                for t in range(TT):
                    act.wait_ge(*mink_ready.now(b, t + 1))
                    nc.scalar.activation(expk[t % 2][:, :], expk[t % 2][:, :], ACT.Exp).then_inc(expk_ready.sem, 1)
                if first:
                    for h in range(AHEAD):
                        high(h)
                act.wait_ge(*ring.product(("kvT", 0), b))
                nc.scalar.activation(flat(kvT[:, :, :]), ring.place(("kvT", 0))[:, :], ACT.Copy).then_inc(kvT_ready.sem, 1)
                act.wait_ge(*ring.product(("ksum", 0), b))
                nc.scalar.activation(ksum[:, :], ring.place(("ksum", 0))[:, 0:KVH], ACT.Copy).then_inc(ksum_ready.sem, 1)
                act.wait_ge(w_loaded, 3 * 16)
                act.wait_ge(*sk_ready.now(b, TT))
                for h in range(QH):
                    if first and h + AHEAD < QH:
                        high(h + AHEAD)
                    act.wait_ge(*ring.product(("q", h), b))
                    act.wait_ge(*(sq_ready.now(b, h - 1) if h >= 2 else sq_ready.before(b, QH - 1 + h)))
                    nc.scalar.activation(reluq[h % 2][:, :], ring.place(("q", h))[:, :], ACT.Relu,
                                         bias=bq[:, h:h + 1]).then_inc(reluq_ready.sem, 1)
                    act.wait_ge(*minq_ready.now(b, h + 1))
                    nc.scalar.activation(expq[h % 2][:, :], expq[h % 2][:, :], ACT.Exp).then_inc(expq_ready.sem, 1)
                    act.wait_ge(*ring.product(("M", h), b))
                    act.wait_ge(*(ring.product(("head", h - 2, TT - 1), b) if h >= 2 else
                                  ring.product_before(("head", QH - 2 + h, TT - 1), b)))
                    nc.scalar.activation(M_part[h % 2][0][:, :], ring.place(("M", h))[:, :],
                                         ACT.Copy).then_inc(M_hi_ready.sem, 1)

            sequence(0, True)
            with act.Fori(1, B) as b:
                sequence(b, False)

        @block.tensor
        def _(pe):
            pe.wait_ge(ident_loaded, 16)
            pe.wait_ge(const_set, 2)
            ring.done.ahead(pe)

            def sequence(b, first):
                for job in jobs:
                    kind, n = job[0], job[1]
                    place = ring.place(job)
                    pe.wait_ge(*ring.vacated(job, b))
                    if kind == "xT":
                        for t in range(TT):
                            pe.wait_ge(*xn_ready.now(b, t + 1))
                            last = nc.tensor.transpose(place[:, t * P:(t + 1) * P], x_tok[:, t, n * P:(n + 1) * P],
                                                       ident[:, :])
                    elif kind in "kv":
                        if n == 0:
                            pe.wait_ge(handed, 3 * 16)
                        for kt in range(KT):
                            pe.wait_ge(*xT_ready.now(b, kt + 1))
                            last = nc.tensor.matmul(place[:, :], xT[:, kt, n * P:(n + 1) * P], Wkv[kind][:, kt, :],
                                                    start=(kt == 0), stop=(kt == KT - 1))
                    elif kind == "kvT":
                        pe.wait_ge(*sk_ready.now(b, TT))
                        pe.wait_ge(*v_ready.now(b, TT))
                        for g in range(KVH):
                            for t in range(TT):
                                last = nc.tensor.matmul(place[:, g * D:(g + 1) * D], v[:, t, g * D:(g + 1) * D],
                                                        sk[:, t, g * D:(g + 1) * D], start=(t == 0),
                                                        stop=(t == TT - 1))
                    elif kind == "ksum":
                        for g in range(KVH):
                            for t in range(TT):
                                last = nc.tensor.matmul(place[:, g:g + 1], sk[:, t, g * D:(g + 1) * D], ones[:, :],
                                                        start=(t == 0), stop=(t == TT - 1))
                    elif kind == "q":
                        if first:
                            pe.wait_ge(wq_lo_ready, n + 1)
                        if n == 0:
                            pe.wait_ge(*x_lo_ready.now(b, KT))
                        for kt in range(KT):
                            last = product3(nc, place[:, :], [q[:, kt, n * D:(n + 1) * D] for q in Wq],
                                            [q[:, kt, :] for q in x_part], kt == 0, kt == KT - 1)
                    elif kind == "M":
                        pe.wait_ge(*kvT_ready.now(b, 1))
                        if first and n == 0:
                            pe.wait_ge(wo_loaded, 16)
                        last = nc.tensor.matmul(place[:, :], kvT[:, n // GROUPS, :], Wo[:, n, :], start=True, stop=True)
                    elif kind == "norm":
                        pe.wait_ge(*sq_ready.now(b, n + 1))
                        pe.wait_ge(*ksum_ready.now(b, 1))
                        for t in range(TT):
                            last = nc.tensor.matmul(place[:, t:t + 1], sq[n % 2][:, t * P:(t + 1) * P],
                                                    ksum[:, n // GROUPS:n // GROUPS + 1], start=True, stop=True)
                    else:
                        t = job[2]
                        pe.wait_ge(*M_lo_ready.now(b, n + 1))
                        pe.wait_ge(*sq_lo_ready.now(b, n + 1))
                        last = product3(nc, place[:, :], [q[:, t * P:(t + 1) * P] for q in sq_part[n % 2]],
                                        [q[:, :] for q in M_part[n % 2]], True, True)
                    last.then_inc(ring.done.sem, 1)

            sequence(0, True)
            with pe.Fori(1, B) as b:
                sequence(b, False)


def relu_gate(nc, w, x1, spill, out, relay, parts, handed):
    LAG = 2
    OB = I1 // C
    Z_STEPS = [[("z", 0), ("z", 1), ("g", 0), ("z", 2)], [("g", 1), ("z", 3), ("g", 2)], [("g", 3)]]
    TANH_TILES = [[0], [1], [2, 3]]
    first_tiles = [("up", 0, kt) for kt in range(KT)]

    def tiles_at(j):
        return ([("up", j // 4 + 1, j % 4)] if j // 4 + 1 < OB else []) + [("dn", j)]

    order = first_tiles + [x for j in range(UT) for x in tiles_at(j)]
    number = {x: i for i, x in enumerate(order)}
    items = []
    for x in order:
        if x[0] == "dn" or x[2] == 0:
            items.append(("scale", x))
        items.append(("lora", x))
    made = {item: i + 1 for i, item in enumerate(items)}

    with ExitStack() as ctx:
        def sb(name, shape, dt=F32):
            return ctx.enter_context(nc.sbuf_tensor("g_" + name, shape, dt))

        def signal(name, per, unit=1):
            return Signal(ctx, nc, "g_" + name, per, unit)

        Wup = [sb(f"Wup{i}", [P, KT, I1], F32R) for i in range(2)]
        Wdn = [sb(f"Wdn{i}", [P, UT, C], F32R) for i in range(2)]
        wide, factors = flat(relay[1][:, :, :]), flat(parts[1][:, :, :])
        low_rows = sb("low_rows", [P, 1])
        narrow_part = [sb("narrow_hi", [P, C], F32R)]
        with nc.sbuf_tensor("g_narrow_lo", [P, C], F32R) as part:
            narrow_part.append(part)
        narrow = sb("narrow", [P, C])
        b_up = sb("b_up", [P, UT])
        b_dn = sb("b_dn", [P, C])
        xT = relay[2]
        x_part = [sb(f"x_part{i}", [P, KT, T], F32R) for i in range(2)]
        whole = [sb(f"whole{i}", [P, C]) for i in range(2)]
        x2 = [sb(f"x2{i}", [P, T]) for i in range(2)]
        x2_part = [[sb(f"x2_part{i}{j}", [P, T], F32R) for i in range(2)] for j in range(3)]
        z = [sb(f"z{i}", [P, C]) for i in range(2)]
        tanh_z = [sb(f"tanh_z{i}", [P, C]) for i in range(2)]
        s = relay[0]
        xs = sb("xs", [P, 2, C])
        up_q, dn_q = s[:, :, :].bitcast(I32), xs[:, :, :].bitcast(I32)
        banks = [ctx.enter_context(nc.psum_tensor(f"g_ps{i}", [P, 512], F32)) for i in range(8)]
        scale_ps, pre_ps = banks[0], banks[1]

        def lora_place(x):
            return banks[4 + x[2]] if x in first_tiles else pre_ps


        factor_hi_ready = ctx.enter_context(nc.semaphore("g_factor_hi_ready"))
        factor_ready = ctx.enter_context(nc.semaphore("g_factor_ready"))
        narrow_loaded = ctx.enter_context(nc.semaphore("g_narrow_loaded"))
        small_loaded = ctx.enter_context(nc.semaphore("g_small_loaded"))
        up_loaded = ctx.enter_context(nc.semaphore("g_up_loaded"))
        dn_loaded = ctx.enter_context(nc.semaphore("g_dn_loaded"))
        expansion = ctx.enter_context(nc.semaphore("g_expansion"))
        expanded = ctx.enter_context(nc.semaphore("g_expanded"))
        w_hi_ready = ctx.enter_context(nc.semaphore("g_w_hi_ready"))
        w_lo_ready = ctx.enter_context(nc.semaphore("g_w_lo_ready"))
        xT_loaded = signal("xT_loaded", 1, 16)
        s_loaded = signal("s_loaded", 1, 16)
        x1_loaded = [signal(f"x1_loaded{i}", TT // 2, 16) for i in range(2)]
        x_hi_ready = signal("x_hi_ready", KT)
        x_lo_ready = signal("x_lo_ready", KT)
        x2_ready = signal("x2_ready", UT)
        x2_hi_ready = signal("x2_hi_ready", UT)
        x2_lo_ready = signal("x2_lo_ready", UT)
        x2_used = signal("x2_used", UT - 1)
        z_ready = signal("z_ready", TT)
        tanh_z_ready = signal("tanh_z_ready", TT)
        u_ready = signal("u_ready", TT)
        sg_ready = signal("sg_ready", TT)
        out_ready = signal("out_ready", TT)
        out_stored = [signal(f"out_stored{i}", TT // 2, 16) for i in range(2)]
        U = Ring(ctx, nc, "g_U", banks[2:4], [("up", j) for j in range(UT)],
                 {("up", j): (x2_ready, j + 1) for j in range(UT)})
        Y = Ring(ctx, nc, "g_Y", banks[4:8], [("down", t) for t in range(TT)],
                 {("down", t): (z_ready, t + 1) for t in range(TT)})

        block = ctx.enter_context(nc.Block())

        @block.sync
        def _(sp):
            for q in (xT_loaded, s_loaded, *x1_loaded, *out_stored):
                q.ahead(sp)

            def load_up(ob):
                sp.wait_ge(expanded, 2 * number["up", ob - 1, KT - 1] + 1)
                sp.dma_start(up_q, w["up_q"].rearrange("p (k c) -> p k c", k=KT)[:, :, ob * C:(ob + 1) * C]).then_inc(
                    up_loaded, 16)

            def load_down(c):
                if c > 0:
                    sp.wait_ge(expanded, 2 * number["dn", 2 * c - 1] + 1)
                sp.dma_start(dn_q.rearrange("p a b -> p (a b)"), w["dn_q"][:, c * 2 * C:(c + 1) * 2 * C]).then_inc(
                    dn_loaded, 16)

            def load_x(b):
                sp.wait_ge(*x_lo_ready.before(b, KT))
                sp.dma_start(flat(xT[:, :, :]), slab(spill["x2"], b)).then_inc(xT_loaded.sem, 16)

            def finish(b):
                sp.wait_ge(*out_ready.before(b, TT))
                sp.dma_start(flat(s[:, :, :]), slab(spill["s"], b)).then_inc(s_loaded.sem, 16)

                def load(t):
                    stored = out_stored[t % 2]
                    sp.wait_ge(*(stored.now(b, t // 2) if t >= 2 else stored.before(b, TT // 2)))
                    sp.dma_start(xs[:, t % 2, :], x1[bass.ds(b * T + t * P, P), :]).then_inc(x1_loaded[t % 2].sem, 16)

                load(0)
                load(1)
                for t in range(TT):
                    sp.wait_ge(*out_ready.now(b, t + 1))
                    sp.dma_start(out[bass.ds(b * T + t * P, P), :], xs[:, t % 2, :]).then_inc(out_stored[t % 2].sem, 16)
                    if t + 2 < TT:
                        load(t + 2)

            sp.dma_start(narrow[:, :], w["g_narrow"]).then_inc(narrow_loaded, 16)
            sp.dma_start(low_rows[:, :], w["low_rows"]).then_inc(narrow_loaded, 16)
            sp.dma_start(b_up[:, :], w["b_up"]).then_inc(small_loaded, 16)
            sp.dma_start(b_dn[:, :], w["b_dn"]).then_inc(small_loaded, 16)
            sp.wait_ge(handed, 3 * 16)
            sp.sem_inc(up_loaded, 16)
            sp.sem_inc(xT_loaded.sem, 16)
            load_down(0)
            for j in range(0, UT, 2):
                if j % 4 == 0 and j // 4 + 1 < OB:
                    load_up(j // 4 + 1)
                if j + 2 < UT:
                    load_down(j // 2 + 1)
            sp.wait_ge(expanded, 2 * len(order))
            with sp.Fori(1, B) as b:
                load_x(b)
                finish(b - 1)
            finish(B - 1)
            for q in out_stored:
                sp.wait_ge(q.sem, 16 * (TT // 2) * (B + 1))

        @block.gpsimd
        def _(pool):
            out_ready.ahead(pool)
            for i, x in enumerate(order):
                part = Wup[1][:, x[2], x[1] * C:(x[1] + 1) * C] if x[0] == "up" else Wdn[1][:, x[1], :]
                high = Wup[0][:, x[2], x[1] * C:(x[1] + 1) * C] if x[0] == "up" else Wdn[0][:, x[1], :]
                pool.wait_ge(w_hi_ready, i + 1)
                nc.gpsimd.tensor_tensor(part, whole[i % 2][:, :], high.bitcast(F32), ALU.subtract).then_inc(
                    w_lo_ready, 1)

            def finish(b):
                for t in range(TT):
                    pool.wait_ge(*sg_ready.now(b, t + 1))
                    pool.wait_ge(*x1_loaded[t % 2].now(b, t // 2 + 1))
                    nc.gpsimd.tensor_tensor(xs[:, t % 2, :], xs[:, t % 2, :], s[:, t, :], ALU.add).then_inc(
                        out_ready.sem, 1)

            with pool.Fori(1, B) as b:
                finish(b - 1)
            finish(B - 1)

        @block.vector
        def _(dve):
            for q in (x_lo_ready, x2_hi_ready, x2_lo_ready, z_ready, u_ready, sg_ready):
                q.ahead(dve)

            def expand(x):
                i = number[x]
                if x[0] == "up":
                    dve.wait_ge(up_loaded, 16 * (x[1] + 1))
                    q, scale, before = up_q[:, x[2], :], scale_ps, ("scale", ("up", x[1], 0))
                else:
                    dve.wait_ge(dn_loaded, 16 * (x[1] // 2 + 1))
                    q, scale, before = dn_q[:, x[1] % 2, :], pre_ps, ("scale", x)
                dve.wait_ge(expansion, made[before])
                if i >= 2:
                    dve.wait_ge(w_lo_ready, i - 1)
                nc.vector.scalar_tensor_tensor(whole[i % 2][:, :], q, -7.5, scale[:, :], ALU.add,
                                               ALU.mult).then_inc(expanded, 1)
                dve.wait_ge(expanded, 2 * i + 1)
                dve.wait_ge(expansion, made["lora", x])
                nc.vector.tensor_tensor(whole[i % 2][:, :], whole[i % 2][:, :], lora_place(x)[:, :],
                                        ALU.add).then_inc(
                    expanded, 1)

            def finish(b, steps=Z_STEPS[0] + Z_STEPS[1] + Z_STEPS[2]):
                for kind, t in steps:
                    if kind == "z":
                        if t == 0:
                            dve.wait_ge(small_loaded, 2 * 16)
                            dve.wait_ge(*s_loaded.now(b, 1))
                        dve.wait_ge(*Y.product(("down", t), b))
                        dve.wait_ge(*(sg_ready.now(b, t - 1) if t >= 2 else sg_ready.before(b, TT - 1 + t)))
                        nc.vector.tensor_tensor(z[t % 2][:, :], Y.place(("down", t))[:, :], b_dn[:, :],
                                                ALU.add).then_inc(z_ready.sem, 1)
                        continue
                    dve.wait_ge(*tanh_z_ready.now(b, t + 1))
                    nc.vector.scalar_tensor_tensor(z[t % 2][:, :], tanh_z[t % 2][:, :], 1.0, z[t % 2][:, :], ALU.add,
                                                   ALU.mult).then_inc(u_ready.sem, 1)
                    dve.wait_ge(*u_ready.now(b, t + 1))
                    nc.vector.scalar_tensor_tensor(s[:, t, :], s[:, t, :], 0.5, z[t % 2][:, :], ALU.mult,
                                                   ALU.mult).then_inc(sg_ready.sem, 1)

            def sequence(b, first):
                dve.wait_ge(*U.product_before(("up", UT - 1), b))
                for kt in range(KT):
                    dve.wait_ge(*x_hi_ready.now(b, kt + 1))
                    nc.vector.tensor_tensor(x_part[1][:, kt, :], xT[:, kt, :], x_part[0][:, kt, :].bitcast(F32),
                                            ALU.subtract).then_inc(x_lo_ready.sem, 1)
                for j in range(UT):
                    if first:
                        for x in tiles_at(j):
                            expand(x)
                    elif j < len(Z_STEPS):
                        finish(b - 1, Z_STEPS[j])
                    dve.wait_ge(*x2_ready.now(b, j + 1))
                    dve.wait_ge(*(x2_used.now(b, j - 2) if j >= 3 else Y.product_before(("down", TT - 1), b)))
                    hi, lo = x2_part[j % 3]
                    nc.vector.tensor_copy(hi[:, :], x2[j % 2][:, :]).then_inc(x2_hi_ready.sem, 1)
                    dve.wait_ge(*x2_hi_ready.now(b, j + 1))
                    nc.vector.tensor_tensor(lo[:, :], x2[j % 2][:, :], hi[:, :].bitcast(F32), ALU.subtract).then_inc(
                        x2_lo_ready.sem, 1)

            dve.wait_ge(narrow_loaded, 2 * 16)
            dve.wait_ge(factor_hi_ready, 1)
            nc.vector.tensor_tensor(narrow_part[1][:, :], narrow[:, :], narrow_part[0][:, :].bitcast(F32),
                                    ALU.subtract).then_inc(factor_ready, 1)
            for n in range(OB):
                cols = slice(n * C, (n + 1) * C)
                dve.wait_ge(factor_hi_ready, n + 2)
                nc.vector.scalar_tensor_tensor(factors[:, cols], flat(x_part[1][:, :, :])[:, cols].bitcast(F32),
                                               low_rows[:, 0:1], wide[:, cols], ALU.mult, ALU.add).then_inc(
                                                   factor_ready, 1)
            for x in first_tiles:
                expand(x)
            dve.wait_ge(factor_ready, OB + 1)
            sequence(0, True)
            with dve.Fori(1, B) as b:
                sequence(b, False)
            finish(B - 1)

        @block.scalar
        def _(act):
            for q in (x_hi_ready, x2_ready, tanh_z_ready):
                q.ahead(act)

            def high(x):
                part = Wup[0][:, x[2], x[1] * C:(x[1] + 1) * C] if x[0] == "up" else Wdn[0][:, x[1], :]
                act.wait_ge(expanded, 2 * number[x] + 2)
                nc.scalar.activation(part, whole[number[x] % 2][:, :], ACT.Copy).then_inc(w_hi_ready, 1)

            def finish(b, tiles=range(TT)):
                for t in tiles:
                    act.wait_ge(*z_ready.now(b, t + 1))
                    act.wait_ge(*(u_ready.now(b, t - 1) if t >= 2 else u_ready.before(b, TT - 1 + t)))
                    nc.scalar.activation(tanh_z[t % 2][:, :], z[t % 2][:, :], ACT.Tanh, scale=0.5).then_inc(
                        tanh_z_ready.sem, 1)

            def sequence(b, first):
                act.wait_ge(small_loaded, 2 * 16)
                act.wait_ge(*xT_loaded.now(b, 1))
                act.wait_ge(*U.product_before(("up", UT - 1), b))
                for kt in range(KT):
                    nc.scalar.activation(x_part[0][:, kt, :], xT[:, kt, :], ACT.Copy).then_inc(x_hi_ready.sem, 1)
                for j in range(UT):
                    if first:
                        for x in tiles_at(j):
                            high(x)
                    elif j < len(TANH_TILES):
                        finish(b - 1, TANH_TILES[j])
                    act.wait_ge(*U.product(("up", j), b))
                    act.wait_ge(*(x2_lo_ready.now(b, j - 1) if j >= 2 else x2_lo_ready.before(b, UT - 1 + j)))
                    nc.scalar.activation(x2[j % 2][:, :], U.place(("up", j))[:, :], ACT.Relu,
                                         bias=b_up[:, j:j + 1]).then_inc(x2_ready.sem, 1)

            act.wait_ge(narrow_loaded, 2 * 16)
            nc.scalar.activation(narrow_part[0][:, :], narrow[:, :], ACT.Copy).then_inc(factor_hi_ready, 1)
            act.wait_ge(handed, 3 * 16)
            for n in range(OB):
                nc.scalar.activation(x_part[1][:, n, :], wide[:, n * C:(n + 1) * C], ACT.Copy).then_inc(
                    factor_hi_ready, 1)
            for x in first_tiles:
                high(x)
            sequence(0, True)
            with act.Fori(1, B) as b:
                sequence(b, False)
            finish(B - 1)

        @block.tensor
        def _(pe):
            for q in (U.done, Y.done, x2_used):
                q.ahead(pe)

            def make(item):
                what, x = item
                i = number[x]
                up = x[0] == "up"
                place = scale_ps if what == "scale" and up else pre_ps if what == "scale" else lora_place(x)
                pe.wait_ge(factor_ready, (x[1] if up else x[1] * P // C) + 2)
                if what == "scale" and up:
                    if x[1] > 0:
                        pe.wait_ge(expanded, 2 * number["up", x[1] - 1, KT - 1] + 1)
                elif what == "scale":
                    pe.wait_ge(expanded, 2 * i)
                elif x not in first_tiles:
                    pe.wait_ge(expanded, 2 * i if up else 2 * i + 1)
                hi, lo = narrow_part
                if up:
                    block, tile = slice(x[1] * C, (x[1] + 1) * C), slice(x[2] * P, (x[2] + 1) * P)
                    pairs = ([(hi[64:80, 0:P], factors[64:80, block])] if what == "scale" else
                             [(hi[0:2 * RANK, tile], factors[0:2 * RANK, block]),
                              (lo[0:RANK, tile], factors[0:RANK, block])])
                else:
                    tile = slice(x[1] * P, (x[1] + 1) * P)
                    pairs = ([(factors[96:128, tile], part[96:128, :]) for part in (hi, lo)] if what == "scale" else
                             [(factors[32:32 + 2 * RANK, tile], hi[32:32 + 2 * RANK, :]),
                              (factors[32:32 + RANK, tile], lo[32:32 + RANK, :])])
                for k, (left, right) in enumerate(pairs):
                    last = nc.tensor.matmul(place[:, :], left, right, start=(k == 0), stop=(k == len(pairs) - 1))
                last.then_inc(expansion, 1)

            def sequence(b, first):
                for n in range(UT + LAG):
                    pre = [item for item in items if first and n < UT and item[1] in tiles_at(n)]
                    while len(pre) > 2:
                        make(pre.pop(0))
                    if n < UT:
                        pe.wait_ge(*U.vacated(("up", n), b))
                        if first and n % 4 == 0:
                            pe.wait_ge(w_lo_ready, number["up", n // 4, KT - 1] + 1)
                        cols = slice(n * P, (n + 1) * P)
                        for kt in range(KT):
                            if n == 0:
                                pe.wait_ge(*x_lo_ready.now(b, kt + 1))
                            last = product3(nc, U.place(("up", n))[:, :], [q[:, kt, cols] for q in Wup],
                                            [q[:, kt, :] for q in x_part], kt == 0, kt == KT - 1)
                        last.then_inc(U.done.sem, 1)
                    if pre:
                        make(pre.pop(0))
                    i = n - LAG
                    if i >= 0:
                        pe.wait_ge(*x2_lo_ready.now(b, i + 1))
                        if first:
                            pe.wait_ge(w_lo_ready, number["dn", i] + 1)
                        for t in range(TT):
                            if t == 2 and pre:
                                make(pre.pop(0))
                            if i == 0:
                                pe.wait_ge(*Y.vacated(("down", t), b))
                            last = product3(nc, Y.place(("down", t))[:, :],
                                            [q[:, t * P:(t + 1) * P] for q in x2_part[i % 3]],
                                            [q[:, i, :] for q in Wdn], i == 0, i == UT - 1)
                            if i == UT - 1:
                                last.then_inc(Y.done.sem, 1)
                        if i < UT - 1:
                            last.then_inc(x2_used.sem, 1)
                    elif pre:
                        make(pre.pop(0))

            for item in items:
                if item[1] in first_tiles:
                    make(item)
            sequence(0, True)
            with pe.Fori(1, B) as b:
                sequence(b, False)


SCRATCH = {"x": KT * T, "r": HH * T, "k": HH * T, "v": HH * T, "w": HH * T, "g": TT * KD,
           "x2": KT * T, "s": TT * C}


def layouts(inputs):
    a = {k: np.asarray(v) for k, v in inputs.items()}

    def tiles(m, order=None):
        m = m if order is None else m[order]
        n = m.shape[0] // P
        return m.reshape(n, P, -1).transpose(1, 0, 2).reshape(P, -1)

    def every(v):
        return np.broadcast_to(v, (P,) + v.shape)

    o = {}
    o["x"] = a["L0_attn_x"].reshape(B * T, C)[:, CHANNELS]
    o["ident"] = np.eye(P, dtype=np.float32)
    o["front"] = tiles(np.concatenate([a["L0_attn_Wx1"], a["L0_attn_Wr"], a["L0_attn_Wk"], a["L0_attn_Wv"],
                                       a["L0_attn_Ww_a"], a["L0_attn_Wg_a"]], axis=1), CHANNELS)
    x2 = a["L0_attn_Wx2"][CHANNELS].transpose(1, 2, 0)
    pad = np.concatenate([x2, x2[4:5]])
    o["Wx2"] = pad.reshape(3, 2 * LOW, C).transpose(1, 0, 2).reshape(P, -1)
    o["Wb"] = np.concatenate([a["L0_attn_Ww_b"], a["L0_attn_Wg_b"]], axis=1)
    o["front_col"] = np.concatenate([tiles(a["L0_attn_mu_x"][:, None], CHANNELS),
                                     a["L0_attn_x_bias"][:, CHANNELS].reshape(5 * KT, P).T,
                                     a["L0_attn_bw"].reshape(HH, P).T], axis=1)
    o["bg"] = every(a["L0_attn_bg"])
    hidden = np.concatenate([HIDDEN0, I0 + HIDDEN0])
    o["gu_words"] = np.tile(a["L0_ffn_gate_up_packed"][hidden].T, (2, 1))
    o["gu_scale"] = a["L0_ffn_gate_up_scales"][:, hidden][np.arange(P) % 64 // 16]
    words = a["L0_ffn_down_packed"][CHANNELS].T.reshape(JT, 16, C)
    words = np.concatenate([words, words[:B * DQ - JT]])
    o["dn_words"] = np.tile(words.transpose(1, 0, 2), (8, 1, 1)).reshape(P, -1)
    scale = a["L0_ffn_down_scales"][:, CHANNELS]
    o["dn_scale"] = every(np.concatenate([scale, scale[:B * DQ - JT]]).reshape(-1))
    nibble = [2 * jj + np.arange(P) // 64 for jj in range(2)] + [np.arange(P) // 16 % 4]
    o["shift"] = np.stack([12 - 4 * j for j in nibble], axis=1).astype(np.int32)
    key = np.arange(P)
    o["spread"] = np.stack([(key[:, None] // DK == key // DK) & (key[:, None] % DK == v) for v in range(DK)],
                           axis=1).astype(np.float32).reshape(P, -1)
    o["heads"] = (key[:, None] // DK == np.arange(HPT)).astype(np.float32)
    o["bonus"] = a["L0_attn_bonus"].reshape(HH, P).T
    o["lnw"] = every(np.tile(a["L0_attn_ln_w"], NH))
    o["lnb"] = every(np.tile(a["L0_attn_ln_b"], NH))
    o["Wo0"] = tiles(a["L0_attn_Wo"][:, CHANNELS])
    for s in "kv":
        o[f"W{s}1"] = tiles(a[f"L1_attn_W{s}"].T, CHANNELS)
        o["b" + s] = every(a["L1_attn_b" + s])
    o["Wq1"] = tiles(a["L1_attn_Wq"].T, CHANNELS)
    o["bq"] = a["L1_attn_bq"].reshape(QH, D).T
    o["Wo1"] = tiles(a["L1_attn_Wo"].T[:, CHANNELS])
    o["up_q"] = tiles(a["L1_ffn_w_up_q"].T, CHANNELS)
    o["dn_q"] = tiles(a["L1_ffn_w_down_q"][CHANNELS].T)
    up_pick = (key % 64 // 8 == np.arange(8)[:, None]).astype(np.float32)
    dn_pick = np.stack([2 * j + key // 64 == np.arange(32)[:, None] for j in range(UT)],
                       axis=1).astype(np.float32).reshape(32, -1)
    wide, narrow = np.zeros((P, I1), np.float32), np.zeros((P, C), np.float32)
    low_rows = np.zeros((P, 1), np.float32)
    for i, n in ((0, RANK), (32, RANK), (64, C // 64)):
        for at in (i, i + n):
            if i == 0:
                wide[at:at + n], narrow[at:at + n] = a["L1_ffn_w_up_lora_b"], a["L1_ffn_w_up_lora_a"][CHANNELS].T
            elif i == 32:
                wide[at:at + n] = a["L1_ffn_w_down_lora_a"].T
                narrow[at:at + n] = a["L1_ffn_w_down_lora_b"][:, CHANNELS]
            else:
                wide[at:at + n], narrow[at:at + n, 0:P] = a["L1_ffn_w_up_scale"].T, up_pick
        low_rows[i + n:i + 2 * n] = -1.0
    wide[96:128], narrow[96:128] = dn_pick, a["L1_ffn_w_down_scale"][CHANNELS].T
    o["g_wide"], o["g_narrow"], o["low_rows"] = wide, narrow, low_rows
    o["b_up"] = a["L1_ffn_b_up"].reshape(UT, P).T
    o["b_dn"] = every(a["L1_ffn_b_down"][CHANNELS])
    return {k: np.ascontiguousarray(v) for k, v in o.items()}


def build(nc, w, out):
    def scratch(name, shape):
        return nc.dram_tensor("scratch_" + name, shape, F32, kind="Internal").ap()

    spill = {k: scratch(k, (B * P, n)) for k, n in SCRATCH.items()}
    x1 = scratch("x1", (B * T, C))
    shape = [P, TT, C]
    with ExitStack() as outer:
        with ExitStack() as ctx:
            parts = [ctx.enter_context(nc.sbuf_tensor(f"relay_part{i}", shape, F32R)) for i in range(3)]
        relay = [outer.enter_context(nc.sbuf_tensor(f"relay{i}", shape, F32)) for i in range(3)]
        handed = [outer.enter_context(nc.semaphore(f"handed{i}")) for i in range(3)]
        stages(nc, w, out, spill, x1, relay, parts, handed)


def stages(nc, w, out, spill, x1, relay, parts, handed):
    with ExitStack() as ctx:
        Wgu = ctx.enter_context(nc.sbuf_tensor("Wgu", [P, KT, 2 * I0], F32))
        Wdn = ctx.enter_context(nc.sbuf_tensor("Wdn", [P, B * DQ, C], F32))
        front(nc, w, w["x"], spill, Wgu, Wdn, relay, handed[0])
        recurrence_and_gate(nc, w, w["x"], spill, Wgu, Wdn, x1, relay, parts, *handed[0:2])
    linear_attention(nc, w, x1, spill, relay, *handed[1:3])
    relu_gate(nc, w, x1, spill, out, relay, parts, handed[2])


def kernel(**inputs):
    import concourse.bacc as bacc
    from concourse.bass_utils import run_bass_kernel_spmd as run

    nc = bacc.Bacc("TRN2", target_bir_lowering=False, num_devices=1)
    arrays = {"in_" + k: v for k, v in layouts(inputs).items()}
    w = {k[3:]: nc.dram_tensor(k, v.shape, mybir.dt.from_np(v.dtype), kind="ExternalInput").ap()
         for k, v in arrays.items()}
    out = nc.dram_tensor("out", (B * T, C), F32, kind="ExternalOutput").ap()
    build(nc, w, out)
    r = run(nc, [arrays], core_ids=[0])
    return np.ascontiguousarray(r.results[0]["out"][:, np.argsort(CHANNELS)].reshape(B, T, C))
```
